# Optimizing a Trainium2 kernel written in Bass

```python
import numpy as np
import jax
import jax.numpy as jnp

def _softmax(x, axis=-1):
    return jax.nn.softmax(x, axis=axis)

def _gelu(x):
    return jax.nn.gelu(x, approximate=True)

def _silu(x):
    return jax.nn.silu(x)

def _sigmoid(x):
    return jax.nn.sigmoid(x)

def _layernorm(x, axis=-1, eps=1e-05):
    m = jnp.mean(x, axis=axis, keepdims=True)
    v = jnp.var(x, axis=axis, keepdims=True)
    return (x - m) / jnp.sqrt(v + eps)

def _scatter_add(tgt, idx, src, axis=0):
    return tgt.at[idx].add(src)

def _segment_sum(src, seg, n):
    return jax.ops.segment_sum(src, seg, n)
kernel_name = 'mk_adaln_d1_jaxref_r8_4765b1'

def setup_inputs(seed: int=0):
    np.random.seed(seed)
    _w = jnp.asarray

    def _L0_attn_setup():
        import jax, jax.numpy as jnp
        import numpy as np
        B, S, M = (1, 256, 256)
        H, HKV, D = (32, 8, 64)
        SW = 128
        WAVELENGTH = 150000.0
        SCALE = D ** (-0.25)
        NEG = -1000000000.0

        def _cos_sin(seq_len, dtype):
            half = D // 2
            inv_freq = 1.0 / WAVELENGTH ** (jnp.arange(half, dtype=jnp.float32) * 2.0 / D)
            t = jnp.arange(seq_len, dtype=jnp.float32)
            freqs = t[:, None] * inv_freq[None, :]
            return (jnp.cos(freqs)[None, :, None, :].astype(dtype), jnp.sin(freqs)[None, :, None, :].astype(dtype))

        def _interleaved_rope(x, cos, sin):
            x_even = x[..., ::2]
            x_odd = x[..., 1::2]
            first = x_even * cos - x_odd * sin
            second = x_odd * cos + x_even * sin
            return jnp.stack([first, second], axis=-1).reshape(x.shape)
        key = jax.random.key(seed)
        ks = jax.random.split(key, 8)
        return {'hidden_states': jax.random.normal(ks[0], (B, S, M), jnp.float32), 'Wq': jax.random.normal(ks[1], (M, H, D), jnp.float32) * 0.02, 'bq': jnp.zeros((H, D), jnp.float32), 'Wk': jax.random.normal(ks[2], (M, HKV, D), jnp.float32) * 0.02, 'bk': jnp.zeros((HKV, D), jnp.float32), 'Wv': jax.random.normal(ks[3], (M, HKV, D), jnp.float32) * 0.02, 'bv': jnp.zeros((HKV, D), jnp.float32), 'Wo': jax.random.normal(ks[4], (H, D, M), jnp.float32) * 0.02, 'bo': jnp.zeros((M,), jnp.float32), 'sinks': jax.random.normal(ks[5], (H,), jnp.float32)}
    _L0_attn_in = _L0_attn_setup()

    def _L0_ffn_setup():
        import jax, jax.numpy as jnp
        import numpy as np
        E, K, H, F = (64, 6, 256, 96)
        G, KG = (8, 4)
        SHARED_F = 96
        SCALE = 2.5
        T = 2 * 128
        CAP = 2 * (T * K // E)

        def _grouped_topk(logits, bias):
            scores = jax.nn.sigmoid(logits.astype(jnp.float32))
            scores_b = scores + bias[None, :]
            gs = scores_b.reshape(-1, G, E // G)
            group_scores = jnp.sum(jax.lax.top_k(gs, 2)[0], axis=-1)
            gidx = jax.lax.top_k(group_scores, KG)[1]
            rows = jnp.arange(group_scores.shape[0])[:, None]
            group_mask = jnp.zeros_like(group_scores).at[rows, gidx].set(1.0)
            score_mask = jnp.repeat(group_mask, E // G, axis=-1) > 0
            tmp = jnp.where(score_mask, scores_b, -jnp.inf)
            topk_ids = jax.lax.top_k(tmp, K)[1]
            topk_w = jnp.take_along_axis(scores, topk_ids, axis=-1)
            topk_w = topk_w / jnp.sum(topk_w, axis=-1, keepdims=True)
            return (topk_w * SCALE, topk_ids)

        def _routed_moe(x, topk_w, topk_ids, w_gate, w_up, w_down):
            Tn = x.shape[0]
            flat_e = topk_ids.reshape(-1)
            order = jnp.argsort(flat_e)
            se = flat_e[order]
            pos = jnp.arange(Tn * K) - jnp.searchsorted(se, se, side='left')
            tok = order // K
            valid = pos < CAP
            slot = jnp.where(valid, pos, CAP)
            buf = jnp.zeros((E, CAP + 1, H), x.dtype).at[se, slot].set(x[tok])[:, :CAP]
            h = jax.nn.silu(jnp.einsum('ech,ehf->ecf', buf, w_gate)) * jnp.einsum('ech,ehf->ecf', buf, w_up)
            out = jnp.einsum('ecf,efh->ech', h, w_down)
            gathered = out[se, jnp.minimum(pos, CAP - 1)] * valid.astype(x.dtype)[:, None]
            w = topk_w.reshape(-1)[order].astype(x.dtype)[:, None]
            return jax.ops.segment_sum(gathered * w, tok, num_segments=Tn)
        key = jax.random.key(seed)
        ks = jax.random.split(key, 9)
        s = 0.02
        return dict(hidden_states=jax.random.normal(ks[0], (2, 128, H), jnp.float32), gate_w=jax.random.normal(ks[1], (H, E), jnp.float32) * s, bias=jax.random.normal(ks[2], (E,), jnp.float32) * s, w_gate=jax.random.normal(ks[3], (E, H, F), jnp.float32) * s, w_up=jax.random.normal(ks[4], (E, H, F), jnp.float32) * s, w_down=jax.random.normal(ks[5], (E, F, H), jnp.float32) * s, ws_gate=jax.random.normal(ks[6], (H, SHARED_F), jnp.float32) * s, ws_up=jax.random.normal(ks[7], (H, SHARED_F), jnp.float32) * s, ws_down=jax.random.normal(ks[8], (SHARED_F, H), jnp.float32) * s)
    _L0_ffn_in = _L0_ffn_setup()
    _L0_c = _w((lambda *s: np.random.randn(*s).astype(np.float32) * 0.05)(8, 256))
    _L0_wmod = _w((lambda *s: np.random.randn(*s).astype(np.float32) * 0.05)(256, 6 * 256) * 256 ** (-0.5))
    _d = {'L0_attn_hidden_states': _L0_attn_in['hidden_states'], 'L0_attn_Wq': _L0_attn_in['Wq'], 'L0_attn_bq': _L0_attn_in['bq'], 'L0_attn_Wk': _L0_attn_in['Wk'], 'L0_attn_bk': _L0_attn_in['bk'], 'L0_attn_Wv': _L0_attn_in['Wv'], 'L0_attn_bv': _L0_attn_in['bv'], 'L0_attn_Wo': _L0_attn_in['Wo'], 'L0_attn_bo': _L0_attn_in['bo'], 'L0_attn_sinks': _L0_attn_in['sinks'], 'L0_ffn_gate_w': _L0_ffn_in['gate_w'], 'L0_ffn_bias': _L0_ffn_in['bias'], 'L0_ffn_w_gate': _L0_ffn_in['w_gate'], 'L0_ffn_w_up': _L0_ffn_in['w_up'], 'L0_ffn_w_down': _L0_ffn_in['w_down'], 'L0_ffn_ws_gate': _L0_ffn_in['ws_gate'], 'L0_ffn_ws_up': _L0_ffn_in['ws_up'], 'L0_ffn_ws_down': _L0_ffn_in['ws_down'], 'L0_c': _L0_c, 'L0_wmod': _L0_wmod}
    _x0 = _d['L0_attn_hidden_states']
    _d['L0_attn_hidden_states'] = jax.random.normal(jax.random.fold_in(jax.random.key(seed), 1), (8, 256, 256), dtype=_x0.dtype)
    del _x0
    return _d

def reference(L0_attn_hidden_states, L0_attn_Wq, L0_attn_bq, L0_attn_Wk, L0_attn_bk, L0_attn_Wv, L0_attn_bv, L0_attn_Wo, L0_attn_bo, L0_attn_sinks, L0_ffn_gate_w, L0_ffn_bias, L0_ffn_w_gate, L0_ffn_w_up, L0_ffn_w_down, L0_ffn_ws_gate, L0_ffn_ws_up, L0_ffn_ws_down, L0_c, L0_wmod):

    def _L0_attn_ref(hidden_states, Wq, bq, Wk, bk, Wv, bv, Wo, bo, sinks):
        import jax, jax.numpy as jnp
        import numpy as np
        B, S, M = (1, 256, 256)
        H, HKV, D = (32, 8, 64)
        SW = 128
        WAVELENGTH = 150000.0
        SCALE = D ** (-0.25)
        NEG = -1000000000.0

        def _cos_sin(seq_len, dtype):
            half = D // 2
            inv_freq = 1.0 / WAVELENGTH ** (jnp.arange(half, dtype=jnp.float32) * 2.0 / D)
            t = jnp.arange(seq_len, dtype=jnp.float32)
            freqs = t[:, None] * inv_freq[None, :]
            return (jnp.cos(freqs)[None, :, None, :].astype(dtype), jnp.sin(freqs)[None, :, None, :].astype(dtype))

        def _interleaved_rope(x, cos, sin):
            x_even = x[..., ::2]
            x_odd = x[..., 1::2]
            first = x_even * cos - x_odd * sin
            second = x_odd * cos + x_even * sin
            return jnp.stack([first, second], axis=-1).reshape(x.shape)
        b, s, _ = hidden_states.shape
        groups = H // HKV
        q = jnp.einsum('bqm,muh->bquh', hidden_states, Wq) + bq
        k = jnp.einsum('bkm,mvh->bkvh', hidden_states, Wk) + bk
        v = jnp.einsum('bkm,mvh->bkvh', hidden_states, Wv) + bv
        cos, sin = _cos_sin(s, hidden_states.dtype)
        q = _interleaved_rope(q, cos, sin) * SCALE
        k = _interleaved_rope(k, cos, sin) * SCALE
        k = jnp.repeat(k, groups, axis=2)
        v = jnp.repeat(v, groups, axis=2)
        scores = jnp.einsum('bquh,bkuh->buqk', q, k)
        pos = jnp.arange(s)
        sw_mask = jnp.abs(pos[:, None] - pos[None, :]) <= SW
        scores = jnp.where(sw_mask[None, None, :, :], scores, NEG)
        sink_logits = jnp.broadcast_to(sinks[None, :, None, None], (b, H, s, 1))
        combined = jnp.concatenate([scores, sink_logits], axis=-1)
        probs = jax.nn.softmax(combined.astype(jnp.float32), axis=-1)
        attn = probs[..., :-1].astype(hidden_states.dtype)
        out = jnp.einsum('buqk,bkuh->bquh', attn, v)
        return jnp.einsum('bquh,uhm->bqm', out, Wo) + bo

    def _L0_ffn_ref(hidden_states, gate_w, bias, w_gate, w_up, w_down, ws_gate, ws_up, ws_down):
        import jax, jax.numpy as jnp
        import numpy as np
        E, K, H, F = (64, 6, 256, 96)
        G, KG = (8, 4)
        SHARED_F = 96
        SCALE = 2.5
        T = 2 * 128
        CAP = 2 * (T * K // E)

        def _grouped_topk(logits, bias):
            scores = jax.nn.sigmoid(logits.astype(jnp.float32))
            scores_b = scores + bias[None, :]
            gs = scores_b.reshape(-1, G, E // G)
            group_scores = jnp.sum(jax.lax.top_k(gs, 2)[0], axis=-1)
            gidx = jax.lax.top_k(group_scores, KG)[1]
            rows = jnp.arange(group_scores.shape[0])[:, None]
            group_mask = jnp.zeros_like(group_scores).at[rows, gidx].set(1.0)
            score_mask = jnp.repeat(group_mask, E // G, axis=-1) > 0
            tmp = jnp.where(score_mask, scores_b, -jnp.inf)
            topk_ids = jax.lax.top_k(tmp, K)[1]
            topk_w = jnp.take_along_axis(scores, topk_ids, axis=-1)
            topk_w = topk_w / jnp.sum(topk_w, axis=-1, keepdims=True)
            return (topk_w * SCALE, topk_ids)

        def _routed_moe(x, topk_w, topk_ids, w_gate, w_up, w_down):
            Tn = x.shape[0]
            flat_e = topk_ids.reshape(-1)
            order = jnp.argsort(flat_e)
            se = flat_e[order]
            pos = jnp.arange(Tn * K) - jnp.searchsorted(se, se, side='left')
            tok = order // K
            valid = pos < CAP
            slot = jnp.where(valid, pos, CAP)
            buf = jnp.zeros((E, CAP + 1, H), x.dtype).at[se, slot].set(x[tok])[:, :CAP]
            h = jax.nn.silu(jnp.einsum('ech,ehf->ecf', buf, w_gate)) * jnp.einsum('ech,ehf->ecf', buf, w_up)
            out = jnp.einsum('ecf,efh->ech', h, w_down)
            gathered = out[se, jnp.minimum(pos, CAP - 1)] * valid.astype(x.dtype)[:, None]
            w = topk_w.reshape(-1)[order].astype(x.dtype)[:, None]
            return jax.ops.segment_sum(gathered * w, tok, num_segments=Tn)
        orig_shape = hidden_states.shape
        x = hidden_states.reshape(-1, H)
        router_logits = x @ gate_w
        topk_w, topk_ids = _grouped_topk(router_logits, bias)
        y = _routed_moe(x, topk_w, topk_ids, w_gate, w_up, w_down)
        shared = jax.nn.silu(x @ ws_gate) * (x @ ws_up) @ ws_down
        return (y + shared).reshape(orig_shape)
    x = L0_attn_hidden_states
    mod = (_silu(L0_c) @ L0_wmod).reshape(L0_c.shape[0], 6, 1, -1)
    sa, ca, ga, sb, cb, gb = (mod[:, 0], mod[:, 1], mod[:, 2], mod[:, 3], mod[:, 4], mod[:, 5])
    ga = (2 * (ga >= 0) - 1) * jnp.maximum(jnp.abs(ga), 0.25)
    gb = (2 * (gb >= 0) - 1) * jnp.maximum(jnp.abs(gb), 0.25)
    h = _layernorm(x, axis=-1) * (1 + ca) + sa
    x = x + ga * _L0_attn_ref(h, L0_attn_Wq, L0_attn_bq, L0_attn_Wk, L0_attn_bk, L0_attn_Wv, L0_attn_bv, L0_attn_Wo, L0_attn_bo, L0_attn_sinks)
    h = _layernorm(x, axis=-1) * (1 + cb) + sb
    x = x + gb * _L0_ffn_ref(h, L0_ffn_gate_w, L0_ffn_bias, L0_ffn_w_gate, L0_ffn_w_up, L0_ffn_w_down, L0_ffn_ws_gate, L0_ffn_ws_up, L0_ffn_ws_down)
    return x

_drawn_inputs = setup_inputs


def setup_inputs(seed=0):
    import zlib

    import numpy as np

    out = dict(_drawn_inputs(seed))
    spreads = {'L0_attn_bq': (0.0, 0.8),
     'L0_attn_bk': (0.0, 0.8),
     'L0_attn_bv': (0.0, 0.364),
     'L0_attn_bo': (0.0, 0.331)}
    factors = {'L0_attn_Wq': 8.0,
     'L0_attn_Wk': 8.0,
     'L0_attn_Wv': 8.0,
     'L0_attn_sinks': 8.0,
     'L0_ffn_gate_w': 8.0,
     'L0_ffn_bias': 8.0,
     'L0_ffn_w_gate': 8.0,
     'L0_ffn_w_up': 8.0,
     'L0_ffn_w_down': 8.0,
     'L0_ffn_ws_gate': 8.0,
     'L0_ffn_ws_up': 8.0,
     'L0_ffn_ws_down': 8.0}
    for name, (base, spread) in spreads.items():
        noise = np.random.default_rng([zlib.crc32(name.encode()), seed]).standard_normal(out[name].shape)
        drawn = base * np.exp(spread * noise) if base else spread * noise
        out[name] = jnp.asarray(drawn.astype(out[name].dtype))
    for name, factor in factors.items():
        out[name] = (out[name] * factor).astype(out[name].dtype)
    return out
```

```python
from contextlib import ExitStack

import numpy as np

import concourse.bass as bass
from concourse import mybir

F32, F32R, BF16, U32, I32 = (mybir.dt.float32, mybir.dt.float32r, mybir.dt.bfloat16,
                             mybir.dt.uint32, mybir.dt.int32)
ALU = mybir.AluOpType
ACT = mybir.ActivationFunctionType
AX = mybir.AxisListType

P = 128
B, S, M = 8, 256, 256
H, HKV, D = 32, 8, 64
R = H // HKV
NT = S // P
KM = M // P
QW = R * D
RW = QW + D
GW = RW + D
WINDOW = 128
NEG = -1.0e9
EPS = 1e-5
E, K, F = 64, 6, 96
G, KG = 8, 4
CAP = 2 * (2 * 128 * K // E)
SLOTS = E * CAP
ROUTE_SCALE = 2.5
BIG = 1.0e30
NX = E + 2 * F
SEED = 0x5F3759DF
assert HKV == 8 and NT == 2 and KM == 2 and R == 4


class Tickets:

    def __init__(self):
        self.seq = 0
        self.count = [0, 0]
        self.table = {}
        self.section("prologue", ["H", "Q0", "Q1", "KT"])
        self.section("first", batch_units(True, False))
        at = self.seq, list(self.count)
        self.section("mid", batch_units(False, False))
        n = self.seq - at[0]
        assert n % 2 == 0
        self.per = n // 2
        self.seq += (B - 3) * n
        self.count = [c + (B - 3) * self.per for c in self.count]
        self.section("last", batch_units(False, True))
        self.section("epilogue", ["AT0", "P0", "P1", "P2", "P3", "AT1", "H2T", "RS", "HST", "POS", "SD"])

    def section(self, section, names):
        for name in names:
            bank = self.seq % 2
            self.seq += 1
            self.count[bank] += 1
            self.table[section, name] = bank, self.count[bank]

    def use(self, section, name, b):
        bank, v = self.table[section, name]
        if section == "mid":
            return bank, v + (b - 1) * self.per, v + (b - 1) * self.per - 1
        return bank, v, v - 1 if v > 1 else None


def batch_units(first, last):
    names = []
    for s in range(HKV):
        if not (first and s < 2):
            names.append(f"AT{s}")
        if not (last and s > HKV - 2):
            names += [f"Q0{s}", f"Q1{s}", f"KT{s}"]
        if not (first and s < 1):
            names += [f"P{h}{s}" for h in range(R)]
        if not first:
            names += {4: ["H2T"], 5: ["RS"], 6: ["HST"], 7: ["POS", "SD"]}.get(s, [])
        if not last and s == 5:
            names.append("H")
    return names


def build(nc, t):
    xbuf = nc.dram_tensor("expert_rows_in", [SLOTS, M], F32, kind="Internal").ap()
    ybuf = nc.dram_tensor("expert_rows_out", [SLOTS, M], F32, kind="Internal").ap()
    mod_dram = nc.dram_tensor("modulation", [B, 6, M], F32, kind="Internal").ap()

    with ExitStack() as ctx:
        def sb(name, shape, dt=F32, c=ctx):
            return c.enter_context(nc.sbuf_tensor(name, shape, dt))

        x = sb("x", [P, B * NT, M])
        ident = sb("ident", [P, P])
        slot_index = sb("slot_index", [P, B * NT, 8], U32)
        slot_weight = sb("slot_weight", [P, B * NT, K])
        with ExitStack() as c:
            def sa(name, shape, dt=F32):
                return sb(name, shape, dt, c)

            k = dict(
                x=x, ident=ident, slot_index=slot_index, slot_weight=slot_weight,
                w_hi=sa("w_hi", [P, KM, HKV, GW], F32R), w_lo=sa("w_lo", [P, KM, HKV, GW], F32R),
                wo=sa("wo", [P, H * D // P, M]),
                bias=sa("bias", [P, HKV, GW]), bo=sa("bo", [P, M]),
                cos=sa("cos", [P, NT, D]), sin=sa("sin", [P, NT, D]),
                ident_r=sa("ident_r", [P, P], F32R), ident_b=sa("ident_b", [P, P], BF16),
                ones_b=sa("ones_b", [P, P], BF16), tri_b=sa("tri_b", [P, P], BF16),
                mask_b=sa("mask_b", [P, NT, P], BF16),
                sink=sa("sink", [P, HKV, R]), neg_sink=sa("neg_sink", [P, HKV, R]),
                w_router=sa("w_router", [P, KM, NX]), w_sdown=sa("w_sdown", [F, M]),
                r_bias=sa("r_bias", [P, E]), slot_base=sa("slot_base", [P, E]),
                mean=sa("mean", [P, B * NT]), rstd=sa("rstd", [P, B * NT]),
                nmr=sa("nmr", [P, B * NT]),
            )
            setup(nc, t, k, xbuf, mod_dram)
            attention(nc, t, k, xbuf, mod_dram)
        experts(nc, t, x, ident, slot_index, slot_weight, xbuf, ybuf, mod_dram)


def split(dve_or_pool, hi, lo, full):
    return dve_or_pool.tensor_tensor(lo, full, hi.bitcast(F32), ALU.subtract)


def wait_alone(eng, semaphore, value, met):
    if not isinstance(value, int):
        value = eng.to_reg(value)
    eng.wait_ge(met, 1)
    eng.wait_ge(semaphore, value)


def setup(nc, t, k, xbuf, mod_dram):
    with ExitStack() as c:
        def sb(name, shape, dt=F32):
            return c.enter_context(nc.sbuf_tensor(name, shape, dt))

        def sem(name):
            return c.enter_context(nc.semaphore(name))

        w_raw = sb("w_raw", [P, HKV, KM, GW])
        cond = sb("cond", [B, M])
        cond_e = sb("cond_e", [B, M])
        cond_s = sb("cond_s", [B, M])
        cond_t = sb("cond_t", [P, KM, B])
        w_mod = sb("w_mod", [P, KM, 6 * M])
        mod = sb("mod", [B, 6, M])
        sign = sb("sign", [B, 2, M])
        size = sb("size", [B, 2, M])
        zero = sb("zero", [P, M])
        stats = sb("stats", [P, B * NT, 6])
        mv = sb("mv", [P, B * NT, 2])
        eps = sb("eps", [P, 1])
        tri = sb("tri", [P, P])
        mask = sb("mask", [P, NT, P])
        std = sb("std", [P, B * NT])
        nwt = sb("nwt", [P, B * NT])
        ps_t = c.enter_context(nc.psum_tensor("ps_cond", [P, KM, B], F32))
        ps_m = c.enter_context(nc.psum_tensor("ps_mod", [B, 3, 512], F32))

        small_in, x_in, mod_in, w_in, wo_in = (sem(n) for n in ("small_in", "x_in", "mod_in", "w_in", "wo_in"))
        const_in, zeroed, zero_out = sem("const_in"), sem("zeroed"), sem("zero_out")
        cond_exp, cond_step, cond_turned, cond_copied = (sem(n) for n in ("cond_exp", "cond_step", "cond_turned", "cond_copied"))
        mod_done, mod_step, mod_out, hi_done, lo_done = (sem(n) for n in ("mod_done", "mod_step", "mod_out", "hi_done", "lo_done"))
        stat_step, std_done, eps_set, neg_done, idr_done = (sem(n) for n in ("stat_step", "std_done", "eps_set", "neg_done", "idr_done"))
        block = c.enter_context(nc.Block())
        N_CONST = 11

        @block.sync
        def _(sp):
            sp.dma_start(cond[:], t["c"]).then_inc(small_in, 16)
            sp.dma_start(k["ident"][:], t["ident"]).then_inc(small_in, 16)
            sp.dma_start(w_mod[:], t["wmod"].rearrange("(k p) n -> p k n", p=P)).then_inc(mod_in, 16)
            sp.dma_start(k["x"][:], t["x"].rearrange("(t p) m -> p t m", p=P)).then_inc(x_in, 16)
            for name, dst, src in (
                ("bias", k["bias"][:].rearrange("p g w -> p (g w)"), t["bias"].to_broadcast((P, HKV * GW))),
                ("bo", k["bo"][:], t["bo"].to_broadcast((P, M))),
                ("cos", k["cos"][:], t["cos"]), ("sin", k["sin"][:], t["sin"]),
                ("tri", tri[:], t["tri"]), ("mask", mask[:], t["mask"]),
                ("sink", k["sink"][:].rearrange("p g r -> p (g r)"), t["sinks"].to_broadcast((P, H))),
                ("w_router", k["w_router"][:], t["w_router"].rearrange("(k p) n -> p k n", p=P)),
                ("w_sdown", k["w_sdown"][:], t["ws_down"]),
                ("r_bias", k["r_bias"][:], t["r_bias"].to_broadcast((P, E))),
                ("slot_base", k["slot_base"][:], t["slot_base"].to_broadcast((P, E))),
            ):
                sp.dma_start(dst, src).then_inc(const_in, 16)
            sp.dma_start(k["wo"][:], t["wo"].rearrange("(d p) m -> p d m", p=P)).then_inc(wo_in, 16)
            sp.wait_ge(zeroed, 1)
            sp.dma_start(xbuf.rearrange("(p n) m -> p n m", p=P),
                         zero[:].unsqueeze(1).to_broadcast((P, SLOTS // P, M))).then_inc(zero_out, 16)
            sp.wait_ge(mod_step, 8)
            sp.dma_start(mod_dram, mod[:]).then_inc(mod_out, 16)
            sp.wait_ge(mod_out, 16)
            sp.wait_ge(zero_out, 16)
            sp.wait_ge(wo_in, 16)
            sp.wait_ge(const_in, 16 * N_CONST)

        @block.gpsimd
        def _(pool):
            pool.memset(zero[:], 0.0).then_inc(zeroed, 1)

        @block.scalar
        def _(act):
            for g in range(HKV):
                act.dma_start(w_raw[:, g], t["wqkv"][g].rearrange("(k p) w -> p k w", p=P)).then_inc(w_in, 16)
            act.wait_ge(small_in, 32)
            nc.scalar.activation(cond_e[:], cond[:], ACT.Exp, scale=-1.0).then_inc(cond_exp, 1)
            act.wait_ge(stat_step, 2 * B * NT)
            act.wait_ge(eps_set, 1)
            nc.scalar.activation(std[:], mv[:, :, 1], ACT.Sqrt, bias=eps[:]).then_inc(std_done, 1)
            act.wait_ge(w_in, 16 * HKV)
            for g in range(HKV):
                nc.scalar.activation(k["w_hi"][:, :, g], w_raw[:, g], ACT.Copy).then_inc(hi_done, 1)

        @block.vector
        def _(dve):
            link_count = [0]

            def link(ins):
                link_count[0] += 1
                ins.then_inc(cond_step, 1)
                dve.wait_ge(cond_step, link_count[0])

            nc.vector.memset(eps[:], EPS).then_inc(eps_set, 1)
            dve.wait_ge(cond_exp, 1)
            link(nc.vector.tensor_scalar_add(cond_e[:], cond_e[:], 1.0))
            link(nc.vector.reciprocal(cond_e[:], cond_e[:]))
            link(nc.vector.tensor_tensor(cond_s[:], cond_e[:], cond[:], ALU.mult))
            dve.wait_ge(cond_turned, 1)
            nc.vector.tensor_copy(cond_t[:], ps_t[:]).then_inc(cond_copied, 1)
            dve.wait_ge(x_in, 16)
            for i in range(B * NT):
                nc.vector.bn_stats(stats[:, i], k["x"][:, i]).then_inc(stat_step, 1)
            for i in range(B * NT):
                dve.wait_ge(stat_step, i + B * NT)
                nc.vector.bn_aggr(mv[:, i], stats[:, i]).then_inc(stat_step, 1)
            dve.wait_ge(mod_done, 1)
            nc.vector.tensor_copy(mod[:].rearrange("b a m -> b (a m)"),
                                  ps_m[:].rearrange("b a m -> b (a m)")).then_inc(mod_step, 1)
            dve.wait_ge(mod_step, 1)
            scales = mod[:].rearrange("b (l a) m -> b l a m", l=2)[:, :, 1]
            gates = mod[:].rearrange("b (l a) m -> b l a m", l=2)[:, :, 2]
            nc.vector.tensor_scalar_add(scales, scales, 1.0).then_inc(mod_step, 1)
            nc.vector.tensor_scalar(sign[:], gates, 0.0, 2.0, ALU.is_ge, ALU.mult).then_inc(mod_step, 1)
            nc.vector.scalar_tensor_tensor(size[:], gates, -1.0, gates, ALU.mult, ALU.max).then_inc(mod_step, 1)
            dve.wait_ge(mod_step, 4)
            nc.vector.tensor_scalar_add(sign[:], sign[:], -1.0).then_inc(mod_step, 1)
            nc.vector.tensor_scalar_max(size[:], size[:], 0.25).then_inc(mod_step, 1)
            dve.wait_ge(mod_step, 6)
            nc.vector.tensor_tensor(gates, size[:], sign[:], ALU.mult).then_inc(mod_step, 2)
            dve.wait_ge(stat_step, 2 * B * NT)
            dve.wait_ge(std_done, 1)
            rstd, nmr = k["rstd"], k["nmr"]
            link(nc.vector.reciprocal(rstd[:], std[:]))
            link(nc.vector.tensor_tensor(nwt[:], rstd[:], rstd[:], ALU.mult))
            link(nc.vector.tensor_scalar_add(std[:], mv[:, :, 1], EPS))
            link(nc.vector.tensor_tensor(nwt[:], nwt[:], std[:], ALU.mult))
            link(nc.vector.tensor_scalar(nwt[:], nwt[:], -0.5, 1.5, ALU.mult, ALU.add))
            link(nc.vector.tensor_tensor(rstd[:], rstd[:], nwt[:], ALU.mult))
            link(nc.vector.scalar_tensor_tensor(nmr[:], mv[:, :, 0], -1.0, rstd[:], ALU.mult, ALU.mult))
            dve.wait_ge(const_in, 16 * N_CONST)
            nc.vector.tensor_scalar_mul(k["neg_sink"][:], k["sink"][:], -1.0).then_inc(neg_done, 1)
            nc.vector.tensor_copy(k["ident_r"][:], k["ident"][:]).then_inc(idr_done, 1)
            nc.vector.tensor_copy(k["ident_b"][:], k["ident"][:]).then_inc(idr_done, 1)
            nc.vector.tensor_copy(k["tri_b"][:], tri[:]).then_inc(idr_done, 1)
            nc.vector.tensor_copy(k["mask_b"][:], mask[:]).then_inc(idr_done, 1)
            nc.vector.memset(k["ones_b"][:], 1.0).then_inc(idr_done, 1)
            for g in range(HKV):
                dve.wait_ge(hi_done, g + 1)
                split(nc.vector, k["w_hi"][:, :, g], k["w_lo"][:, :, g], w_raw[:, g]).then_inc(lo_done, 1)

        @block.tensor
        def _(pe):
            pe.wait_ge(small_in, 32)
            pe.wait_ge(cond_step, 3)
            for m in range(KM):
                last = nc.tensor.transpose(ps_t[:, m], cond_s[:, m * P:(m + 1) * P], k["ident"][0:B, 0:B])
            last.then_inc(cond_turned, 1)
            pe.wait_ge(cond_copied, 1)
            pe.wait_ge(mod_in, 16)
            for n in range(3):
                for m in range(KM):
                    last = nc.tensor.matmul(ps_m[:, n], cond_t[:, m], w_mod[:, m, n * 512:(n + 1) * 512],
                                            start=(m == 0), stop=(m == KM - 1))
            last.then_inc(mod_done, 1)


def attention(nc, t, k, xbuf, mod_dram):
    x, ident = k["x"], k["ident"]
    tickets = Tickets()
    with ExitStack() as c:
        def sb(name, shape, dt=F32):
            return c.enter_context(nc.sbuf_tensor(name, shape, dt))

        def psum(name, shape):
            return c.enter_context(nc.psum_tensor(name, shape, F32))

        def sem(name):
            return c.enter_context(nc.semaphore(name))

        mod_a = sb("mod_a", [P, 2, M])
        h_norm = sb("h_norm", [P, NT, M])
        ht_hi = sb("ht_hi", [P, KM, S], F32R)
        ht_lo = sb("ht_lo", [P, KM, S], F32R)
        qk_raw = sb("qk_raw", [P, NT, RW])
        v = sb("v", [P, 4, NT, D + 1])
        rope_a = sb("rope_a", [P, NT, RW])
        rope_b = sb("rope_b", [P, NT, RW])
        qk_split = sb("qk_split", [P, 2, NT, 2 * R + 3, D], F32R)
        q_t = sb("q_t", [P, 2, R, S], F32R)
        k_t = sb("k_t", [P, 2, 2, S], F32R)
        row_max = sb("row_max", [P, 2, NT, R])
        neg_max = sb("neg_max", [P, 2, NT, R])
        sink_arg = sb("sink_arg", [P, 2, NT, R])
        sink_exp = sb("sink_exp", [P, 2, NT, R])
        probs = sb("probs", [P, 2, NT, R, S])
        probs_t = sb("probs_t", [P, R, NT, S])
        denom = sb("denom", [P, NT, R])
        heads = sb("heads", [P, 2, NT, QW])
        heads_t = sb("heads_t", [P, QW // P, S])
        mod_b = sb("mod_b", [P, 4, M])
        attn = sb("attn", [P, NT, M])
        st2 = sb("st2", [P, NT, 6])
        mv2 = sb("mv2", [P, NT, 2])
        var2 = sb("var2", [P, NT])
        y2 = sb("y2", [P, NT])
        z2 = sb("z2", [P, NT])
        nmr2 = sb("nmr2", [P, NT])
        magic = sb("magic", [P, NT], I32)
        h2 = sb("h2", [P, NT, M])
        h2_t = sb("h2_t", [P, KM, S])
        rs = sb("rs", [P, NT, NX])
        sg = sb("sg", [P, NT, E + F])
        hs = sb("hs", [P, NT, F])
        hs_t = sb("hs_t", [F, S])
        shared = sb("shared", [P, NT, M])
        sbias = sb("sbias", [P, NT, E])
        top2 = sb("top2", [P, NT, G, 8])
        gscore = sb("gscore", [P, NT, 2 * G])
        gtop = sb("gtop", [P, NT, 8])
        grep = sb("grep", [P, NT, 2 * G])
        gmask = sb("gmask", [P, NT, G])
        gneg = sb("gneg", [P, NT, G])
        cand = sb("cand", [P, NT, E])
        etop = sb("etop", [P, NT, 8])
        erep = sb("erep", [P, NT, E])
        sel = sb("sel", [P, NT, E], BF16)
        taken = sb("taken", [P, E], BF16)
        wsum = sb("wsum", [P, NT])
        weight = sb("weight", [P, NT, E])
        valid = sb("valid", [P, NT, E])
        key = sb("key", [P, NT, E])
        ktop = sb("ktop", [P, NT, 8])
        match = sb("match", [P, NT, K, E])
        kmiss = sb("kmiss", [P, NT, 8])
        scatter_index = sb("scatter_index", [P, NT, 8], U32)

        pj = psum("pj", [P, 512])
        tb = [psum(f"tb{i}", [P, 512]) for i in range(2)]
        sc = psum("sc", [P, R, S])
        po = [psum(f"po{i}", [P, 512]) for i in range(NT)]
        op = psum("op", [P, NT, M])

        mod_a_in, mod_b_in = sem("mod_a_in"), sem("mod_b_in")
        preset, h_scaled, h_mult, h_ready, ht_hi_done, ht_ready = (
            sem(n) for n in ("preset", "h_scaled", "h_mult", "h_ready", "ht_hi_done", "ht_ready"))
        proj_done, proj_read, v_read, rope_terms, roped, qk_hi_done, qk_lo_done, key_again_done = (
            sem(n) for n in ("proj_done", "proj_read", "v_read", "rope_terms", "roped", "qk_hi_done", "qk_lo_done", "key_again_done"))
        filled = [sem(f"filled{i}") for i in range(2)]
        drained = [sem(f"drained{i}") for i in range(2)]
        scores_done, row_max_done, neg_max_done, sink_arg_done, probs_done, sink_exp_done = (
            sem(n) for n in ("scores_done", "row_max_done", "neg_max_done", "sink_arg_done", "probs_done", "sink_exp_done"))
        pv_done, denom_done, heads_done, op_done = (sem(n) for n in ("pv_done", "denom_done", "heads_done", "op_done"))
        attn_read, attn_gated, x1_done, norm_step, seed_done, h2_scaled, h2_mult, h2_done = (
            sem(n) for n in ("attn_read", "attn_gated", "x1_done", "norm_step", "seed_done", "h2_scaled", "h2_mult", "h2_done"))
        sg_exp, rs_copied, sg_step, hs_step, shared_gated, x_done = (
            sem(n) for n in ("sg_exp", "rs_copied", "sg_step", "hs_step", "shared_gated", "x_done"))
        route_step, sel_done, scattered, index_done = (sem(n) for n in ("route_step", "sel_done", "scattered", "index_done"))
        block = c.enter_context(nc.Block())

        def loop(eng, body, prologue=None, epilogue=None):
            if prologue:
                prologue()
            body(0, "first")
            with eng.Fori(1, B - 1) as b:
                body(b, "mid")
            body(B - 1, "last")
            if epilogue:
                epilogue()

        def lagging(section, s, lag):
            return not (section == "first" and s < lag)

        def leading(section, s, lead):
            return not (section == "last" and s + lead >= HKV)

        def behind(section):
            return section != "first"

        def await_full(eng, section, name, b):
            bank, v, _ = tickets.use(section, name, b)
            eng.wait_ge(filled[bank], v)
            return bank

        def await_drained(eng, section, name, b):
            bank, v, _ = tickets.use(section, name, b)
            eng.wait_ge(drained[bank], v)

        def wait_apart(eng, semaphore, value):
            wait_alone(eng, semaphore, value, preset)

        @block.sync
        def _(sp):
            def load_a(b):
                sp.dma_start(mod_a[:], mod_dram[bass.ds(b, 1), 0:2].to_broadcast((P, 2, M))).then_inc(mod_a_in, 16)

            def load_b(b):
                sp.dma_start(mod_b[:], mod_dram[bass.ds(b, 1), 2:6].to_broadcast((P, 4, M))).then_inc(mod_b_in, 16)

            def body(b, section):
                if section != "last":
                    sp.wait_ge(h_ready, 2 * b + 2)
                    load_a(b + 1)
                if section == "mid" or section == "last":
                    sp.wait_ge(shared_gated, b - 1) if section == "last" else sp.wait_ge(shared_gated, b - 1 + SHIFT)
                    load_b(b - 1)

            load_a(0)
            loop(sp, body)
            sp.wait_ge(shared_gated, B - 1 + SHIFT)
            load_b(B - 1)

        @block.gpsimd
        def _(pool):
            def norm_modulate(b):
                pool.wait_ge(h_scaled, 2 * b + 2)
                pool.wait_ge(mod_a_in, 16 * (b + 1))
                nc.gpsimd.tensor_tensor(h_norm[:], h_norm[:], mod_a[:, 1:2].to_broadcast((P, NT, M)), ALU.mult)\
                    .then_inc(h_mult, 1)
                pool.wait_ge(h_mult, b + 1)
                nc.gpsimd.tensor_tensor(h_norm[:], h_norm[:], mod_a[:, 0:1].to_broadcast((P, NT, M)), ALU.add)\
                    .then_inc(h_ready, 2)

            def rope_add(n, par, i):
                pool.wait_ge(rope_terms, 2 * (2 * n + i + 1))
                nc.gpsimd.tensor_tensor(rope_a[:, i], rope_a[:, i], rope_b[:, i], ALU.add).then_inc(roped, 1)

            def rope_lo(n, par, i):
                pool.wait_ge(qk_hi_done, 2 * n + i + 1)
                full = rope_a[:, i].rearrange("p (h d) -> p h d", d=D)
                split(nc.gpsimd, qk_split[:, par, i, 0:2 * R + 1:2], qk_split[:, par, i, 1:2 * R + 2:2], full)\
                    .then_inc(qk_lo_done, 1)

            def residual(b):
                pool.wait_ge(attn_read, b + 1)
                pool.wait_ge(mod_b_in, 16 * (b + 1))
                nc.gpsimd.tensor_tensor(attn[:], attn[:], mod_b[:, 0:1].to_broadcast((P, NT, M)), ALU.mult)\
                    .then_inc(attn_gated, 1)
                wait_apart(pool, attn_gated, b + 1)
                xb = x[:, bass.ds(b * NT, NT)]
                nc.gpsimd.tensor_tensor(xb, xb, attn[:], ALU.add).then_inc(x1_done, 1)

            def norm2_modulate(b):
                pool.wait_ge(h2_scaled, 2 * b + 2)
                nc.gpsimd.tensor_tensor(h2[:], h2[:], mod_b[:, 2:3].to_broadcast((P, NT, M)), ALU.mult)\
                    .then_inc(h2_mult, 1)
                pool.wait_ge(h2_mult, b + 1)
                nc.gpsimd.tensor_tensor(h2[:], h2[:], mod_b[:, 1:2].to_broadcast((P, NT, M)), ALU.add)\
                    .then_inc(h2_done, 1)

            def shared_act(b):
                pool.wait_ge(sg_step, 2 * b + 2)
                pool.wait_ge(rs_copied, b + 1)
                nc.gpsimd.tensor_tensor(hs[:], sg[:, :, E:], rs[:, :, E:E + F], ALU.mult).then_inc(hs_step, 1)
                pool.wait_ge(hs_step, 2 * b + 1)
                nc.gpsimd.tensor_tensor(hs[:], hs[:], rs[:, :, E + F:], ALU.mult).then_inc(hs_step, 1)

            def add_shared(b):
                wait_apart(pool, shared_gated, b + 1)
                xb = x[:, bass.ds(b * NT, NT)]
                nc.gpsimd.tensor_tensor(xb, xb, shared[:], ALU.add).then_inc(x_done, 1)

            def scatter(b):
                wait_apart(pool, index_done, b + 1)
                for i in range(NT):
                    for j in range(K):
                        nc.gpsimd.indirect_dma_start(
                            xbuf, bass.IndirectOffsetOnAxis(ap=scatter_index[:, i, j:j + 1], axis=0),
                            h2[:, i], None, bounds_check=SLOTS - 1, oob_is_err=False).then_inc(scattered, 16)

            def qk(n, par):
                for i in range(NT):
                    rope_add(n, par, i)
                    rope_lo(n, par, i)

            def body(b, section):
                for s in range(HKV):
                    if leading(section, s, 2):
                        qk(b * HKV + s + 2, s % 2)
                    if section != "last" and s == 3:
                        norm_modulate(b + 1)
                    if behind(section):
                        if s == 2:
                            residual(b - 1)
                        if s == 4:
                            norm2_modulate(b - 1)
                        if s == 6:
                            shared_act(b - 1)
                if behind(section):
                    add_shared(b - 1)
                    scatter(b - 1)

            def prologue():
                norm_modulate(0)
                qk(0, 0)
                qk(1, 1)

            def epilogue():
                residual(B - 1)
                norm2_modulate(B - 1)
                shared_act(B - 1)
                add_shared(B - 1)
                scatter(B - 1)
                pool.wait_ge(scattered, 16 * NT * K * B)

            loop(pool, body, prologue, epilogue)

        @block.scalar
        def _(act):
            def copy_out(section, name, b, dst, width=512, rows=P):
                bank = await_full(act, section, name, b)
                nc.scalar.activation(dst, tb[bank][0:rows, 0:width], ACT.Copy).then_inc(drained[bank], 1)

            def norm_scale(b):
                if not isinstance(b, int) or b > 0:
                    act.wait_ge(ht_ready, b)
                for i in range(NT):
                    nc.scalar.activation(h_norm[:, i], x[:, bass.ds(b * NT + i, 1)], ACT.Identity,
                                         bias=k["nmr"][:, bass.ds(b * NT + i, 1)],
                                         scale=k["rstd"][:, bass.ds(b * NT + i, 1)]).then_inc(h_scaled, 1)

            def ht_high(section, name, b, nb):
                bank = await_full(act, section, name, b)
                nc.scalar.activation(ht_hi[:].rearrange("p k s -> p (k s)"), tb[bank][:, :], ACT.Copy)\
                    .then_inc(ht_hi_done, 1)

            def qk_high(n, par, i):
                act.wait_ge(roped, 2 * n + i + 1)
                if i == 1:
                    nc.scalar.activation(qk_split[:, par, :, 2 * R + 2], rope_a[:, :, QW:RW], ACT.Copy)\
                        .then_inc(key_again_done, 1)
                nc.scalar.activation(qk_split[:, par, i, 0:2 * R + 1:2], rope_a[:, i].rearrange("p (h d) -> p h d", d=D),
                                     ACT.Copy).then_inc(qk_hi_done, 1)

            def turn_qk(section, names, b, par):
                for i in range(NT):
                    copy_out(section, names[i], b, q_t[:, par, :, i * P:(i + 1) * P])
                copy_out(section, names[2], b, k_t[:, par])

            def exps(n, par, i):
                act.wait_ge(neg_max_done, 2 * n + i + 1)
                for h in range(R):
                    nc.scalar.activation(probs[:, par, i, h], sc[:, h], ACT.Exp,
                                         bias=neg_max[:, par, i, h:h + 1]).then_inc(probs_done, 1)

            def exp_sink(n, par):
                act.wait_ge(sink_arg_done, 2 * n + 2)
                nc.scalar.activation(sink_exp[:, par], sink_arg[:, par], ACT.Exp).then_inc(sink_exp_done, 1)

            def norm2_scale(b):
                act.wait_ge(norm_step, NORM_STEPS * (b + 1))
                if not isinstance(b, int) or b > 0:
                    act.wait_ge(scattered, 16 * NT * K * b)
                for i in range(NT):
                    nc.scalar.activation(h2[:, i], x[:, bass.ds(b * NT + i, 1)], ACT.Identity,
                                         bias=nmr2[:, i:i + 1], scale=y2[:, i:i + 1]).then_inc(h2_scaled, 1)

            def router_out(section, b, fb):
                bank = await_full(act, section, "RS", b)
                full = tb[bank][:, :].rearrange("p (i n) -> p i n", i=NT)
                nc.scalar.activation(sg[:], full[:, :, 0:E + F], ACT.Exp, scale=-1.0).then_inc(sg_exp, 1)
                nc.scalar.activation(rs[:], full, ACT.Copy).then_inc(rs_copied, 1)

            def body(b, section):
                for s in range(HKV):
                    n = b * HKV + s
                    if leading(section, s, 1):
                        turn_qk(section, [f"Q0{s}", f"Q1{s}", f"KT{s}"], b, (s + 1) % 2)
                    exps(n, s % 2, 0)
                    if lagging(section, s, 1):
                        for h in (0, 2):
                            copy_out(section, f"P{h}{s}", b, probs_t[:, h].rearrange("p i s -> p (i s)"))
                    exps(n, s % 2, 1)
                    exp_sink(n, s % 2)
                    if leading(section, s, 2):
                        for i in range(NT):
                            qk_high(n + 2, s % 2, i)
                    if behind(section):
                        if s == 4:
                            norm2_scale(b - 1)
                            copy_out(section, "H2T", b, h2_t[:].rearrange("p k s -> p (k s)"))
                        if s == 5:
                            router_out(section, b, b - 1)
                        if s == 6:
                            copy_out(section, "HST", b, hs_t[:], S, F)
                    if section != "last":
                        if s == 2:
                            norm_scale(b + 1)
                        if s == 5:
                            ht_high(section, "H", b, b + 1)

            def prologue():
                norm_scale(0)
                ht_high("prologue", "H", 0, 0)
                for n in range(2):
                    for i in range(NT):
                        qk_high(n, n, i)
                turn_qk("prologue", ["Q0", "Q1", "KT"], 0, 0)

            def epilogue():
                for h in (0, 2):
                    copy_out("epilogue", f"P{h}", 0, probs_t[:, h].rearrange("p i s -> p (i s)"))
                norm2_scale(B - 1)
                copy_out("epilogue", "H2T", 0, h2_t[:].rearrange("p k s -> p (k s)"))
                router_out("epilogue", 0, B - 1)
                copy_out("epilogue", "HST", 0, hs_t[:], S, F)

            act.wait_ge(preset, 1)
            loop(act, body, prologue, epilogue)

        @block.vector
        def _(dve):
            def copy_out(section, name, b, dst, width=512):
                bank = await_full(dve, section, name, b)
                nc.vector.tensor_copy(dst, tb[bank][:, 0:width]).then_inc(drained[bank], 1)

            def ht_low(section, name, b, nb):
                bank, v_, _ = tickets.use(section, name, b)
                dve.wait_ge(ht_hi_done, nb + 1)
                split(nc.vector, ht_hi[:].rearrange("p k s -> p (k s)"), ht_lo[:].rearrange("p k s -> p (k s)"),
                      tb[bank][:, :]).then_inc(ht_ready, 1)
                dve.wait_ge(ht_ready, nb + 1)
                dve.sem_inc(drained[bank], 1)

            def add_bias(n, s, i):
                dve.wait_ge(proj_done, 2 * n + i + 1)
                g = s % HKV
                nc.vector.tensor_tensor(qk_raw[:, i], pj[:, 0:RW], k["bias"][:, g, 0:RW], ALU.add)\
                    .then_inc(proj_read, 1)
                nc.vector.tensor_tensor(v[:, s % 4, i, 0:D], pj[:, RW:GW], k["bias"][:, g, RW:GW], ALU.add)\
                    .then_inc(v_read, 1)

            def rope(n, i):
                dve.wait_ge(proj_read, 2 * n + i + 1)
                if not (isinstance(n, int) and n == 0):
                    dve.wait_ge(qk_lo_done, 2 * n + i - 1)
                    dve.wait_ge(key_again_done, n)
                q = qk_raw[:, i].rearrange("p (h d) -> p h d", d=D)
                a = rope_a[:, i].rearrange("p (h d) -> p h d", d=D)
                nc.vector.tensor_tensor(a, q, k["cos"][:, i:i + 1].to_broadcast((P, R + 1, D)), ALU.mult)\
                    .then_inc(rope_terms, 1)
                q2 = qk_raw[:, i].rearrange("p (h e d) -> p h e d", e=2, d=D // 2)[:, :, ::-1]
                b2 = rope_b[:, i].rearrange("p (h e d) -> p h e d", e=2, d=D // 2)
                sn = k["sin"][:, i:i + 1].rearrange("p o (e d) -> p o e d", e=2).to_broadcast((P, R + 1, 2, D // 2))
                nc.vector.tensor_tensor(b2, q2, sn, ALU.mult).then_inc(rope_terms, 1)

            def maxima(n, s, par, i):
                dve.wait_ge(scores_done, 2 * n + i + 1)
                nc.vector.tensor_reduce(row_max[:, par, i], sc[:], AX.X, ALU.max).then_inc(row_max_done, 1)
                dve.wait_ge(row_max_done, 2 * n + i + 1)
                nc.vector.scalar_tensor_tensor(neg_max[:, par, i], row_max[:, par, i], -1.0,
                                               k["neg_sink"][:, s % HKV], ALU.mult, ALU.min).then_inc(neg_max_done, 1)
                dve.wait_ge(neg_max_done, 2 * n + i + 1)
                nc.vector.tensor_tensor(sink_arg[:, par, i], neg_max[:, par, i], k["sink"][:, s % HKV], ALU.add)\
                    .then_inc(sink_arg_done, 1)

            def normalise(n, par, i):
                dve.wait_ge(pv_done, 2 * n + i + 1)
                dve.wait_ge(sink_exp_done, n + 1)
                full = po[i][:, 0:R * (D + 1)].rearrange("p (h w) -> p h w", w=D + 1)
                d = denom[:, i].unsqueeze(2)
                nc.vector.tensor_tensor(d, full[:, :, D:D + 1], sink_exp[:, par, i].unsqueeze(2), ALU.add)\
                    .then_inc(denom_done, 1)
                dve.wait_ge(denom_done, 2 * (2 * n + i) + 1)
                nc.vector.reciprocal(denom[:, i], denom[:, i]).then_inc(denom_done, 1)
                dve.wait_ge(denom_done, 2 * (2 * n + i) + 2)
                nc.vector.tensor_tensor(heads[:, par, i].rearrange("p (h d) -> p h d", d=D), full[:, :, 0:D],
                                        d.to_broadcast((P, R, D)), ALU.mult).then_inc(heads_done, 1)

            def attention_out(b):
                dve.wait_ge(op_done, HKV * (b + 1))
                if not isinstance(b, int) or b > 0:
                    dve.wait_ge(x1_done, b)
                nc.vector.tensor_tensor(attn[:], op[:], k["bo"][:].unsqueeze(1).to_broadcast((P, NT, M)), ALU.add)\
                    .then_inc(attn_read, 1)

            def norm2_stats(b):
                done = [NORM_STEPS * b]

                def link(ins):
                    done[0] = done[0] + 1
                    ins.then_inc(norm_step, 1)
                    wait_apart(dve, norm_step, done[0])

                dve.wait_ge(x1_done, b + 1)
                if not isinstance(b, int) or b > 0:
                    dve.wait_ge(h2_scaled, 2 * b)
                for i in range(NT):
                    link(nc.vector.bn_stats(st2[:, i], x[:, bass.ds(b * NT + i, 1)]))
                for i in range(NT):
                    link(nc.vector.bn_aggr(mv2[:, i], st2[:, i]))
                link(nc.vector.tensor_scalar_add(var2[:], mv2[:, :, 1], EPS))
                link(nc.vector.tensor_scalar(z2[:].bitcast(I32), var2[:].bitcast(I32), 1, None,
                                             ALU.logical_shift_right))
                link(nc.vector.tensor_scalar(y2[:].bitcast(I32), z2[:].bitcast(I32), -1.0, float(SEED),
                                             ALU.mult, ALU.add))
                for _ in range(4):
                    link(nc.vector.tensor_tensor(z2[:], y2[:], y2[:], ALU.mult))
                    link(nc.vector.scalar_tensor_tensor(z2[:], z2[:], -0.5, var2[:], ALU.mult, ALU.mult))
                    link(nc.vector.scalar_tensor_tensor(y2[:], z2[:], 1.5, y2[:], ALU.add, ALU.mult))
                link(nc.vector.scalar_tensor_tensor(nmr2[:], mv2[:, :, 0], -1.0, y2[:], ALU.mult, ALU.mult))
                return done[0]

            def sigmoids(b):
                dve.wait_ge(sg_exp, b + 1)
                nc.vector.tensor_scalar_add(sg[:], sg[:], 1.0).then_inc(sg_step, 1)
                dve.wait_ge(sg_step, 2 * b + 1)
                nc.vector.reciprocal(sg[:], sg[:]).then_inc(sg_step, 1)
                dve.wait_ge(sg_step, 2 * b + 2)

            def release_rs(section, b, fb):
                bank, _, _ = tickets.use(section, "RS", b)
                dve.wait_ge(rs_copied, fb + 1)
                dve.sem_inc(drained[bank], 1)

            def route(section, b, fb, part):
                done = [ROUTE_STEPS * fb + (ROUTE_A if part else 0)]

                def link(*many):
                    for ins in many:
                        ins.then_inc(route_step, 1)
                        done[0] = done[0] + 1
                    wait_apart(dve, route_step, done[0])

                two = range(NT)
                if part == 0:
                    score = sg[:, :, 0:E]
                    link(nc.vector.tensor_tensor(sbias[:], score, k["r_bias"][:].unsqueeze(1).to_broadcast((P, NT, E)), ALU.add))
                    link(*[nc.vector.max(top2[:, i, g], sbias[:, i, g * 8:g * 8 + 8]) for i in two for g in range(G)])
                    link(nc.vector.tensor_tensor(gscore[:, :, 0:G], top2[:, :, :, 0], top2[:, :, :, 1], ALU.add))
                    link(*[nc.vector.max(gtop[:, i], gscore[:, i]) for i in two])
                    link(nc.vector.memset(gtop[:, :, KG:], -BIG))
                    link(*[nc.vector.match_replace(grep[:, i], gtop[:, i], gscore[:, i], -2.0 * BIG) for i in two])
                    link(nc.vector.tensor_tensor(gmask[:], grep[:, :, 0:G], gscore[:, :, 0:G], ALU.not_equal))
                    full = (P, NT, G, E // G)
                    each = lambda a: a[:].rearrange("p i (g e) -> p i g e", g=G)
                    link(nc.vector.tensor_scalar(gneg[:], gmask[:], -1.0, BIG, ALU.add, ALU.mult),
                         nc.vector.tensor_tensor(each(cand), each(sbias), gmask[:].unsqueeze(3).to_broadcast(full), ALU.mult))
                    link(nc.vector.tensor_tensor(each(cand), each(cand), gneg[:].unsqueeze(3).to_broadcast(full), ALU.add))
                    link(*[nc.vector.max(etop[:, i], cand[:, i]) for i in two])
                    link(nc.vector.memset(etop[:, :, K:], -BIG))
                    link(*[nc.vector.match_replace(erep[:, i], etop[:, i], cand[:, i], -2.0 * BIG) for i in two])
                    link(nc.vector.tensor_tensor(erep[:], erep[:], cand[:], ALU.not_equal))
                    link(nc.vector.tensor_tensor(each(sel), each(erep), gmask[:].unsqueeze(3).to_broadcast(full), ALU.mult))
                    link(nc.vector.tensor_tensor(weight[:], score, sel[:], ALU.mult))
                    link(nc.vector.tensor_reduce(wsum[:], weight[:], AX.X, ALU.add))
                    link(nc.vector.reciprocal(wsum[:], wsum[:]))
                    link(nc.vector.scalar_tensor_tensor(weight[:], weight[:], ROUTE_SCALE,
                                                        wsum[:].unsqueeze(2).to_broadcast((P, NT, E)), ALU.mult, ALU.mult))
                else:
                    bank = await_full(dve, section, "POS", b)
                    pos = tb[bank][:, 0:NT * E].rearrange("p (i e) -> p i e", i=NT)
                    if not isinstance(fb, int) or fb > 0:
                        dve.wait_ge(scattered, 16 * NT * K * fb)
                    link(nc.vector.scalar_tensor_tensor(valid[:], pos, float(CAP), sel[:], ALU.is_lt, ALU.mult),
                         nc.vector.tensor_tensor(key[:], pos, k["slot_base"][:].unsqueeze(1).to_broadcast((P, NT, E)), ALU.add),
                         nc.vector.tensor_tensor(taken[:], taken[:], sel[:, 0], ALU.add))
                    dve.sem_inc(drained[bank], 1)
                    link(nc.vector.tensor_tensor(key[:], key[:], valid[:], ALU.mult),
                         nc.vector.tensor_tensor(weight[:], weight[:], valid[:], ALU.mult),
                         nc.vector.tensor_tensor(taken[:], taken[:], sel[:, 1], ALU.add))
                    link(*[nc.vector.max(ktop[:, i], key[:, i]) for i in two])
                    link(nc.vector.tensor_scalar(kmiss[:], ktop[:], 0.0, 1.0e6, ALU.is_equal, ALU.mult))
                    link(nc.vector.scalar_tensor_tensor(kmiss[:], ktop[:], -1.0, kmiss[:], ALU.add, ALU.add))
                    link(nc.vector.tensor_copy(scatter_index[:], kmiss[:]),
                         nc.vector.tensor_copy(k["slot_index"][:, bass.ds(fb * NT, NT)], kmiss[:]))
                    dve.sem_inc(index_done, 1)
                    wide = (P, K, E)
                    link(*[nc.vector.tensor_tensor(match[:, i], key[:, i:i + 1].to_broadcast(wide),
                                                   ktop[:, i, 0:K].unsqueeze(2).to_broadcast(wide), ALU.is_equal) for i in two])
                    link(*[nc.vector.tensor_tensor(match[:, i], match[:, i], weight[:, i:i + 1].to_broadcast(wide), ALU.mult) for i in two])
                    link(nc.vector.tensor_reduce(k["slot_weight"][:, bass.ds(fb * NT, NT)], match[:], AX.X, ALU.add))
                return done[0]

            def shared_out(section, b, fb):
                bank = await_full(dve, section, "SD", b)
                if not isinstance(fb, int) or fb > 0:
                    dve.wait_ge(x_done, fb)
                nc.vector.tensor_tensor(shared[:], tb[bank][:, :].rearrange("p (i m) -> p i m", i=NT),
                                        mod_b[:, 3:4].to_broadcast((P, NT, M)), ALU.mult).then_inc(shared_gated, 1)
                dve.wait_ge(shared_gated, fb + 1)
                dve.sem_inc(drained[bank], 1)

            def body(b, section):
                for s in range(HKV):
                    n = b * HKV + s
                    if behind(section) and s == 2:
                        attention_out(b - 1)
                    if leading(section, s, 2):
                        add_bias(n + 2, s + 2, 0)
                    maxima(n, s, s % 2, 0)
                    if leading(section, s, 2):
                        rope(n + 2, 0)
                    if lagging(section, s, 2):
                        copy_out(section, f"AT{s}", b, heads_t[:].rearrange("p k s -> p (k s)"))
                    if leading(section, s, 2):
                        add_bias(n + 2, s + 2, 1)
                        rope(n + 2, 1)
                    if lagging(section, s, 1):
                        for h in (1, 3):
                            copy_out(section, f"P{h}{s}", b, probs_t[:, h].rearrange("p i s -> p (i s)"))
                    maxima(n, s, s % 2, 1)
                    if lagging(section, s, 1):
                        for i in range(NT):
                            normalise(n - 1, (s - 1) % 2, i)
                    if behind(section):
                        if s == 3:
                            norm2_stats(b - 1)
                        if s == 5:
                            sigmoids(b - 1)
                            release_rs(section, b, b - 1)
                        if s == 6:
                            route(section, b, b - 1, 0)
                        if s == 7:
                            route(section, b, b - 1, 1)
                            shared_out(section, b, b - 1)
                    if section != "last" and s == 5:
                        ht_low(section, "H", b, b + 1)

            def prologue():
                ht_low("prologue", "H", 0, 0)
                for n in range(2):
                    for i in range(NT):
                        add_bias(n, n, i)
                        rope(n, i)

            def epilogue():
                copy_out("epilogue", "AT0", 0, heads_t[:].rearrange("p k s -> p (k s)"))
                for h in (1, 3):
                    copy_out("epilogue", f"P{h}", 0, probs_t[:, h].rearrange("p i s -> p (i s)"))
                for i in range(NT):
                    normalise(B * HKV - 1, 1, i)
                copy_out("epilogue", "AT1", 0, heads_t[:].rearrange("p k s -> p (k s)"))
                attention_out(B - 1)
                norm2_stats(B - 1)
                sigmoids(B - 1)
                release_rs("epilogue", 0, B - 1)
                route("epilogue", 0, B - 1, 0)
                route("epilogue", 0, B - 1, 1)
                shared_out("epilogue", 0, B - 1)

            nc.vector.memset(v[:, :, :, D:D + 1], 1.0)
            nc.vector.memset(taken[:], 0.0)
            nc.vector.memset(gscore[:, :, G:], -BIG).then_inc(preset, 1)
            loop(dve, body, prologue, epilogue)

        @block.tensor
        def _(pe):
            def claim(section, name, b):
                bank, _, before = tickets.use(section, name, b)
                if before is not None:
                    pe.wait_ge(drained[bank], before)
                return bank

            def turn_norm(section, name, b, nb):
                pe.wait_ge(h_ready, 2 * nb + 2)
                bank = claim(section, name, b)
                for m in range(KM):
                    for i in range(NT):
                        last = nc.tensor.transpose(tb[bank][:, m * S + i * P:m * S + (i + 1) * P],
                                                   h_norm[:, i, m * P:(m + 1) * P], ident[:])
                last.then_inc(filled[bank], 1)

            def project(nb, n, s, i):
                pe.wait_ge(ht_ready, nb + 1)
                if not (isinstance(n, int) and n == 0 and i == 0):
                    pe.wait_ge(proj_read, 2 * n + i)
                    pe.wait_ge(v_read, 2 * n + i)
                rows = slice(i * P, (i + 1) * P)
                terms = [(a, w, m) for m in range(KM) for a, w in
                         ((ht_hi, k["w_hi"]), (ht_hi, k["w_lo"]), (ht_lo, k["w_hi"]))]
                for j, (a, w, m) in enumerate(terms):
                    last = nc.tensor.matmul(pj[:, 0:GW], a[:, m, rows], w[:, m, s % HKV],
                                            start=(j == 0), stop=(j == len(terms) - 1))
                last.then_inc(proj_done, 1)

            def turn_q(section, name, b, n, par, i):
                pe.wait_ge(qk_lo_done, 2 * n + i + 1)
                bank = claim(section, name, b)
                for h in range(R):
                    last = nc.tensor.matmul(tb[bank][:, h * P:(h + 1) * P],
                                            qk_split[:, par, i, 2 * h:2 * h + 2].rearrange("p e d -> p (e d)"),
                                            k["ident_r"][:], start=True, stop=True)
                last.then_inc(filled[bank], 1)

            def turn_k(section, name, b, n, par):
                pe.wait_ge(key_again_done, n + 1)
                bank = claim(section, name, b)
                for e in range(2):
                    for i in range(NT):
                        pair = qk_split[:, par, i, 2 * R + e:2 * R + e + 2].rearrange("p e d -> p (e d)")
                        last = nc.tensor.matmul(tb[bank][:, e * S + i * P:e * S + (i + 1) * P], pair,
                                                k["ident_r"][:], start=True, stop=True)
                last.then_inc(filled[bank], 1)

            def turn_qk(section, names, b, n, par):
                for i in range(NT):
                    turn_q(section, names[i], b, n, par, i)
                turn_k(section, names[2], b, n, par)

            def scores(section, turned, b, n, par, i):
                if i == 0 and not (isinstance(n, int) and n == 0):
                    pe.wait_ge(probs_done, 2 * R * n)
                if i == 1:
                    pe.wait_ge(probs_done, 2 * R * n + R)
                rows = slice(i * P, (i + 1) * P)
                far = slice((1 - i) * P, (2 - i) * P)
                for h in range(R):
                    nc.tensor.matmul(sc[:, h], q_t[:, par, h, rows], k_t[:, par, 0], start=True, stop=False)
                    nc.tensor.matmul(sc[:, h, far], k["ident_b"][:], k["mask_b"][:, i], start=False, stop=False)
                    last = nc.tensor.matmul(sc[:, h], q_t[:, par, h, rows], k_t[:, par, 1], start=False, stop=True)
                last.then_inc(scores_done, 1)

            def turn_probs(section, name, b, n, par, h):
                pe.wait_ge(probs_done, 2 * R * (n + 1))
                bank = claim(section, name, b)
                for j in range(NT):
                    for i in range(NT):
                        last = nc.tensor.transpose(tb[bank][:, j * S + i * P:j * S + (i + 1) * P],
                                                   probs[:, par, i, h, j * P:(j + 1) * P], ident[:])
                last.then_inc(filled[bank], 1)

            def values(section, names, b, n, quad, i):
                if i == 0:
                    for name in names:
                        await_drained(pe, section, name, b)
                if not (isinstance(n, int) and n == 0):
                    pe.wait_ge(heads_done, 2 * n + i - 1)
                for h in range(R):
                    for j in range(NT):
                        last = nc.tensor.matmul(po[i][:, h * (D + 1):(h + 1) * (D + 1)],
                                                probs_t[:, h, j, i * P:(i + 1) * P], v[:, quad, j],
                                                start=(j == 0), stop=(j == NT - 1))
                last.then_inc(pv_done, 1)

            def turn_heads(section, name, b, n, par):
                pe.wait_ge(heads_done, 2 * n + 2)
                bank = claim(section, name, b)
                for m in range(QW // P):
                    for i in range(NT):
                        last = nc.tensor.transpose(tb[bank][:, m * S + i * P:m * S + (i + 1) * P],
                                                   heads[:, par, i, m * P:(m + 1) * P], ident[:])
                last.then_inc(filled[bank], 1)

            def project_out(section, name, b, n, g, nb):
                await_drained(pe, section, name, b)
                if g == 0 and not (isinstance(nb, int) and nb == 0):
                    pe.wait_ge(attn_read, nb)
                for i in range(NT):
                    for m in range(QW // P):
                        last = nc.tensor.matmul(op[:, i], heads_t[:, m, i * P:(i + 1) * P],
                                                k["wo"][:, g * (QW // P) + m],
                                                start=(g == 0 and i == 0 and m == 0),
                                                stop=(g == HKV - 1 and m == QW // P - 1), skip_group_check=True)
                last.then_inc(op_done, 1)

            def turn_norm2(section, b, fb):
                pe.wait_ge(h2_done, fb + 1)
                bank = claim(section, "H2T", b)
                for m in range(KM):
                    for i in range(NT):
                        last = nc.tensor.transpose(tb[bank][:, m * S + i * P:m * S + (i + 1) * P],
                                                   h2[:, i, m * P:(m + 1) * P], ident[:])
                last.then_inc(filled[bank], 1)

            def router(section, b):
                await_drained(pe, section, "H2T", b)
                bank = claim(section, "RS", b)
                for i in range(NT):
                    for m in range(KM):
                        last = nc.tensor.matmul(tb[bank][:, i * NX:(i + 1) * NX], h2_t[:, m, i * P:(i + 1) * P],
                                                k["w_router"][:, m], start=(m == 0), stop=(m == KM - 1))
                last.then_inc(filled[bank], 1)

            def turn_shared(section, b, fb):
                pe.wait_ge(hs_step, 2 * fb + 2)
                bank = claim(section, "HST", b)
                for i in range(NT):
                    last = nc.tensor.transpose(tb[bank][0:F, i * P:(i + 1) * P], hs[:, i], ident[:])
                last.then_inc(filled[bank], 1)

            def positions(section, b, fb):
                pe.wait_ge(route_step, ROUTE_STEPS * fb + ROUTE_A)
                bank = claim(section, "POS", b)
                for i in range(NT):
                    out = tb[bank][:, i * E:(i + 1) * E]
                    nc.tensor.matmul(out, k["tri_b"][:], sel[:, i], start=True, stop=False)
                    last = nc.tensor.matmul(out, k["ones_b"][:], taken[:], start=False, stop=(i == 0))
                    if i == 1:
                        last = nc.tensor.matmul(out, k["ones_b"][:], sel[:, 0], start=False, stop=True)
                last.then_inc(filled[bank], 1)

            def shared_down(section, b):
                await_drained(pe, section, "HST", b)
                bank = claim(section, "SD", b)
                for i in range(NT):
                    last = nc.tensor.matmul(tb[bank][:, i * M:(i + 1) * M], hs_t[:, i * P:(i + 1) * P],
                                            k["w_sdown"][:], start=True, stop=True)
                last.then_inc(filled[bank], 1)

            def body(b, section):
                for s in range(HKV):
                    n = b * HKV + s
                    nb = b if s + 2 < HKV else b + 1
                    lb = b if s - 2 >= 0 else b - 1
                    if leading(section, s, 2):
                        project(nb, n + 2, s + 2, 0)
                    scores(section, None, b, n, s % 2, 0)
                    if lagging(section, s, 2):
                        turn_heads(section, f"AT{s}", b, n - 2, s % 2)
                    if leading(section, s, 1):
                        turn_qk(section, [f"Q0{s}", f"Q1{s}", f"KT{s}"], b, n + 1, (s + 1) % 2)
                    if leading(section, s, 2):
                        project(nb, n + 2, s + 2, 1)
                    if lagging(section, s, 1):
                        for h in range(R):
                            turn_probs(section, f"P{h}{s}", b, n - 1, (s - 1) % 2, h)
                    if lagging(section, s, 2):
                        project_out(section, f"AT{s}", b, n - 2, (s - 2) % HKV, lb)
                    scores(section, None, b, n, s % 2, 1)
                    if lagging(section, s, 1):
                        for i in range(NT):
                            values(section, [f"P{h}{s}" for h in range(R)], b, n - 1, (s - 1) % 4, i)
                    if behind(section):
                        if s == 4:
                            turn_norm2(section, b, b - 1)
                        if s == 5:
                            router(section, b)
                        if s == 6:
                            turn_shared(section, b, b - 1)
                        if s == 7:
                            positions(section, b, b - 1)
                            shared_down(section, b)
                    if section != "last" and s == 5:
                        turn_norm(section, "H", b, b + 1)
                    if leading(section, s, 1):
                        for name in (f"Q0{s}", f"Q1{s}", f"KT{s}"):
                            await_drained(pe, section, name, b)

            def prologue():
                turn_norm("prologue", "H", 0, 0)
                for n in range(2):
                    for i in range(NT):
                        project(0, n, n, i)
                turn_qk("prologue", ["Q0", "Q1", "KT"], 0, 0, 0)
                for name in ("Q0", "Q1", "KT"):
                    await_drained(pe, "prologue", name, 0)

            def epilogue():
                n = B * HKV
                turn_heads("epilogue", "AT0", 0, n - 2, 0)
                for h in range(R):
                    turn_probs("epilogue", f"P{h}", 0, n - 1, 1, h)
                project_out("epilogue", "AT0", 0, n - 2, HKV - 2, B - 1)
                for i in range(NT):
                    values("epilogue", [f"P{h}" for h in range(R)], 0, n - 1, 3, i)
                turn_heads("epilogue", "AT1", 0, n - 1, 1)
                project_out("epilogue", "AT1", 0, n - 1, HKV - 1, B - 1)
                turn_norm2("epilogue", 0, B - 1)
                router("epilogue", 0)
                turn_shared("epilogue", 0, B - 1)
                positions("epilogue", 0, B - 1)
                shared_down("epilogue", 0)

            pe.wait_ge(preset, 1)
            loop(pe, body, prologue, epilogue)


SHIFT = 0
NORM_STEPS = 2 * NT + 3 + 3 * 4 + 1
ROUTE_A = 1 + NT * G + 1 + NT + 1 + NT + 1 + 2 + 1 + NT + 1 + NT + 1 + 1 + 1 + 1 + 1 + 1
ROUTE_STEPS = ROUTE_A + 3 + 3 + NT + 1 + 1 + 2 + NT + NT + 1


CHUNK = 4
CS = CHUNK * CAP
RING = 4
NCHUNK = E // CHUNK
HALF = CS // 2


def experts(nc, t, x, ident, slot_index, slot_weight, xbuf, ybuf, mod_dram):
    with ExitStack() as c:
        def sb(name, shape, dt=F32):
            return c.enter_context(nc.sbuf_tensor(name, shape, dt))

        def sem(name):
            return c.enter_context(nc.semaphore(name))

        wg = sb("wg", [P, RING, CHUNK, KM * F])
        wu = sb("wu", [P, RING, CHUNK, KM * F])
        wd = sb("wd", [F, RING, CHUNK, M])
        rows = sb("rows", [HALF, RING, 2, M])
        rows_t = sb("rows_t", [P, 2, KM, CS])
        ex = sb("ex", [F, 2, CS])
        hid = sb("hid", [F, 2, CS])
        out_rows = sb("out_rows", [CAP, 2, CHUNK, M])
        gathered = sb("gathered", [P, 2, K, M])
        index = sb("index", [P, 2, 8], U32)
        wts = sb("wts", [P, 2, K])
        total = sb("total", [P, 2, M])
        gate = sb("gate", [P, B, M])
        result = sb("result", [P, 2, M])
        pt = [c.enter_context(nc.psum_tensor(f"pt{i}", [P, 512], F32)) for i in range(2)]
        pg = [c.enter_context(nc.psum_tensor(f"pg{i}", [P, 512], F32)) for i in range(2)]
        pd = [c.enter_context(nc.psum_tensor(f"pd{i}", [P, 512], F32)) for i in range(4)]

        loaded = [sem(f"loaded{i}") for i in range(RING)]
        turned, turned_out, hidden_done, exp_done, act_step, hid_done, down_done = (
            sem(n) for n in ("turned", "turned_out", "hidden_done", "exp_done", "act_step", "hid_done", "down_done"))
        out_act, out_dve, stored = sem("out_act"), sem("out_dve"), [sem(f"stored{i}") for i in range(2)]
        gate_in, cleared, picked, gathered_in, summed, result_done, written = (
            sem(n) for n in ("gate_in", "cleared", "picked", "gathered_in", "summed", "result_done", "written"))
        gathered_in = [sem(f"gathered_in{i}") for i in range(2)]
        written = [sem(f"written{i}") for i in range(2)]
        sum_step = sem("sum_step")
        block = c.enter_context(nc.Block())
        y_rows = ybuf.rearrange("(e s) m -> s e m", s=CAP)
        w_gate = t["w_gate"].rearrange("e (p k) f -> p e (k f)", k=KM)
        w_up = t["w_up"].rearrange("e (p k) f -> p e (k f)", k=KM)
        w_down = t["w_down"].rearrange("e f m -> f e m")
        x_rows = xbuf.rearrange("(a h s) m -> s a h m", h=2, s=HALF)
        LOADS = 4

        def chunks(eng, step):
            for r in range(RING):
                step(r, r, True)
            with eng.Fori(1, NCHUNK // RING) as i:
                for r in range(RING):
                    step(i * RING + r, r, False)

        @block.sync
        def _(sp):
            sp.dma_start(gate[:], mod_dram[:, 5].unsqueeze(0).to_broadcast((P, B, M))).then_inc(gate_in, 16)

            def load(a, r, first):
                if not first:
                    sp.wait_ge(down_done, 2 * (a - RING) + 2)
                e = bass.ds(a * CHUNK, CHUNK)
                sp.dma_start(rows[:, r], x_rows[:, bass.ds(a, 1)]).then_inc(loaded[r], 16)
                sp.dma_start(wg[:, r], w_gate[:, e]).then_inc(loaded[r], 16)
                sp.dma_start(wu[:, r], w_up[:, e]).then_inc(loaded[r], 16)
                sp.dma_start(wd[:, r], w_down[:, e]).then_inc(loaded[r], 16)

            chunks(sp, load)
            out = t["out"].rearrange("(t p) m -> p t m", p=P)
            with sp.Fori(0, B) as b:
                for i in range(NT):
                    sp.wait_ge(result_done, b * NT + i + 1)
                    sp.dma_start(out[:, bass.ds(b * NT + i, 1)], result[:, i]).then_inc(written[i], 16)
            for i in range(NT):
                sp.wait_ge(written[i], 16 * B)

        @block.tensor
        def _(pe):
            def step(a, r, first):
                par = r % 2
                pe.wait_ge(loaded[r], 16 * LOADS * (a // RING + 1) if first else 16 * LOADS * ((a - r) // RING + 1))
                if not (first and r < 2):
                    pe.wait_ge(turned_out, a - 1)
                for m in range(KM):
                    for h in range(2):
                        src = rows[:, r, h].rearrange("s (p k) -> s k p", k=KM)[:, m]
                        last = nc.tensor.transpose(pt[par][:, m * CS + h * HALF:m * CS + (h + 1) * HALF],
                                                   src, ident[0:HALF, 0:HALF])
                last.then_inc(turned, 1)
                pe.wait_ge(turned_out, a + 1)
                if not (first and r < 2):
                    pe.wait_ge(hid_done, a - 1)
                for u, w in enumerate((wg, wu)):
                    for e in range(CHUNK):
                        for m in range(KM):
                            last = nc.tensor.matmul(
                                pg[par][0:F, u * CS + e * CAP:u * CS + (e + 1) * CAP],
                                w[:, r, e, m * F:(m + 1) * F], rows_t[:, par, m, e * CAP:(e + 1) * CAP],
                                start=(m == 0), stop=(m == KM - 1))
                last.then_inc(hidden_done, 1)
                pe.wait_ge(hid_done, a + 1)
                if not (first and r < 2):
                    pe.wait_ge(out_act, a - 1)
                    pe.wait_ge(out_dve, a - 1)
                for e in range(CHUNK):
                    last = nc.tensor.matmul(pd[2 * par + e // 2][0:CAP, (e % 2) * M:(e % 2 + 1) * M],
                                            hid[:, par, e * CAP:(e + 1) * CAP], wd[:, r, e], start=True, stop=True)
                    if e % 2:
                        last.then_inc(down_done, 1)

            chunks(pe, step)

        @block.scalar
        def _(act):
            def step(a, r, first):
                par = r % 2
                act.wait_ge(turned, a + 1)
                nc.scalar.activation(rows_t[:, par].rearrange("p k s -> p (k s)"), pt[par][:, 0:KM * CS],
                                     ACT.Copy).then_inc(turned_out, 1)
                act.wait_ge(hidden_done, a + 1)
                nc.scalar.activation(ex[:, par], pg[par][0:F, 0:CS], ACT.Exp, scale=-1.0).then_inc(exp_done, 1)
                act.wait_ge(down_done, 2 * a + 1)
                if not (first and r < 2):
                    act.wait_ge(stored[par], 16 * ((a - r) // 2 + r // 2) if not first else 16 * (r // 2))
                nc.scalar.activation(out_rows[:, par, 0:2].rearrange("s e m -> s (e m)"), pd[2 * par][0:CAP, :],
                                     ACT.Copy).then_inc(out_act, 1)
                act.wait_ge(out_act, a + 1)
                act.wait_ge(out_dve, a + 1)
                act.dma_start(y_rows[:, bass.ds(a * CHUNK, CHUNK)], out_rows[:, par]).then_inc(stored[par], 16)

            chunks(act, step)

        @block.vector
        def _(dve):
            nc.vector.memset(gathered[:], 0.0).then_inc(cleared, 1)

            def step(a, r, first):
                par = r % 2
                dve.wait_ge(exp_done, a + 1)
                nc.vector.tensor_scalar_add(ex[:, par], ex[:, par], 1.0).then_inc(act_step, 1)
                dve.wait_ge(act_step, 3 * a + 1)
                nc.vector.reciprocal(ex[:, par], ex[:, par]).then_inc(act_step, 1)
                dve.wait_ge(act_step, 3 * a + 2)
                nc.vector.tensor_tensor(ex[:, par], ex[:, par], pg[par][0:F, 0:CS], ALU.mult).then_inc(act_step, 1)
                dve.wait_ge(act_step, 3 * a + 3)
                nc.vector.tensor_tensor(hid[:, par], ex[:, par], pg[par][0:F, CS:2 * CS], ALU.mult)\
                    .then_inc(hid_done, 1)
                dve.wait_ge(down_done, 2 * a + 2)
                if not (first and r < 2):
                    dve.wait_ge(stored[par], 16 * ((a - r) // 2 + r // 2) if not first else 16 * (r // 2))
                nc.vector.tensor_copy(out_rows[:, par, 2:4].rearrange("s e m -> s (e m)"),
                                      pd[2 * par + 1][0:CAP, :]).then_inc(out_dve, 1)

            chunks(dve, step)

            dve.wait_ge(gate_in, 16)

            def pick(b):
                for i in range(NT):
                    nc.vector.tensor_copy(index[:, i], slot_index[:, bass.ds(b * NT + i, 1)]).then_inc(picked, 1)

            def tile(b, i, first):
                n = b * NT + i
                nc.vector.tensor_copy(wts[:, i], slot_weight[:, bass.ds(n, 1)]).then_inc(sum_step, 1)
                dve.wait_ge(gathered_in[i], 16 * K * (b + 1))
                if not first:
                    dve.wait_ge(written[i], 16 * b)
                step0 = (K + 2) * n + 1
                dve.wait_ge(sum_step, step0)
                nc.vector.tensor_scalar(total[:, i], gathered[:, i, 0], wts[:, i, 0:1], None, ALU.mult).then_inc(sum_step, 1)
                for j in range(1, K):
                    dve.wait_ge(sum_step, step0 + j)
                    nc.vector.scalar_tensor_tensor(total[:, i], gathered[:, i, j], wts[:, i, j:j + 1], total[:, i],
                                                   ALU.mult, ALU.add).then_inc(sum_step, 1)
                dve.wait_ge(sum_step, step0 + K)
                nc.vector.tensor_tensor(total[:, i], total[:, i], gate[:, bass.ds(b, 1)].rearrange("p o m -> p (o m)"), ALU.mult)\
                    .then_inc(sum_step, 1)
                dve.wait_ge(sum_step, step0 + K + 1)
                nc.vector.tensor_tensor(result[:, i], total[:, i], x[:, bass.ds(n, 1)].rearrange("p o m -> p (o m)"), ALU.add)\
                    .then_inc(result_done, 1)

            pick(0)
            for i in range(NT):
                tile(0, i, True)
            with dve.Fori(1, B) as b:
                pick(b)
                for i in range(NT):
                    tile(b, i, False)

        @block.gpsimd
        def _(pool):
            pool.wait_ge(cleared, 1)
            for par in range(2):
                pool.wait_ge(stored[par], 16 * NCHUNK // 2)

            def tile(b, i, first):
                wait_alone(pool, picked, b * NT + NT, cleared)
                if not first:
                    wait_alone(pool, result_done, (b - 1) * NT + i + 1, cleared)
                for j in range(K):
                    nc.gpsimd.indirect_dma_start(
                        gathered[:, i, j], None, ybuf,
                        bass.IndirectOffsetOnAxis(ap=index[:, i, j:j + 1], axis=0),
                        bounds_check=SLOTS - 1, oob_is_err=False).then_inc(gathered_in[i], 16)

            for i in range(NT):
                tile(0, i, True)
            with pool.Fori(1, B) as b:
                for i in range(NT):
                    tile(b, i, False)


def constants():
    half = D // 2
    inv = (1.0 / np.float32(150000.0) ** (np.arange(half, dtype=np.float32) * 2.0 / D)).astype(np.float32)
    angle = np.arange(S, dtype=np.float32)[:, None] * inv[None, :]
    scale = np.float32(D ** -0.25)
    cos, sin = np.cos(angle) * scale, np.sin(angle) * scale
    tiles = lambda a: np.ascontiguousarray(a.reshape(NT, P, D).transpose(1, 0, 2)).astype(np.float32)
    i, j = np.arange(P)[:, None], np.arange(P)[None, :]
    mask = np.stack([np.where(P + j - i > WINDOW, NEG, 0.0), np.where(P + i - j > WINDOW, NEG, 0.0)], 1)
    return {
        "cos": tiles(np.concatenate([cos, cos], 1)), "sin": tiles(np.concatenate([-sin, sin], 1)),
        "ident": np.eye(P, dtype=np.float32), "tri": (i < j).astype(np.float32), "mask": mask.astype(np.float32),
        "slot_base": (np.arange(E) * CAP + 1).astype(np.float32)[None, :],
    }


def kernel(**inputs):
    import concourse.bacc as bacc
    from concourse.bass_utils import run_bass_kernel_spmd

    a = {n: np.asarray(v) for n, v in inputs.items()}
    turn = lambda w: np.concatenate([w[..., 0::2], w[..., 1::2]], -1)
    wq = turn(a["L0_attn_Wq"]).reshape(M, HKV, QW)
    wk, wv = turn(a["L0_attn_Wk"]), a["L0_attn_Wv"]
    bq = turn(a["L0_attn_bq"]).reshape(HKV, QW)
    bk, bv = turn(a["L0_attn_bk"]), a["L0_attn_bv"]
    arrays = {
        "x": a["L0_attn_hidden_states"].reshape(B * S, M),
        "wqkv": np.concatenate([wq, wk, wv], -1).transpose(1, 0, 2),
        "bias": np.concatenate([bq, bk, bv], -1).reshape(1, HKV * GW),
        "wo": a["L0_attn_Wo"].reshape(H * D, M), "bo": a["L0_attn_bo"].reshape(1, M),
        "sinks": a["L0_attn_sinks"].reshape(1, H),
        "w_router": np.concatenate([a["L0_ffn_gate_w"], a["L0_ffn_ws_gate"], a["L0_ffn_ws_up"]], -1),
        "ws_down": a["L0_ffn_ws_down"], "r_bias": a["L0_ffn_bias"].reshape(1, E),
        "w_gate": a["L0_ffn_w_gate"], "w_up": a["L0_ffn_w_up"], "w_down": a["L0_ffn_w_down"],
        "c": a["L0_c"], "wmod": a["L0_wmod"],
        **constants(),
    }
    nc = bacc.Bacc("TRN2", target_bir_lowering=False, num_devices=1)
    feed, t = {}, {}
    for name, value in arrays.items():
        value = np.ascontiguousarray(value)
        feed[f"in_{name}"] = value
        t[name] = nc.dram_tensor(f"in_{name}", value.shape, mybir.dt.from_np(value.dtype), kind="ExternalInput").ap()
    t["out"] = nc.dram_tensor("out", [B * S, M], F32, kind="ExternalOutput").ap()
    build(nc, t)
    got = run_bass_kernel_spmd(nc, [feed], core_ids=[0])
    return got.results[0]["out"].reshape(B, S, M)
```

```python
from contextlib import ExitStack

import numpy as np

import concourse.bass as bass
from concourse import mybir

F32, F32R, BF16, U32, I32 = (mybir.dt.float32, mybir.dt.float32r, mybir.dt.bfloat16,
                             mybir.dt.uint32, mybir.dt.int32)
ALU = mybir.AluOpType
ACT = mybir.ActivationFunctionType
AX = mybir.AxisListType

P = 128
B, S, M = 8, 256, 256
H, HKV, D = 32, 8, 64
R = H // HKV
NT = S // P
KM = M // P
QW = R * D
RW = QW + D
GW = RW + D
WINDOW = 128
NEG = -1.0e9
EPS = 1e-5
E, K, F = 64, 6, 96
G, KG = 8, 4
CAP = 2 * (2 * 128 * K // E)
SLOTS = E * CAP
ROUTE_SCALE = 2.5
BIG = 1.0e30
NX = E + 2 * F
SEED = 0x5F3759DF
assert HKV == 8 and NT == 2 and KM == 2 and R == 4


class Tickets:

    def __init__(self):
        self.seq = 0
        self.count = [0, 0]
        self.table = {}
        self.section("start", ["H", "Q0", "Q1", "KT"])
        self.section("steps 0, 1", [u for n in range(AHEAD) for u in step_units(n, n, None)])
        self.section("first", round_units(0))
        self.section("second", round_units(1))
        at = self.seq
        self.section("mid", round_units("mid"))
        n = self.seq - at
        assert n % 2 == 0
        self.per = n // 2
        self.seq += (MID_ROUNDS - 1) * n
        self.count = [c + (MID_ROUNDS - 1) * self.per for c in self.count]
        self.section("last", round_units(B - 1))
        self.section("end", FFN_UNITS)

    def section(self, section, names):
        for name in names:
            bank = self.seq % 2
            self.seq += 1
            self.count[bank] += 1
            self.table[section, name] = bank, self.count[bank]

    def use(self, section, name, b):
        bank, v = self.table[section, name]
        if section == "mid":
            return bank, v + (b - 2) * self.per, v + (b - 2) * self.per - 1
        return bank, v, v - 1 if v > 1 else None


AHEAD = 2
MID_ROUNDS = B - 3
NG_ALL = B * HKV
NORM_AT = 3
MID_AT = {2: "RS", 4: "POS", 5: "SD"}
END_AT = {1: "H2T", 3: "HST"}
FFN_UNITS = ["H2T", "RS", "HST", "POS", "SD"]


def exists(n):
    return not isinstance(n, int) or 0 <= n < NG_ALL


def step_units(n, tag, b):
    ffn = b is not None and b != 0
    names = []
    if exists(n - 2):
        names.append(f"AT{tag}")
    if exists(n - 1):
        names += [f"P{h}{tag}" for h in range(R)]
    if exists(n + 1):
        names += [f"Q0{tag}", f"Q1{tag}"]
    if ffn and tag in MID_AT:
        names.append(MID_AT[tag])
    if b is not None and b != B - 1 and tag == NORM_AT:
        names.append("H")
    if exists(n + 1):
        names.append(f"KT{tag}")
    if ffn and tag in END_AT:
        names.append(END_AT[tag])
    return names


def round_units(b):
    names = []
    for l in range(HKV):
        names += step_units(NG_ALL // 2 if b == "mid" else b * HKV + AHEAD + l, l, b)
    return names


def build(nc, t):
    xbuf = nc.dram_tensor("expert_rows_in", [SLOTS, M], F32, kind="Internal").ap()
    ybuf = nc.dram_tensor("expert_rows_out", [SLOTS, M], F32, kind="Internal").ap()
    mod_dram = nc.dram_tensor("modulation", [B, 6, M], F32, kind="Internal").ap()

    with ExitStack() as ctx:
        def sb(name, shape, dt=F32, c=ctx):
            return c.enter_context(nc.sbuf_tensor(name, shape, dt))

        x = sb("x", [P, B * NT, M])
        ident = sb("ident", [P, P])
        slot_index = sb("slot_index", [P, B * NT, 8], U32)
        slot_weight = sb("slot_weight", [P, B * NT, K])
        with ExitStack() as c:
            def sa(name, shape, dt=F32):
                return sb(name, shape, dt, c)

            k = dict(
                x=x, ident=ident, slot_index=slot_index, slot_weight=slot_weight,
                w_hi=sa("w_hi", [P, KM, HKV, GW], F32R), w_lo=sa("w_lo", [P, KM, HKV, GW], F32R),
                wo=sa("wo", [P, H * D // P, M]),
                bias=sa("bias", [P, HKV, GW]), bo=sa("bo", [P, M]),
                cos=sa("cos", [P, NT, D]), sin=sa("sin", [P, NT, D]),
                ident_r=sa("ident_r", [P, P], F32R), ident_b=sa("ident_b", [P, P], BF16),
                ones_b=sa("ones_b", [P, P], BF16), tri_b=sa("tri_b", [P, P], BF16),
                mask_b=sa("mask_b", [P, NT, P], BF16),
                sink=sa("sink", [P, HKV, R]), neg_sink=sa("neg_sink", [P, HKV, R]),
                w_router=sa("w_router", [P, KM, NX]), w_sdown=sa("w_sdown", [F, M]),
                r_bias=sa("r_bias", [P, E]), slot_base=sa("slot_base", [P, E]),
                mean=sa("mean", [P, B * NT]), rstd=sa("rstd", [P, B * NT]),
                nmr=sa("nmr", [P, B * NT]),
            )
            setup(nc, t, k, xbuf, mod_dram)
            attention(nc, t, k, xbuf, mod_dram)
        experts(nc, t, x, ident, slot_index, slot_weight, xbuf, ybuf, mod_dram)


def split(dve_or_pool, hi, lo, full):
    return dve_or_pool.tensor_tensor(lo, full, hi.bitcast(F32), ALU.subtract)


def wait_alone(eng, semaphore, value, met):
    if not isinstance(value, int):
        value = eng.to_reg(value)
    eng.wait_ge(met, 1)
    eng.wait_ge(semaphore, value)


def setup(nc, t, k, xbuf, mod_dram):
    with ExitStack() as c:
        def sb(name, shape, dt=F32):
            return c.enter_context(nc.sbuf_tensor(name, shape, dt))

        def sem(name):
            return c.enter_context(nc.semaphore(name))

        w_raw = sb("w_raw", [P, HKV, KM, GW])
        cond = sb("cond", [B, M])
        cond_e = sb("cond_e", [B, M])
        cond_s = sb("cond_s", [B, M])
        cond_t = sb("cond_t", [P, KM, B])
        w_mod = sb("w_mod", [P, KM, 6 * M])
        mod = sb("mod", [B, 6, M])
        sign = sb("sign", [B, 2, M])
        size = sb("size", [B, 2, M])
        zero = sb("zero", [P, M])
        stats = sb("stats", [P, B * NT, 6])
        mv = sb("mv", [P, B * NT, 2])
        eps = sb("eps", [P, 1])
        tri = sb("tri", [P, P])
        mask = sb("mask", [P, NT, P])
        std = sb("std", [P, B * NT])
        nwt = sb("nwt", [P, B * NT])
        ps_t = c.enter_context(nc.psum_tensor("ps_cond", [P, KM, B], F32))
        ps_m = c.enter_context(nc.psum_tensor("ps_mod", [B, 3, 512], F32))

        small_in, x_in, mod_in, w_in, wo_in = (sem(n) for n in ("small_in", "x_in", "mod_in", "w_in", "wo_in"))
        const_in, zeroed, zero_out = sem("const_in"), sem("zeroed"), sem("zero_out")
        cond_exp, cond_step, cond_turned, cond_copied = (sem(n) for n in ("cond_exp", "cond_step", "cond_turned", "cond_copied"))
        mod_done, mod_step, mod_out, hi_done, lo_done = (sem(n) for n in ("mod_done", "mod_step", "mod_out", "hi_done", "lo_done"))
        stat_step, std_done, eps_set, neg_done, idr_done = (sem(n) for n in ("stat_step", "std_done", "eps_set", "neg_done", "idr_done"))
        block = c.enter_context(nc.Block())
        N_CONST = 11

        @block.sync
        def _(sp):
            sp.dma_start(cond[:], t["c"]).then_inc(small_in, 16)
            sp.dma_start(k["ident"][:], t["ident"]).then_inc(small_in, 16)
            sp.dma_start(w_mod[:], t["wmod"].rearrange("(k p) n -> p k n", p=P)).then_inc(mod_in, 16)
            sp.dma_start(k["x"][:], t["x"].rearrange("(t p) m -> p t m", p=P)).then_inc(x_in, 16)
            for name, dst, src in (
                ("bias", k["bias"][:].rearrange("p g w -> p (g w)"), t["bias"].to_broadcast((P, HKV * GW))),
                ("bo", k["bo"][:], t["bo"].to_broadcast((P, M))),
                ("cos", k["cos"][:], t["cos"]), ("sin", k["sin"][:], t["sin"]),
                ("tri", tri[:], t["tri"]), ("mask", mask[:], t["mask"]),
                ("sink", k["sink"][:].rearrange("p g r -> p (g r)"), t["sinks"].to_broadcast((P, H))),
                ("w_router", k["w_router"][:], t["w_router"].rearrange("(k p) n -> p k n", p=P)),
                ("w_sdown", k["w_sdown"][:], t["ws_down"]),
                ("r_bias", k["r_bias"][:], t["r_bias"].to_broadcast((P, E))),
                ("slot_base", k["slot_base"][:], t["slot_base"].to_broadcast((P, E))),
            ):
                sp.dma_start(dst, src).then_inc(const_in, 16)
            sp.dma_start(k["wo"][:], t["wo"].rearrange("(d p) m -> p d m", p=P)).then_inc(wo_in, 16)
            sp.wait_ge(zeroed, 1)
            sp.dma_start(xbuf.rearrange("(p n) m -> p n m", p=P),
                         zero[:].unsqueeze(1).to_broadcast((P, SLOTS // P, M))).then_inc(zero_out, 16)
            sp.wait_ge(mod_step, 8)
            sp.dma_start(mod_dram, mod[:]).then_inc(mod_out, 16)
            sp.wait_ge(mod_out, 16)
            sp.wait_ge(zero_out, 16)
            sp.wait_ge(wo_in, 16)
            sp.wait_ge(const_in, 16 * N_CONST)

        @block.gpsimd
        def _(pool):
            pool.memset(zero[:], 0.0).then_inc(zeroed, 1)

        @block.scalar
        def _(act):
            for g in range(HKV):
                act.dma_start(w_raw[:, g], t["wqkv"][g].rearrange("(k p) w -> p k w", p=P)).then_inc(w_in, 16)
            act.wait_ge(small_in, 32)
            nc.scalar.activation(cond_e[:], cond[:], ACT.Exp, scale=-1.0).then_inc(cond_exp, 1)
            act.wait_ge(stat_step, 2 * B * NT)
            act.wait_ge(eps_set, 1)
            nc.scalar.activation(std[:], mv[:, :, 1], ACT.Sqrt, bias=eps[:]).then_inc(std_done, 1)
            act.wait_ge(w_in, 16 * HKV)
            for g in range(HKV):
                nc.scalar.activation(k["w_hi"][:, :, g], w_raw[:, g], ACT.Copy).then_inc(hi_done, 1)

        @block.vector
        def _(dve):
            link_count = [0]

            def link(ins):
                link_count[0] += 1
                ins.then_inc(cond_step, 1)
                dve.wait_ge(cond_step, link_count[0])

            nc.vector.memset(eps[:], EPS).then_inc(eps_set, 1)
            dve.wait_ge(cond_exp, 1)
            link(nc.vector.tensor_scalar_add(cond_e[:], cond_e[:], 1.0))
            link(nc.vector.reciprocal(cond_e[:], cond_e[:]))
            link(nc.vector.tensor_tensor(cond_s[:], cond_e[:], cond[:], ALU.mult))
            dve.wait_ge(cond_turned, 1)
            nc.vector.tensor_copy(cond_t[:], ps_t[:]).then_inc(cond_copied, 1)
            dve.wait_ge(x_in, 16)
            for i in range(B * NT):
                nc.vector.bn_stats(stats[:, i], k["x"][:, i]).then_inc(stat_step, 1)
            for i in range(B * NT):
                dve.wait_ge(stat_step, i + B * NT)
                nc.vector.bn_aggr(mv[:, i], stats[:, i]).then_inc(stat_step, 1)
            dve.wait_ge(mod_done, 1)
            nc.vector.tensor_copy(mod[:].rearrange("b a m -> b (a m)"),
                                  ps_m[:].rearrange("b a m -> b (a m)")).then_inc(mod_step, 1)
            dve.wait_ge(mod_step, 1)
            scales = mod[:].rearrange("b (l a) m -> b l a m", l=2)[:, :, 1]
            gates = mod[:].rearrange("b (l a) m -> b l a m", l=2)[:, :, 2]
            nc.vector.tensor_scalar_add(scales, scales, 1.0).then_inc(mod_step, 1)
            nc.vector.tensor_scalar(sign[:], gates, 0.0, 2.0, ALU.is_ge, ALU.mult).then_inc(mod_step, 1)
            nc.vector.scalar_tensor_tensor(size[:], gates, -1.0, gates, ALU.mult, ALU.max).then_inc(mod_step, 1)
            dve.wait_ge(mod_step, 4)
            nc.vector.tensor_scalar_add(sign[:], sign[:], -1.0).then_inc(mod_step, 1)
            nc.vector.tensor_scalar_max(size[:], size[:], 0.25).then_inc(mod_step, 1)
            dve.wait_ge(mod_step, 6)
            nc.vector.tensor_tensor(gates, size[:], sign[:], ALU.mult).then_inc(mod_step, 2)
            dve.wait_ge(stat_step, 2 * B * NT)
            dve.wait_ge(std_done, 1)
            rstd, nmr = k["rstd"], k["nmr"]
            link(nc.vector.reciprocal(rstd[:], std[:]))
            link(nc.vector.tensor_tensor(nwt[:], rstd[:], rstd[:], ALU.mult))
            link(nc.vector.tensor_scalar_add(std[:], mv[:, :, 1], EPS))
            link(nc.vector.tensor_tensor(nwt[:], nwt[:], std[:], ALU.mult))
            link(nc.vector.tensor_scalar(nwt[:], nwt[:], -0.5, 1.5, ALU.mult, ALU.add))
            link(nc.vector.tensor_tensor(rstd[:], rstd[:], nwt[:], ALU.mult))
            link(nc.vector.scalar_tensor_tensor(nmr[:], mv[:, :, 0], -1.0, rstd[:], ALU.mult, ALU.mult))
            dve.wait_ge(const_in, 16 * N_CONST)
            nc.vector.tensor_scalar_mul(k["neg_sink"][:], k["sink"][:], -1.0).then_inc(neg_done, 1)
            nc.vector.tensor_copy(k["ident_r"][:], k["ident"][:]).then_inc(idr_done, 1)
            nc.vector.tensor_copy(k["ident_b"][:], k["ident"][:]).then_inc(idr_done, 1)
            nc.vector.tensor_copy(k["tri_b"][:], tri[:]).then_inc(idr_done, 1)
            nc.vector.tensor_copy(k["mask_b"][:], mask[:]).then_inc(idr_done, 1)
            nc.vector.memset(k["ones_b"][:], 1.0).then_inc(idr_done, 1)
            for g in range(HKV):
                dve.wait_ge(hi_done, g + 1)
                split(nc.vector, k["w_hi"][:, :, g], k["w_lo"][:, :, g], w_raw[:, g]).then_inc(lo_done, 1)

        @block.tensor
        def _(pe):
            pe.wait_ge(small_in, 32)
            pe.wait_ge(cond_step, 3)
            for m in range(KM):
                last = nc.tensor.transpose(ps_t[:, m], cond_s[:, m * P:(m + 1) * P], k["ident"][0:B, 0:B])
            last.then_inc(cond_turned, 1)
            pe.wait_ge(cond_copied, 1)
            pe.wait_ge(mod_in, 16)
            for n in range(3):
                for m in range(KM):
                    last = nc.tensor.matmul(ps_m[:, n], cond_t[:, m], w_mod[:, m, n * 512:(n + 1) * 512],
                                            start=(m == 0), stop=(m == KM - 1))
            last.then_inc(mod_done, 1)


def attention(nc, t, k, xbuf, mod_dram):
    x, ident = k["x"], k["ident"]
    tickets = Tickets()
    with ExitStack() as c:
        def sb(name, shape, dt=F32):
            return c.enter_context(nc.sbuf_tensor(name, shape, dt))

        def psum(name, shape):
            return c.enter_context(nc.psum_tensor(name, shape, F32))

        def sem(name):
            return c.enter_context(nc.semaphore(name))

        mod_a = sb("mod_a", [P, 2, M])
        h_norm = sb("h_norm", [P, NT, M])
        ht_hi = sb("ht_hi", [P, KM, S], F32R)
        ht_lo = sb("ht_lo", [P, KM, S], F32R)
        qk_raw = sb("qk_raw", [P, NT, RW])
        v = sb("v", [P, 4, NT, D + 1])
        rope_a = sb("rope_a", [P, NT, RW])
        rope_b = sb("rope_b", [P, NT, RW])
        qk_split = sb("qk_split", [P, 2, NT, 2 * R + 3, D], F32R)
        q_t = sb("q_t", [P, 2, R, S], F32R)
        k_t = sb("k_t", [P, 2, 2, S], F32R)
        row_max = sb("row_max", [P, 2, NT, R])
        neg_max = sb("neg_max", [P, 2, NT, R])
        sink_arg = sb("sink_arg", [P, 2, NT, R])
        sink_exp = sb("sink_exp", [P, 2, NT, R])
        probs = sb("probs", [P, 2, NT, R, S])
        probs_t = sb("probs_t", [P, R, NT, S])
        denom = sb("denom", [P, NT, R])
        heads = sb("heads", [P, 2, NT, QW])
        heads_t = sb("heads_t", [P, QW // P, S])
        gate_a = sb("gate_a", [P, 1, M])
        mod_b = sb("mod_b", [P, 3, M])
        attn = sb("attn", [P, NT, M])
        st2 = sb("st2", [P, NT, 6])
        mv2 = sb("mv2", [P, NT, 2])
        var2 = sb("var2", [P, NT])
        y2 = sb("y2", [P, NT])
        z2 = sb("z2", [P, NT])
        nmr2 = sb("nmr2", [P, NT])
        magic = sb("magic", [P, NT], I32)
        h2 = sb("h2", [P, NT, M])
        h2_t = sb("h2_t", [P, KM, S])
        rs = sb("rs", [P, NT, NX])
        sg = sb("sg", [P, NT, E + F])
        hs = sb("hs", [P, NT, F])
        hs_t = sb("hs_t", [F, S])
        shared = sb("shared", [P, NT, M])
        sbias = sb("sbias", [P, NT, E])
        top2 = sb("top2", [P, NT, G, 8])
        gscore = sb("gscore", [P, NT, 2 * G])
        gtop = sb("gtop", [P, NT, 8])
        grep = sb("grep", [P, NT, 2 * G])
        gmask = sb("gmask", [P, NT, G])
        gneg = sb("gneg", [P, NT, G])
        cand = sb("cand", [P, NT, E])
        etop = sb("etop", [P, NT, 8])
        erep = sb("erep", [P, NT, E])
        sel = sb("sel", [P, NT, E], BF16)
        taken = sb("taken", [P, E], BF16)
        wsum = sb("wsum", [P, NT])
        weight = sb("weight", [P, NT, E])
        pos = sb("pos", [P, NT, E])
        valid = sb("valid", [P, NT, E])
        key = sb("key", [P, NT, E])
        ktop = sb("ktop", [P, NT, 8])
        match = sb("match", [P, NT, K, E])
        kmiss = sb("kmiss", [P, NT, 8])
        scatter_index = sb("scatter_index", [P, NT, 8], U32)

        pj = psum("pj", [P, 512])
        tb = [psum(f"tb{i}", [P, 512]) for i in range(2)]
        sc = [psum(f"sc{i}", [P, 2, S]) for i in range(2)]
        po = [psum(f"po{i}", [P, 512]) for i in range(NT)]
        op = psum("op", [P, NT, M])

        mod_a_in, mod_b_in, gate_a_in = sem("mod_a_in"), sem("mod_b_in"), sem("gate_a_in")
        preset, h_scaled, h_mult, h_ready, ht_hi_done, ht_ready = (
            sem(n) for n in ("preset", "h_scaled", "h_mult", "h_ready", "ht_hi_done", "ht_ready"))
        proj_done, proj_read, v_read, sin_done, cos_done, roped, qk_hi_done, qk_lo_done, key_again_done = (
            sem(n) for n in ("proj_done", "proj_read", "v_read", "sin_done", "cos_done", "roped", "qk_hi_done", "qk_lo_done", "key_again_done"))
        filled = [sem(f"filled{i}") for i in range(2)]
        drained = [sem(f"drained{i}") for i in range(2)]
        scores_done, row_max_done, neg_max_done, sink_arg_done, probs_done, sink_exp_done = (
            sem(n) for n in ("scores_done", "row_max_done", "neg_max_done", "sink_arg_done", "probs_done", "sink_exp_done"))
        pv_done, denom_done, heads_done, op_done = (sem(n) for n in ("pv_done", "denom_done", "heads_done", "op_done"))
        attn_read, attn_gated, x1_done, norm_step, seed_done, h2_scaled, h2_mult, h2_done = (
            sem(n) for n in ("attn_read", "attn_gated", "x1_done", "norm_step", "seed_done", "h2_scaled", "h2_mult", "h2_done"))
        sg_exp, rs_copied, sg_step, hs_step, shared_gated, x_done = (
            sem(n) for n in ("sg_exp", "rs_copied", "sg_step", "hs_step", "shared_gated", "x_done"))
        route_step, sel_done, pos_copied, scattered, index_done = (
            sem(n) for n in ("route_step", "sel_done", "pos_copied", "scattered", "index_done"))
        block = c.enter_context(nc.Block())

        def rounds(eng, step, start, end):
            start()
            for n in range(AHEAD):
                step("steps 0, 1", n, 0, n, None)
            for b, section in enumerate(("first", "second")):
                for l in range(HKV):
                    step(section, l, b, b * HKV + AHEAD + l, l)
            with eng.Fori(2, B - 1) as b:
                for l in range(HKV):
                    step("mid", l, b, b * HKV + AHEAD + l, l)
            for l in range(HKV):
                step("last", l, B - 1, (B - 1) * HKV + AHEAD + l, l)
            end()

        def n_par(l, n):
            return (n if l is None else l) % 2

        def group_of(l, n, lag):
            return (n if l is None else AHEAD + l) % HKV + lag & HKV - 1

        def batch_of(l, n, b, lag):
            return (n + lag) // HKV if l is None else b + (AHEAD + l + lag) // HKV

        def await_full(eng, section, name, b):
            bank, v, _ = tickets.use(section, name, b)
            eng.wait_ge(filled[bank], v)
            return bank

        def await_drained(eng, section, name, b):
            bank, v, _ = tickets.use(section, name, b)
            eng.wait_ge(drained[bank], v)

        def wait_apart(eng, semaphore, value):
            wait_alone(eng, semaphore, value, preset)

        @block.sync
        def _(sp):
            def load_a(b):
                sp.dma_start(mod_a[:], mod_dram[bass.ds(b, 1), 0:2].to_broadcast((P, 2, M))).then_inc(mod_a_in, 16)

            def load_gate(b):
                sp.dma_start(gate_a[:], mod_dram[bass.ds(b, 1), 2:3].to_broadcast((P, 1, M))).then_inc(gate_a_in, 16)

            def load_b(b):
                sp.dma_start(mod_b[:], mod_dram[bass.ds(b, 1), 3:6].to_broadcast((P, 3, M))).then_inc(mod_b_in, 16)

            def step(section, tag, b, n, l):
                if l == 0:
                    if section != "last":
                        sp.wait_ge(h_ready, 2 * b + 2)
                        load_a(b + 1)
                    if section != "first":
                        sp.wait_ge(x1_done, b)
                    load_gate(b)
                    if not isinstance(b, int) or b > 1:
                        sp.wait_ge(shared_gated, b - 1)
                    if section != "first":
                        load_b(b - 1)

            def end():
                sp.wait_ge(shared_gated, B - 1)
                load_b(B - 1)

            rounds(sp, step, lambda: load_a(0), end)

        @block.gpsimd
        def _(pool):
            def norm_modulate(b):
                pool.wait_ge(h_scaled, 2 * b + 2)
                pool.wait_ge(mod_a_in, 16 * (b + 1))
                nc.gpsimd.tensor_tensor(h_norm[:], h_norm[:], mod_a[:, 1:2].to_broadcast((P, NT, M)), ALU.mult)\
                    .then_inc(h_mult, 1)
                pool.wait_ge(h_mult, b + 1)
                nc.gpsimd.tensor_tensor(h_norm[:], h_norm[:], mod_a[:, 0:1].to_broadcast((P, NT, M)), ALU.add)\
                    .then_inc(h_ready, 2)

            def rope_cos(n, i):
                pool.wait_ge(proj_read, 2 * n + i + 1)
                if not (isinstance(n, int) and n == 0):
                    pool.wait_ge(key_again_done, n)
                nc.gpsimd.tensor_tensor(rope_a[:, i].rearrange("p (h d) -> p h d", d=D),
                                        qk_raw[:, i].rearrange("p (h d) -> p h d", d=D),
                                        k["cos"][:, i:i + 1].to_broadcast((P, R + 1, D)), ALU.mult).then_inc(cos_done, 1)

            def rope_add(n, i):
                pool.wait_ge(cos_done, 2 * n + i + 1)
                pool.wait_ge(sin_done, 2 * n + i + 1)
                nc.gpsimd.tensor_tensor(rope_a[:, i], rope_a[:, i], rope_b[:, i], ALU.add).then_inc(roped, 1)

            def rope_lo(n, par, i):
                pool.wait_ge(qk_hi_done, 2 * n + i + 1)
                full = rope_a[:, i].rearrange("p (h d) -> p h d", d=D)
                split(nc.gpsimd, qk_split[:, par, i, 0:2 * R + 1:2], qk_split[:, par, i, 1:2 * R + 2:2], full)\
                    .then_inc(qk_lo_done, 1)

            def residual(b):
                pool.wait_ge(attn_read, b + 1)
                pool.wait_ge(gate_a_in, 16 * (b + 1))
                nc.gpsimd.tensor_tensor(attn[:], attn[:], gate_a[:].to_broadcast((P, NT, M)), ALU.mult)\
                    .then_inc(attn_gated, 1)
                wait_apart(pool, attn_gated, b + 1)
                xb = x[:, bass.ds(b * NT, NT)]
                nc.gpsimd.tensor_tensor(xb, xb, attn[:], ALU.add).then_inc(x1_done, 1)

            def norm2_modulate(b):
                pool.wait_ge(h2_scaled, 2 * b + 2)
                pool.wait_ge(mod_b_in, 16 * (b + 1))
                nc.gpsimd.tensor_tensor(h2[:], h2[:], mod_b[:, 1:2].to_broadcast((P, NT, M)), ALU.mult)\
                    .then_inc(h2_mult, 1)
                pool.wait_ge(h2_mult, b + 1)
                nc.gpsimd.tensor_tensor(h2[:], h2[:], mod_b[:, 0:1].to_broadcast((P, NT, M)), ALU.add)\
                    .then_inc(h2_done, 1)

            def shared_act(b):
                pool.wait_ge(sg_step, 3 * b + 3)
                pool.wait_ge(rs_copied, b + 1)
                nc.gpsimd.tensor_tensor(hs[:], sg[:, :, E:], rs[:, :, E:E + F], ALU.mult).then_inc(hs_step, 1)
                pool.wait_ge(hs_step, 2 * b + 1)
                nc.gpsimd.tensor_tensor(hs[:], hs[:], rs[:, :, E + F:], ALU.mult).then_inc(hs_step, 1)

            def add_shared(b):
                wait_apart(pool, shared_gated, b + 1)
                xb = x[:, bass.ds(b * NT, NT)]
                nc.gpsimd.tensor_tensor(xb, xb, shared[:], ALU.add).then_inc(x_done, 1)

            def scatter(b, pairs):
                wait_apart(pool, index_done, b + 1)
                for i, j in pairs:
                    nc.gpsimd.indirect_dma_start(
                        xbuf, bass.IndirectOffsetOnAxis(ap=scatter_index[:, i, j:j + 1], axis=0),
                        h2[:, i], None, bounds_check=SLOTS - 1, oob_is_err=False).then_inc(scattered, 16)

            pairs = [(i, j) for i in range(NT) for j in range(K)]

            def step(section, tag, b, n, l):
                ffn = l is not None and section != "first"
                nxt = l is not None and section != "last"
                if exists(n + 2):
                    rope_cos(n + 2, 0)
                    rope_add(n + 2, 0)
                    rope_cos(n + 2, 1)
                    rope_lo(n + 2, n_par(l, n), 0)
                    rope_add(n + 2, 1)
                if ffn and l == 7:
                    scatter(b - 1, pairs[10:])
                if exists(n + 2):
                    rope_lo(n + 2, n_par(l, n), 1)
                if ffn and l == 1:
                    norm2_modulate(b - 1)
                if nxt and l == 2:
                    norm_modulate(b + 1)
                if ffn and l == 3:
                    shared_act(b - 1)
                if ffn and l == 5:
                    scatter(b - 1, pairs[:5])
                if ffn and l == 6:
                    scatter(b - 1, pairs[5:10])
                if l == 7:
                    residual(b)
                if ffn and l == 7:
                    add_shared(b - 1)

            def start():
                norm_modulate(0)
                for n in range(2):
                    for i in range(NT):
                        rope_cos(n, i)
                        rope_add(n, i)
                        rope_lo(n, n, i)

            def end():
                norm2_modulate(B - 1)
                shared_act(B - 1)
                scatter(B - 1, pairs)
                add_shared(B - 1)
                pool.wait_ge(scattered, 16 * NT * K * B)

            rounds(pool, step, start, end)

        @block.scalar
        def _(act):
            def copy_out(section, name, b, dst, width=512, rows=P):
                bank = await_full(act, section, name, b)
                nc.scalar.activation(dst, tb[bank][0:rows, 0:width], ACT.Copy).then_inc(drained[bank], 1)

            def norm_scale(b):
                if not isinstance(b, int) or b > 0:
                    act.wait_ge(ht_ready, b)
                for i in range(NT):
                    nc.scalar.activation(h_norm[:, i], x[:, bass.ds(b * NT + i, 1)], ACT.Identity,
                                         bias=k["nmr"][:, bass.ds(b * NT + i, 1)],
                                         scale=k["rstd"][:, bass.ds(b * NT + i, 1)]).then_inc(h_scaled, 1)

            def ht_high(section, name, b, nb):
                bank = await_full(act, section, name, b)
                nc.scalar.activation(ht_hi[:].rearrange("p k s -> p (k s)"), tb[bank][:, :], ACT.Copy)\
                    .then_inc(ht_hi_done, 1)

            def qk_high(n, par, i):
                act.wait_ge(roped, 2 * n + i + 1)
                if i == 1:
                    nc.scalar.activation(qk_split[:, par, :, 2 * R + 2], rope_a[:, :, QW:RW], ACT.Copy)\
                        .then_inc(key_again_done, 1)
                nc.scalar.activation(qk_split[:, par, i, 0:2 * R + 1:2], rope_a[:, i].rearrange("p (h d) -> p h d", d=D),
                                     ACT.Copy).then_inc(qk_hi_done, 1)

            def turn_q(section, names, b, par):
                for i in range(NT):
                    copy_out(section, names[i], b, q_t[:, par, :, i * P:(i + 1) * P])

            def positions_out(section, b, fb):
                bank = await_full(act, section, "POS", b)
                if not isinstance(fb, int) or fb > 0:
                    act.wait_ge(index_done, fb)
                nc.scalar.activation(pos[:].rearrange("p i e -> p (i e)"), tb[bank][:, 0:NT * E], ACT.Copy)\
                    .then_inc(pos_copied, 1)
                act.wait_ge(pos_copied, fb + 1)
                act.sem_inc(drained[bank], 1)

            def exps(n, par, i):
                act.wait_ge(neg_max_done, 2 * n + i + 1)
                for h in range(R):
                    nc.scalar.activation(probs[:, par, i, h], sc[h // 2][:, h % 2], ACT.Exp,
                                         bias=neg_max[:, par, i, h:h + 1]).then_inc(probs_done, 1)

            def exp_sink(n, par):
                act.wait_ge(sink_arg_done, n + 1)
                nc.scalar.activation(sink_exp[:, par], sink_arg[:, par], ACT.Exp).then_inc(sink_exp_done, 1)

            def norm2_scale(b):
                act.wait_ge(norm_step, NORM_STEPS * (b + 1))
                if not isinstance(b, int) or b > 0:
                    act.wait_ge(scattered, 16 * NT * K * b)
                for i in range(NT):
                    nc.scalar.activation(h2[:, i], x[:, bass.ds(b * NT + i, 1)], ACT.Identity,
                                         bias=nmr2[:, i:i + 1], scale=y2[:, i:i + 1]).then_inc(h2_scaled, 1)

            def router_out(section, b, fb):
                bank = await_full(act, section, "RS", b)
                full = tb[bank][:, :].rearrange("p (i n) -> p i n", i=NT)
                nc.scalar.activation(sg[:], full[:, :, 0:E + F], ACT.Exp, scale=-1.0).then_inc(sg_exp, 1)
                nc.scalar.activation(rs[:], full, ACT.Copy).then_inc(rs_copied, 1)

            def turned_probs(section, name, b, h):
                copy_out(section, name, b, probs_t[:, h].rearrange("p i s -> p (i s)"))

            def step(section, tag, b, n, l):
                par = n_par(l, n)
                ffn = l is not None and section != "first"
                nxt = l is not None and section != "last"
                if ffn and l == 1:
                    norm2_scale(b - 1)
                if nxt and l == 2:
                    norm_scale(b + 1)
                if exists(n - 1):
                    turned_probs(section, f"P0{tag}", b, 0)
                if exists(n):
                    exps(n, par, 0)
                if exists(n - 1):
                    turned_probs(section, f"P1{tag}", b, 1)
                if exists(n + 2):
                    qk_high(n + 2, par, 0)
                if exists(n - 1):
                    turned_probs(section, f"P2{tag}", b, 2)
                if exists(n):
                    exps(n, par, 1)
                if exists(n - 1):
                    turned_probs(section, f"P3{tag}", b, 3)
                if exists(n):
                    exp_sink(n, par)
                if exists(n + 2):
                    qk_high(n + 2, par, 1)
                if exists(n + 1):
                    turn_q(section, [f"Q0{tag}", f"Q1{tag}"], b, (par + 1) % 2)
                if ffn and l == 2:
                    router_out(section, b, b - 1)
                if nxt and l == NORM_AT:
                    ht_high(section, "H", b, b + 1)
                if ffn and l == 4:
                    positions_out(section, b, b - 1)
                if exists(n + 1):
                    copy_out(section, f"KT{tag}", b, k_t[:, (par + 1) % 2])
                if ffn and l == 1:
                    copy_out(section, f"H2T", b, h2_t[:].rearrange("p k s -> p (k s)"))
                if ffn and l == 3:
                    copy_out(section, "HST", b, hs_t[:], S, F)

            def start():
                act.wait_ge(preset, 1)
                norm_scale(0)
                ht_high("start", "H", 0, 0)
                for n in range(2):
                    for i in range(NT):
                        qk_high(n, n, i)
                turn_q("start", ["Q0", "Q1"], 0, 0)
                copy_out("start", "KT", 0, k_t[:, 0])

            def end():
                norm2_scale(B - 1)
                copy_out("end", "H2T", 0, h2_t[:].rearrange("p k s -> p (k s)"))
                router_out("end", 0, B - 1)
                copy_out("end", "HST", 0, hs_t[:], S, F)
                positions_out("end", 0, B - 1)

            rounds(act, step, start, end)

        @block.vector
        def _(dve):
            def copy_out(section, name, b, dst, width=512):
                bank = await_full(dve, section, name, b)
                nc.vector.tensor_copy(dst, tb[bank][:, 0:width]).then_inc(drained[bank], 1)

            def ht_low(section, name, b, nb):
                bank, v_, _ = tickets.use(section, name, b)
                dve.wait_ge(ht_hi_done, nb + 1)
                split(nc.vector, ht_hi[:].rearrange("p k s -> p (k s)"), ht_lo[:].rearrange("p k s -> p (k s)"),
                      tb[bank][:, :]).then_inc(ht_ready, 1)
                dve.wait_ge(ht_ready, nb + 1)
                dve.sem_inc(drained[bank], 1)

            def add_bias(n, g, quad, i):
                dve.wait_ge(proj_done, 2 * n + i + 1)
                if not (isinstance(n, int) and n == 0):
                    dve.wait_ge(cos_done, 2 * n + i - 1)
                nc.vector.tensor_tensor(qk_raw[:, i], pj[:, 0:RW], k["bias"][:, g, 0:RW], ALU.add)\
                    .then_inc(proj_read, 1)
                nc.vector.tensor_tensor(v[:, quad, i, 0:D], pj[:, RW:GW], k["bias"][:, g, RW:GW], ALU.add)\
                    .then_inc(v_read, 1)

            def rope_sin(n, i):
                dve.wait_ge(proj_read, 2 * n + i + 1)
                if not (isinstance(n, int) and n == 0):
                    dve.wait_ge(roped, 2 * n + i - 1)
                q2 = qk_raw[:, i].rearrange("p (h e d) -> p h e d", e=2, d=D // 2)[:, :, ::-1]
                b2 = rope_b[:, i].rearrange("p (h e d) -> p h e d", e=2, d=D // 2)
                sn = k["sin"][:, i:i + 1].rearrange("p o (e d) -> p o e d", e=2).to_broadcast((P, R + 1, 2, D // 2))
                nc.vector.tensor_tensor(b2, q2, sn, ALU.mult).then_inc(sin_done, 1)

            def row_maxima(n, par, i, pair):
                dve.wait_ge(scores_done, 2 * (2 * n + i) + pair + 1)
                nc.vector.tensor_reduce(row_max[:, par, i, 2 * pair:2 * pair + 2], sc[pair][:], AX.X, ALU.max)\
                    .then_inc(row_max_done, 1)

            def negate_maxima(n, g, par, i):
                dve.wait_ge(row_max_done, 2 * (2 * n + i) + 2)
                nc.vector.scalar_tensor_tensor(neg_max[:, par, i], row_max[:, par, i], -1.0,
                                               k["neg_sink"][:, g], ALU.mult, ALU.min).then_inc(neg_max_done, 1)

            def sink_exponents(n, g, par):
                dve.wait_ge(neg_max_done, 2 * n + 2)
                nc.vector.tensor_tensor(sink_arg[:, par], neg_max[:, par],
                                        k["sink"][:, g:g + 1].to_broadcast((P, NT, R)), ALU.add)\
                    .then_inc(sink_arg_done, 1)

            def normalise(n, par, i):
                dve.wait_ge(pv_done, 2 * n + i + 1)
                dve.wait_ge(sink_exp_done, n + 1)
                full = po[i][:, 0:R * (D + 1)].rearrange("p (h w) -> p h w", w=D + 1)
                d = denom[:, i].unsqueeze(2)
                nc.vector.tensor_tensor(d, full[:, :, D:D + 1], sink_exp[:, par, i].unsqueeze(2), ALU.add)\
                    .then_inc(denom_done, 1)
                dve.wait_ge(denom_done, 2 * (2 * n + i) + 1)
                nc.vector.reciprocal(denom[:, i], denom[:, i]).then_inc(denom_done, 1)
                dve.wait_ge(denom_done, 2 * (2 * n + i) + 2)
                nc.vector.tensor_tensor(heads[:, par, i].rearrange("p (h d) -> p h d", d=D), full[:, :, 0:D],
                                        d.to_broadcast((P, R, D)), ALU.mult).then_inc(heads_done, 1)

            def attention_out(b):
                dve.wait_ge(op_done, HKV * (b + 1))
                if not isinstance(b, int) or b > 0:
                    dve.wait_ge(x1_done, b)
                nc.vector.tensor_tensor(attn[:], op[:], k["bo"][:].unsqueeze(1).to_broadcast((P, NT, M)), ALU.add)\
                    .then_inc(attn_read, 1)

            class Chain:

                def __init__(self, semaphore, total):
                    self.semaphore, self.total, self.done = semaphore, total, 0

                def __call__(self, fb, *instructions):
                    for ins in instructions:
                        ins.then_inc(self.semaphore, 1)
                        self.done += 1
                    wait_apart(dve, self.semaphore, self.total * fb + self.done)
                    if self.done == self.total:
                        self.done = 0

            norm, pick = Chain(norm_step, NORM_STEPS), Chain(route_step, ROUTE_STEPS)
            two = range(NT)

            def norm2_stats(b):
                dve.wait_ge(x1_done, b + 1)
                if not isinstance(b, int) or b > 0:
                    dve.wait_ge(h2_scaled, 2 * b)
                norm(b, *[nc.vector.bn_stats(st2[:, i], x[:, bass.ds(b * NT + i, 1)]) for i in two])
                norm(b, *[nc.vector.bn_aggr(mv2[:, i], st2[:, i]) for i in two])

            def norm2_guess(b):
                norm(b, nc.vector.tensor_scalar_add(var2[:], mv2[:, :, 1], EPS))
                norm(b, nc.vector.tensor_scalar(z2[:].bitcast(I32), var2[:].bitcast(I32), 1, None,
                                                ALU.logical_shift_right))
                norm(b, nc.vector.tensor_scalar(y2[:].bitcast(I32), z2[:].bitcast(I32), -1.0, float(SEED),
                                                ALU.mult, ALU.add))

            def norm2_newton(b):
                norm(b, nc.vector.tensor_tensor(z2[:], y2[:], y2[:], ALU.mult))
                norm(b, nc.vector.scalar_tensor_tensor(z2[:], z2[:], -0.5, var2[:], ALU.mult, ALU.mult))
                norm(b, nc.vector.scalar_tensor_tensor(y2[:], z2[:], 1.5, y2[:], ALU.add, ALU.mult))

            def norm2_shift(b):
                norm(b, nc.vector.scalar_tensor_tensor(nmr2[:], mv2[:, :, 0], -1.0, y2[:], ALU.mult, ALU.mult))

            def sigmoid_scores(b):
                dve.wait_ge(sg_exp, b + 1)
                nc.vector.tensor_scalar_add(sg[:], sg[:], 1.0).then_inc(sg_step, 1)
                dve.wait_ge(sg_step, 3 * b + 1)
                nc.vector.reciprocal(sg[:, :, 0:E], sg[:, :, 0:E]).then_inc(sg_step, 1)
                dve.wait_ge(sg_step, 3 * b + 2)

            def sigmoid_gate(b):
                nc.vector.reciprocal(sg[:, :, E:], sg[:, :, E:]).then_inc(sg_step, 1)

            def release_rs(section, b, fb):
                bank, _, _ = tickets.use(section, "RS", b)
                dve.wait_ge(rs_copied, fb + 1)
                dve.sem_inc(drained[bank], 1)

            full = (P, NT, G, E // G)

            def each(a):
                return a[:].rearrange("p i (g e) -> p i g e", g=G)

            def route_bests(fb):
                pick(fb, nc.vector.tensor_tensor(sbias[:], sg[:, :, 0:E], k["r_bias"][:].unsqueeze(1).to_broadcast((P, NT, E)), ALU.add))
                pick(fb, *[nc.vector.max(top2[:, i, g], sbias[:, i, g * 8:g * 8 + 8]) for i in two for g in range(G)])

            def route_groups(fb):
                pick(fb, nc.vector.tensor_tensor(gscore[:, :, 0:G], top2[:, :, :, 0], top2[:, :, :, 1], ALU.add))
                pick(fb, *[nc.vector.max(gtop[:, i], gscore[:, i]) for i in two])
                pick(fb, nc.vector.memset(gtop[:, :, KG:], -BIG))
                pick(fb, *[nc.vector.match_replace(grep[:, i], gtop[:, i], gscore[:, i], -2.0 * BIG) for i in two])

            def route_candidates(fb):
                pick(fb, nc.vector.tensor_tensor(gmask[:], grep[:, :, 0:G], gscore[:, :, 0:G], ALU.not_equal))
                pick(fb, nc.vector.tensor_scalar(gneg[:], gmask[:], -1.0, BIG, ALU.add, ALU.mult),
                     nc.vector.tensor_tensor(each(cand), each(sbias), gmask[:].unsqueeze(3).to_broadcast(full), ALU.mult))
                pick(fb, nc.vector.tensor_tensor(each(cand), each(cand), gneg[:].unsqueeze(3).to_broadcast(full), ALU.add))

            def route_experts(fb):
                pick(fb, *[nc.vector.max(etop[:, i], cand[:, i]) for i in two])
                pick(fb, nc.vector.memset(etop[:, :, K:], -BIG))
                pick(fb, *[nc.vector.match_replace(erep[:, i], etop[:, i], cand[:, i], -2.0 * BIG) for i in two])
                pick(fb, nc.vector.tensor_tensor(erep[:], erep[:], cand[:], ALU.not_equal))
                pick(fb, nc.vector.tensor_tensor(each(sel), each(erep), gmask[:].unsqueeze(3).to_broadcast(full), ALU.mult))
                dve.sem_inc(sel_done, 1)

            def route_weights(fb):
                pick(fb, nc.vector.tensor_tensor(weight[:], sg[:, :, 0:E], sel[:], ALU.mult))
                pick(fb, nc.vector.tensor_reduce(wsum[:], weight[:], AX.X, ALU.add))
                pick(fb, nc.vector.reciprocal(wsum[:], wsum[:]))
                pick(fb, nc.vector.scalar_tensor_tensor(weight[:], weight[:], ROUTE_SCALE,
                                                        wsum[:].unsqueeze(2).to_broadcast((P, NT, E)), ALU.mult, ALU.mult))

            def route_slots(fb):
                dve.wait_ge(pos_copied, fb + 1)
                pick(fb, nc.vector.scalar_tensor_tensor(valid[:], pos[:], float(CAP), sel[:], ALU.is_lt, ALU.mult),
                     nc.vector.tensor_tensor(key[:], pos[:], k["slot_base"][:].unsqueeze(1).to_broadcast((P, NT, E)), ALU.add),
                     nc.vector.tensor_tensor(taken[:], taken[:], sel[:, 0], ALU.add))
                pick(fb, nc.vector.tensor_tensor(key[:], key[:], valid[:], ALU.mult),
                     nc.vector.tensor_tensor(weight[:], weight[:], valid[:], ALU.mult),
                     nc.vector.tensor_tensor(taken[:], taken[:], sel[:, 1], ALU.add))
                pick(fb, *[nc.vector.max(ktop[:, i], key[:, i]) for i in two])

            def route_index(fb):
                if not isinstance(fb, int) or fb > 0:
                    dve.wait_ge(scattered, 16 * NT * K * fb)
                pick(fb, nc.vector.tensor_scalar(kmiss[:], ktop[:], 0.0, 1.0e6, ALU.is_equal, ALU.mult))
                pick(fb, nc.vector.scalar_tensor_tensor(kmiss[:], ktop[:], -1.0, kmiss[:], ALU.add, ALU.add))
                pick(fb, nc.vector.tensor_copy(scatter_index[:], kmiss[:]),
                     nc.vector.tensor_copy(k["slot_index"][:, bass.ds(fb * NT, NT)], kmiss[:]))
                dve.sem_inc(index_done, 1)

            def route_match(fb, i):
                wide = (P, K, E)
                pick(fb, nc.vector.tensor_tensor(match[:, i], key[:, i:i + 1].to_broadcast(wide),
                                                 ktop[:, i, 0:K].unsqueeze(2).to_broadcast(wide), ALU.is_equal))
                pick(fb, nc.vector.tensor_tensor(match[:, i], match[:, i], weight[:, i:i + 1].to_broadcast(wide), ALU.mult))

            def route_pairs(fb):
                pick(fb, nc.vector.tensor_reduce(k["slot_weight"][:, bass.ds(fb * NT, NT)], match[:], AX.X, ALU.add))

            def shared_out(section, b, fb):
                bank = await_full(dve, section, "SD", b)
                if not isinstance(fb, int) or fb > 0:
                    dve.wait_ge(x_done, fb)
                nc.vector.tensor_tensor(shared[:], tb[bank][:, :].rearrange("p (i m) -> p i m", i=NT),
                                        mod_b[:, 2:3].to_broadcast((P, NT, M)), ALU.mult).then_inc(shared_gated, 1)
                dve.wait_ge(shared_gated, fb + 1)
                dve.sem_inc(drained[bank], 1)

            def ffn_part(section, b, l, at):
                fb = b - 1
                if (l, at) == (0, 0):
                    norm2_stats(fb)
                    norm2_guess(fb)
                    norm2_newton(fb)
                if (l, at) == (0, 1):
                    norm2_newton(fb)
                if (l, at) == (0, 2):
                    norm2_newton(fb)
                    norm2_shift(fb)
                if (l, at) == (2, 1):
                    sigmoid_scores(fb)
                    release_rs(section, b, fb)
                if (l, at) == (2, 2):
                    sigmoid_gate(fb)
                if (l, at) == (3, 0):
                    route_bests(fb)
                    route_groups(fb)
                if (l, at) == (4, 0):
                    route_candidates(fb)
                    route_experts(fb)
                if (l, at) == (4, 1):
                    route_weights(fb)
                if (l, at) == (5, 0):
                    route_slots(fb)
                    route_index(fb)
                if (l, at) == (5, 1):
                    shared_out(section, b, fb)
                if (l, at) == (6, 0):
                    for i in two:
                        route_match(fb, i)
                if (l, at) == (6, 1):
                    route_pairs(fb)

            def step(section, tag, b, n, l):
                par = n_par(l, n)
                ffn = l is not None and section != "first"
                if exists(n + 2):
                    add_bias(n + 2, group_of(l, n, 2), group_of(l, n, 2) % 4, 0)
                if exists(n):
                    row_maxima(n, par, 0, 0)
                    row_maxima(n, par, 0, 1)
                    negate_maxima(n, group_of(l, n, 0), par, 0)
                if exists(n - 2):
                    copy_out(section, f"AT{tag}", b, heads_t[:].rearrange("p k s -> p (k s)"))
                if exists(n + 2):
                    rope_sin(n + 2, 0)
                    add_bias(n + 2, group_of(l, n, 2), group_of(l, n, 2) % 4, 1)
                if exists(n):
                    row_maxima(n, par, 1, 0)
                if exists(n + 2):
                    rope_sin(n + 2, 1)
                if exists(n):
                    row_maxima(n, par, 1, 1)
                    negate_maxima(n, group_of(l, n, 0), par, 1)
                    sink_exponents(n, group_of(l, n, 0), par)
                if l == 7:
                    attention_out(b)
                if ffn:
                    ffn_part(section, b, l, 0)
                if exists(n - 1):
                    normalise(n - 1, 1 - par, 0)
                if l == NORM_AT and section != "last":
                    ht_low(section, "H", b, b + 1)
                if ffn:
                    ffn_part(section, b, l, 1)
                if exists(n - 1):
                    normalise(n - 1, 1 - par, 1)
                if ffn:
                    ffn_part(section, b, l, 2)

            def start():
                nc.vector.memset(v[:, :, :, D:D + 1], 1.0)
                nc.vector.memset(taken[:], 0.0)
                nc.vector.memset(gscore[:, :, G:], -BIG).then_inc(preset, 1)
                ht_low("start", "H", 0, 0)
                for n in range(2):
                    for i in range(NT):
                        add_bias(n, n, n, i)
                        rope_sin(n, i)

            def end():
                fb = B - 1
                norm2_stats(fb)
                norm2_guess(fb)
                for _ in range(3):
                    norm2_newton(fb)
                norm2_shift(fb)
                sigmoid_scores(fb)
                release_rs("end", 0, fb)
                sigmoid_gate(fb)
                route_bests(fb)
                route_groups(fb)
                route_candidates(fb)
                route_experts(fb)
                route_weights(fb)
                route_slots(fb)
                route_index(fb)
                for i in two:
                    route_match(fb, i)
                route_pairs(fb)
                shared_out("end", 0, fb)

            rounds(dve, step, start, end)

        @block.tensor
        def _(pe):
            def claim(section, name, b):
                bank, _, before = tickets.use(section, name, b)
                if before is not None:
                    pe.wait_ge(drained[bank], before)
                return bank

            def turn_norm(section, name, b, nb):
                pe.wait_ge(h_ready, 2 * nb + 2)
                bank = claim(section, name, b)
                for m in range(KM):
                    for i in range(NT):
                        last = nc.tensor.transpose(tb[bank][:, m * S + i * P:m * S + (i + 1) * P],
                                                   h_norm[:, i, m * P:(m + 1) * P], ident[:])
                last.then_inc(filled[bank], 1)

            def project(nb, n, g, i):
                pe.wait_ge(ht_ready, nb + 1)
                if not (isinstance(n, int) and n == 0 and i == 0):
                    pe.wait_ge(proj_read, 2 * n + i)
                    pe.wait_ge(v_read, 2 * n + i)
                rows = slice(i * P, (i + 1) * P)
                terms = [(a, w, m) for m in range(KM) for a, w in
                         ((ht_hi, k["w_hi"]), (ht_hi, k["w_lo"]), (ht_lo, k["w_hi"]))]
                for j, (a, w, m) in enumerate(terms):
                    last = nc.tensor.matmul(pj[:, 0:GW], a[:, m, rows], w[:, m, g],
                                            start=(j == 0), stop=(j == len(terms) - 1))
                last.then_inc(proj_done, 1)

            def turn_q(section, name, b, n, par, i):
                pe.wait_ge(qk_lo_done, 2 * n + i + 1)
                bank = claim(section, name, b)
                for h in range(R):
                    last = nc.tensor.matmul(tb[bank][:, h * P:(h + 1) * P],
                                            qk_split[:, par, i, 2 * h:2 * h + 2].rearrange("p e d -> p (e d)"),
                                            k["ident_r"][:], start=True, stop=True)
                last.then_inc(filled[bank], 1)

            def turn_k(section, name, b, n, par):
                pe.wait_ge(key_again_done, n + 1)
                bank = claim(section, name, b)
                for e in range(2):
                    for i in range(NT):
                        pair = qk_split[:, par, i, 2 * R + e:2 * R + e + 2].rearrange("p e d -> p (e d)")
                        last = nc.tensor.matmul(tb[bank][:, e * S + i * P:e * S + (i + 1) * P], pair,
                                                k["ident_r"][:], start=True, stop=True)
                last.then_inc(filled[bank], 1)

            def scores(n, par, i, pair):
                if not (isinstance(n, int) and n == 0 and i == 0):
                    pe.wait_ge(probs_done, R * (2 * n + i - 1) + 2 * pair + 2)
                rows = slice(i * P, (i + 1) * P)
                far = slice((1 - i) * P, (2 - i) * P)
                for e in range(2):
                    q, out = q_t[:, par, 2 * pair + e, rows], sc[pair][:, e]
                    nc.tensor.matmul(out, q, k_t[:, par, 0], start=True, stop=False)
                    nc.tensor.matmul(out[:, far], k["ident_b"][:], k["mask_b"][:, i], start=False, stop=False)
                    last = nc.tensor.matmul(out, q, k_t[:, par, 1], start=False, stop=True)
                last.then_inc(scores_done, 1)

            def turn_probs(section, name, b, n, par, h):
                if h == 0:
                    pe.wait_ge(probs_done, 2 * R * (n + 1))
                bank = claim(section, name, b)
                for j in range(NT):
                    for i in range(NT):
                        last = nc.tensor.transpose(tb[bank][:, j * S + i * P:j * S + (i + 1) * P],
                                                   probs[:, par, i, h, j * P:(j + 1) * P], ident[:])
                last.then_inc(filled[bank], 1)

            def values(section, names, b, n, quad, i):
                if i == 0:
                    for name in names[2:]:
                        await_drained(pe, section, name, b)
                if not (isinstance(n, int) and n == 0):
                    pe.wait_ge(heads_done, 2 * n + i - 1)
                for h in range(R):
                    for j in range(NT):
                        last = nc.tensor.matmul(po[i][:, h * (D + 1):(h + 1) * (D + 1)],
                                                probs_t[:, h, j, i * P:(i + 1) * P], v[:, quad, j],
                                                start=(j == 0), stop=(j == NT - 1))
                last.then_inc(pv_done, 1)

            def turn_heads(section, name, b, n, par):
                pe.wait_ge(heads_done, 2 * n + 2)
                bank = claim(section, name, b)
                for m in range(QW // P):
                    for i in range(NT):
                        last = nc.tensor.transpose(tb[bank][:, m * S + i * P:m * S + (i + 1) * P],
                                                   heads[:, par, i, m * P:(m + 1) * P], ident[:])
                last.then_inc(filled[bank], 1)

            def project_out(section, name, b, n, g, nb):
                await_drained(pe, section, name, b)
                if g == 0 and not (isinstance(nb, int) and nb == 0):
                    pe.wait_ge(attn_read, nb)
                for i in range(NT):
                    for m in range(QW // P):
                        last = nc.tensor.matmul(op[:, i], heads_t[:, m, i * P:(i + 1) * P],
                                                k["wo"][:, g * (QW // P) + m],
                                                start=(g == 0 and i == 0 and m == 0),
                                                stop=(g == HKV - 1 and m == QW // P - 1), skip_group_check=True)
                last.then_inc(op_done, 1)

            def turn_norm2(section, b, fb):
                pe.wait_ge(h2_done, fb + 1)
                bank = claim(section, "H2T", b)
                for m in range(KM):
                    for i in range(NT):
                        last = nc.tensor.transpose(tb[bank][:, m * S + i * P:m * S + (i + 1) * P],
                                                   h2[:, i, m * P:(m + 1) * P], ident[:])
                last.then_inc(filled[bank], 1)

            def router(section, b):
                await_drained(pe, section, "H2T", b)
                bank = claim(section, "RS", b)
                for i in range(NT):
                    for m in range(KM):
                        last = nc.tensor.matmul(tb[bank][:, i * NX:(i + 1) * NX], h2_t[:, m, i * P:(i + 1) * P],
                                                k["w_router"][:, m], start=(m == 0), stop=(m == KM - 1))
                last.then_inc(filled[bank], 1)

            def turn_shared(section, b, fb):
                pe.wait_ge(hs_step, 2 * fb + 2)
                bank = claim(section, "HST", b)
                for i in range(NT):
                    last = nc.tensor.transpose(tb[bank][0:F, i * P:(i + 1) * P], hs[:, i], ident[:])
                last.then_inc(filled[bank], 1)

            def positions(section, b, fb):
                pe.wait_ge(sel_done, fb + 1)
                bank = claim(section, "POS", b)
                for i in range(NT):
                    out = tb[bank][:, i * E:(i + 1) * E]
                    nc.tensor.matmul(out, k["tri_b"][:], sel[:, i], start=True, stop=False)
                    last = nc.tensor.matmul(out, k["ones_b"][:], taken[:], start=False, stop=(i == 0))
                    if i == 1:
                        last = nc.tensor.matmul(out, k["ones_b"][:], sel[:, 0], start=False, stop=True)
                last.then_inc(filled[bank], 1)

            def shared_down(section, b):
                await_drained(pe, section, "HST", b)
                bank = claim(section, "SD", b)
                for i in range(NT):
                    last = nc.tensor.matmul(tb[bank][:, i * M:(i + 1) * M], hs_t[:, i * P:(i + 1) * P],
                                            k["w_sdown"][:], start=True, stop=True)
                last.then_inc(filled[bank], 1)

            def step(section, tag, b, n, l):
                par = n_par(l, n)
                ffn = l is not None and section != "first"
                turned = [f"P{h}{tag}" for h in range(R)]

                def probs_unit(h):
                    if exists(n - 1):
                        turn_probs(section, turned[h], b, n - 1, 1 - par, h)

                if exists(n + 2):
                    project(batch_of(l, n, b, 2), n + 2, group_of(l, n, 2), 0)
                if exists(n):
                    scores(n, par, 0, 0)
                if exists(n - 2):
                    turn_heads(section, f"AT{tag}", b, n - 2, par)
                if exists(n):
                    scores(n, par, 0, 1)
                probs_unit(0)
                if exists(n + 2):
                    project(batch_of(l, n, b, 2), n + 2, group_of(l, n, 2), 1)
                probs_unit(1)
                if exists(n):
                    scores(n, par, 1, 0)
                probs_unit(2)
                if exists(n):
                    scores(n, par, 1, 1)
                probs_unit(3)
                if exists(n - 2):
                    project_out(section, f"AT{tag}", b, n - 2, group_of(l, n, -2), batch_of(l, n, b, -2))
                if exists(n + 1):
                    turn_q(section, f"Q0{tag}", b, n + 1, 1 - par, 0)
                if exists(n - 1):
                    values(section, turned, b, n - 1, group_of(l, n, -1) % 4, 0)
                if exists(n + 1):
                    turn_q(section, f"Q1{tag}", b, n + 1, 1 - par, 1)
                if ffn and l == 2:
                    router(section, b)
                if l == NORM_AT and section != "last":
                    turn_norm(section, "H", b, b + 1)
                if ffn and l == 4:
                    positions(section, b, b - 1)
                if ffn and l == 5:
                    shared_down(section, b)
                if exists(n + 1):
                    turn_k(section, f"KT{tag}", b, n + 1, 1 - par)
                if exists(n - 1):
                    values(section, turned, b, n - 1, group_of(l, n, -1) % 4, 1)
                if ffn and l == 1:
                    turn_norm2(section, b, b - 1)
                if ffn and l == 3:
                    turn_shared(section, b, b - 1)
                if exists(n + 1):
                    for unit in ("Q1", "KT"):
                        await_drained(pe, section, f"{unit}{tag}", b)

            def start():
                pe.wait_ge(preset, 1)
                turn_norm("start", "H", 0, 0)
                for n in range(2):
                    for i in range(NT):
                        project(0, n, n, i)
                for i in range(NT):
                    turn_q("start", f"Q{i}", 0, 0, 0, i)
                turn_k("start", "KT", 0, 0, 0)
                for name in ("Q1", "KT"):
                    await_drained(pe, "start", name, 0)

            def end():
                turn_norm2("end", 0, B - 1)
                router("end", 0)
                turn_shared("end", 0, B - 1)
                positions("end", 0, B - 1)
                shared_down("end", 0)

            rounds(pe, step, start, end)


NORM_STEPS = 2 * NT + 3 + 3 * 3 + 1
ROUTE_STEPS = (1 + NT * G) + (1 + NT + 1 + NT) + (1 + 2 + 1) + (NT + 1 + NT + 1 + 1) + 4 \
    + (3 + 3 + NT) + (1 + 1 + 2) + 2 * NT + 1


CHUNK = 4
CS = CHUNK * CAP
RING = 4
NCHUNK = E // CHUNK
HALF = CS // 2


def experts(nc, t, x, ident, slot_index, slot_weight, xbuf, ybuf, mod_dram):
    with ExitStack() as c:
        def sb(name, shape, dt=F32):
            return c.enter_context(nc.sbuf_tensor(name, shape, dt))

        def sem(name):
            return c.enter_context(nc.semaphore(name))

        wg = sb("wg", [P, RING, CHUNK, KM * F])
        wu = sb("wu", [P, RING, CHUNK, KM * F])
        wd = sb("wd", [F, RING, CHUNK, M])
        rows = sb("rows", [HALF, RING, 2, M])
        rows_t = sb("rows_t", [P, 2, KM, CS])
        ex = sb("ex", [F, 2, CS])
        hid = sb("hid", [F, 2, CS])
        out_rows = sb("out_rows", [CAP, 2, CHUNK, M])
        gathered = sb("gathered", [P, 2, K, M])
        index = sb("index", [P, 2, 8], U32)
        wts = sb("wts", [P, 2, K])
        total = sb("total", [P, 2, M])
        gate = sb("gate", [P, B, M])
        result = sb("result", [P, 2, M])
        pt = [c.enter_context(nc.psum_tensor(f"pt{i}", [P, 512], F32)) for i in range(2)]
        pg = [c.enter_context(nc.psum_tensor(f"pg{i}", [P, 512], F32)) for i in range(2)]
        pd = [c.enter_context(nc.psum_tensor(f"pd{i}", [P, 512], F32)) for i in range(4)]

        loaded = [sem(f"loaded{i}") for i in range(RING)]
        turned, turned_out, hidden_done, exp_done, act_step, hid_done, down_done = (
            sem(n) for n in ("turned", "turned_out", "hidden_done", "exp_done", "act_step", "hid_done", "down_done"))
        out_act, out_dve, stored = sem("out_act"), sem("out_dve"), [sem(f"stored{i}") for i in range(2)]
        gate_in, cleared, picked, gathered_in, summed, result_done, written = (
            sem(n) for n in ("gate_in", "cleared", "picked", "gathered_in", "summed", "result_done", "written"))
        gathered_in = [sem(f"gathered_in{i}") for i in range(2)]
        written = [sem(f"written{i}") for i in range(2)]
        sum_step = sem("sum_step")
        block = c.enter_context(nc.Block())
        y_rows = ybuf.rearrange("(e s) m -> s e m", s=CAP)
        w_gate = t["w_gate"].rearrange("e (p k) f -> p e (k f)", k=KM)
        w_up = t["w_up"].rearrange("e (p k) f -> p e (k f)", k=KM)
        w_down = t["w_down"].rearrange("e f m -> f e m")
        x_rows = xbuf.rearrange("(a h s) m -> s a h m", h=2, s=HALF)
        LOADS = 4

        def chunks(eng, step):
            for r in range(RING):
                step(r, r, True)
            with eng.Fori(1, NCHUNK // RING) as i:
                for r in range(RING):
                    step(i * RING + r, r, False)

        @block.sync
        def _(sp):
            sp.dma_start(gate[:], mod_dram[:, 5].unsqueeze(0).to_broadcast((P, B, M))).then_inc(gate_in, 16)

            def load(a, r, first):
                if not first:
                    sp.wait_ge(down_done, 2 * (a - RING) + 2)
                e = bass.ds(a * CHUNK, CHUNK)
                sp.dma_start(rows[:, r], x_rows[:, bass.ds(a, 1)]).then_inc(loaded[r], 16)
                sp.dma_start(wg[:, r], w_gate[:, e]).then_inc(loaded[r], 16)
                sp.dma_start(wu[:, r], w_up[:, e]).then_inc(loaded[r], 16)
                sp.dma_start(wd[:, r], w_down[:, e]).then_inc(loaded[r], 16)

            chunks(sp, load)
            out = t["out"].rearrange("(t p) m -> p t m", p=P)
            with sp.Fori(0, B) as b:
                for i in range(NT):
                    sp.wait_ge(result_done, b * NT + i + 1)
                    sp.dma_start(out[:, bass.ds(b * NT + i, 1)], result[:, i]).then_inc(written[i], 16)
            for i in range(NT):
                sp.wait_ge(written[i], 16 * B)

        @block.tensor
        def _(pe):
            def step(a, r, first):
                par = r % 2
                pe.wait_ge(loaded[r], 16 * LOADS * (a // RING + 1) if first else 16 * LOADS * ((a - r) // RING + 1))
                if not (first and r < 2):
                    pe.wait_ge(turned_out, a - 1)
                for m in range(KM):
                    for h in range(2):
                        src = rows[:, r, h].rearrange("s (p k) -> s k p", k=KM)[:, m]
                        last = nc.tensor.transpose(pt[par][:, m * CS + h * HALF:m * CS + (h + 1) * HALF],
                                                   src, ident[0:HALF, 0:HALF])
                last.then_inc(turned, 1)
                pe.wait_ge(turned_out, a + 1)
                if not (first and r < 2):
                    pe.wait_ge(hid_done, a - 1)
                for u, w in enumerate((wg, wu)):
                    for e in range(CHUNK):
                        for m in range(KM):
                            last = nc.tensor.matmul(
                                pg[par][0:F, u * CS + e * CAP:u * CS + (e + 1) * CAP],
                                w[:, r, e, m * F:(m + 1) * F], rows_t[:, par, m, e * CAP:(e + 1) * CAP],
                                start=(m == 0), stop=(m == KM - 1))
                last.then_inc(hidden_done, 1)
                pe.wait_ge(hid_done, a + 1)
                if not (first and r < 2):
                    pe.wait_ge(out_act, a - 1)
                    pe.wait_ge(out_dve, a - 1)
                for e in range(CHUNK):
                    last = nc.tensor.matmul(pd[2 * par + e // 2][0:CAP, (e % 2) * M:(e % 2 + 1) * M],
                                            hid[:, par, e * CAP:(e + 1) * CAP], wd[:, r, e], start=True, stop=True)
                    if e % 2:
                        last.then_inc(down_done, 1)

            chunks(pe, step)

        @block.scalar
        def _(act):
            def step(a, r, first):
                par = r % 2
                act.wait_ge(turned, a + 1)
                nc.scalar.activation(rows_t[:, par].rearrange("p k s -> p (k s)"), pt[par][:, 0:KM * CS],
                                     ACT.Copy).then_inc(turned_out, 1)
                act.wait_ge(hidden_done, a + 1)
                nc.scalar.activation(ex[:, par], pg[par][0:F, 0:CS], ACT.Exp, scale=-1.0).then_inc(exp_done, 1)
                act.wait_ge(down_done, 2 * a + 1)
                if not (first and r < 2):
                    act.wait_ge(stored[par], 16 * ((a - r) // 2 + r // 2) if not first else 16 * (r // 2))
                nc.scalar.activation(out_rows[:, par, 0:2].rearrange("s e m -> s (e m)"), pd[2 * par][0:CAP, :],
                                     ACT.Copy).then_inc(out_act, 1)
                act.wait_ge(out_act, a + 1)
                act.wait_ge(out_dve, a + 1)
                act.dma_start(y_rows[:, bass.ds(a * CHUNK, CHUNK)], out_rows[:, par]).then_inc(stored[par], 16)

            chunks(act, step)

        @block.vector
        def _(dve):
            nc.vector.memset(gathered[:], 0.0).then_inc(cleared, 1)

            def step(a, r, first):
                par = r % 2
                dve.wait_ge(exp_done, a + 1)
                nc.vector.tensor_scalar_add(ex[:, par], ex[:, par], 1.0).then_inc(act_step, 1)
                dve.wait_ge(act_step, 3 * a + 1)
                nc.vector.reciprocal(ex[:, par], ex[:, par]).then_inc(act_step, 1)
                dve.wait_ge(act_step, 3 * a + 2)
                nc.vector.tensor_tensor(ex[:, par], ex[:, par], pg[par][0:F, 0:CS], ALU.mult).then_inc(act_step, 1)
                dve.wait_ge(act_step, 3 * a + 3)
                nc.vector.tensor_tensor(hid[:, par], ex[:, par], pg[par][0:F, CS:2 * CS], ALU.mult)\
                    .then_inc(hid_done, 1)
                dve.wait_ge(down_done, 2 * a + 2)
                if not (first and r < 2):
                    dve.wait_ge(stored[par], 16 * ((a - r) // 2 + r // 2) if not first else 16 * (r // 2))
                nc.vector.tensor_copy(out_rows[:, par, 2:4].rearrange("s e m -> s (e m)"),
                                      pd[2 * par + 1][0:CAP, :]).then_inc(out_dve, 1)

            chunks(dve, step)

            dve.wait_ge(gate_in, 16)

            def pick(b):
                for i in range(NT):
                    nc.vector.tensor_copy(index[:, i], slot_index[:, bass.ds(b * NT + i, 1)]).then_inc(picked, 1)

            def tile(b, i, first):
                n = b * NT + i
                nc.vector.tensor_copy(wts[:, i], slot_weight[:, bass.ds(n, 1)]).then_inc(sum_step, 1)
                dve.wait_ge(gathered_in[i], 16 * K * (b + 1))
                if not first:
                    dve.wait_ge(written[i], 16 * b)
                step0 = (K + 2) * n + 1
                dve.wait_ge(sum_step, step0)
                nc.vector.tensor_scalar(total[:, i], gathered[:, i, 0], wts[:, i, 0:1], None, ALU.mult).then_inc(sum_step, 1)
                for j in range(1, K):
                    dve.wait_ge(sum_step, step0 + j)
                    nc.vector.scalar_tensor_tensor(total[:, i], gathered[:, i, j], wts[:, i, j:j + 1], total[:, i],
                                                   ALU.mult, ALU.add).then_inc(sum_step, 1)
                dve.wait_ge(sum_step, step0 + K)
                nc.vector.tensor_tensor(total[:, i], total[:, i], gate[:, bass.ds(b, 1)].rearrange("p o m -> p (o m)"), ALU.mult)\
                    .then_inc(sum_step, 1)
                dve.wait_ge(sum_step, step0 + K + 1)
                nc.vector.tensor_tensor(result[:, i], total[:, i], x[:, bass.ds(n, 1)].rearrange("p o m -> p (o m)"), ALU.add)\
                    .then_inc(result_done, 1)

            pick(0)
            for i in range(NT):
                tile(0, i, True)
            with dve.Fori(1, B) as b:
                pick(b)
                for i in range(NT):
                    tile(b, i, False)

        @block.gpsimd
        def _(pool):
            pool.wait_ge(cleared, 1)
            for par in range(2):
                pool.wait_ge(stored[par], 16 * NCHUNK // 2)

            def tile(b, i, first):
                wait_alone(pool, picked, b * NT + NT, cleared)
                if not first:
                    wait_alone(pool, result_done, (b - 1) * NT + i + 1, cleared)
                for j in range(K):
                    nc.gpsimd.indirect_dma_start(
                        gathered[:, i, j], None, ybuf,
                        bass.IndirectOffsetOnAxis(ap=index[:, i, j:j + 1], axis=0),
                        bounds_check=SLOTS - 1, oob_is_err=False).then_inc(gathered_in[i], 16)

            for i in range(NT):
                tile(0, i, True)
            with pool.Fori(1, B) as b:
                for i in range(NT):
                    tile(b, i, False)


def constants():
    half = D // 2
    inv = (1.0 / np.float32(150000.0) ** (np.arange(half, dtype=np.float32) * 2.0 / D)).astype(np.float32)
    angle = np.arange(S, dtype=np.float32)[:, None] * inv[None, :]
    scale = np.float32(D ** -0.25)
    cos, sin = np.cos(angle) * scale, np.sin(angle) * scale
    tiles = lambda a: np.ascontiguousarray(a.reshape(NT, P, D).transpose(1, 0, 2)).astype(np.float32)
    i, j = np.arange(P)[:, None], np.arange(P)[None, :]
    mask = np.stack([np.where(P + j - i > WINDOW, NEG, 0.0), np.where(P + i - j > WINDOW, NEG, 0.0)], 1)
    return {
        "cos": tiles(np.concatenate([cos, cos], 1)), "sin": tiles(np.concatenate([-sin, sin], 1)),
        "ident": np.eye(P, dtype=np.float32), "tri": (i < j).astype(np.float32), "mask": mask.astype(np.float32),
        "slot_base": (np.arange(E) * CAP + 1).astype(np.float32)[None, :],
    }


def kernel(**inputs):
    import concourse.bacc as bacc
    from concourse.bass_utils import run_bass_kernel_spmd

    a = {n: np.asarray(v) for n, v in inputs.items()}
    turn = lambda w: np.concatenate([w[..., 0::2], w[..., 1::2]], -1)
    wq = turn(a["L0_attn_Wq"]).reshape(M, HKV, QW)
    wk, wv = turn(a["L0_attn_Wk"]), a["L0_attn_Wv"]
    bq = turn(a["L0_attn_bq"]).reshape(HKV, QW)
    bk, bv = turn(a["L0_attn_bk"]), a["L0_attn_bv"]
    arrays = {
        "x": a["L0_attn_hidden_states"].reshape(B * S, M),
        "wqkv": np.concatenate([wq, wk, wv], -1).transpose(1, 0, 2),
        "bias": np.concatenate([bq, bk, bv], -1).reshape(1, HKV * GW),
        "wo": a["L0_attn_Wo"].reshape(H * D, M), "bo": a["L0_attn_bo"].reshape(1, M),
        "sinks": a["L0_attn_sinks"].reshape(1, H),
        "w_router": np.concatenate([a["L0_ffn_gate_w"], a["L0_ffn_ws_gate"], a["L0_ffn_ws_up"]], -1),
        "ws_down": a["L0_ffn_ws_down"], "r_bias": a["L0_ffn_bias"].reshape(1, E),
        "w_gate": a["L0_ffn_w_gate"], "w_up": a["L0_ffn_w_up"], "w_down": a["L0_ffn_w_down"],
        "c": a["L0_c"], "wmod": a["L0_wmod"],
        **constants(),
    }
    nc = bacc.Bacc("TRN2", target_bir_lowering=False, num_devices=1)
    feed, t = {}, {}
    for name, value in arrays.items():
        value = np.ascontiguousarray(value)
        feed[f"in_{name}"] = value
        t[name] = nc.dram_tensor(f"in_{name}", value.shape, mybir.dt.from_np(value.dtype), kind="ExternalInput").ap()
    t["out"] = nc.dram_tensor("out", [B * S, M], F32, kind="ExternalOutput").ap()
    build(nc, t)
    got = run_bass_kernel_spmd(nc, [feed], core_ids=[0])
    return got.results[0]["out"].reshape(B, S, M)
```

```python
from contextlib import ExitStack

import numpy as np

import concourse.bass as bass
from concourse import mybir

F32, F32R, BF16, U32, I32 = (mybir.dt.float32, mybir.dt.float32r, mybir.dt.bfloat16,
                             mybir.dt.uint32, mybir.dt.int32)
ALU = mybir.AluOpType
ACT = mybir.ActivationFunctionType
AX = mybir.AxisListType

P = 128
B, S, M = 8, 256, 256
H, HKV, D = 32, 8, 64
R = H // HKV
NT = S // P
KM = M // P
QW = R * D
RW = QW + D
GW = RW + D
WINDOW = 128
NEG = -1.0e9
EPS = 1e-5
E, K, F = 64, 6, 96
G, KG = 8, 4
CAP = 2 * (2 * 128 * K // E)
SLOTS = E * CAP
ROUTE_SCALE = 2.5
BIG = 1.0e30
NX = E + 2 * F
SEED = 0x5F3759DF
assert HKV == 8 and NT == 2 and KM == 2 and R == 4


class Tickets:

    def __init__(self):
        self.seq = 0
        self.count = [0, 0]
        self.table = {}
        self.section("start", ["H", "Q0", "Q1", "KT"])
        self.section("steps 0, 1", [u for n in range(AHEAD) for u in step_units(n, n, None)])
        self.section("first", round_units(0))
        self.section("second", round_units(1))
        at = self.seq
        self.section("mid", round_units("mid"))
        n = self.seq - at
        assert n % 2 == 0
        self.per = n // 2
        self.seq += (MID_ROUNDS - 1) * n
        self.count = [c + (MID_ROUNDS - 1) * self.per for c in self.count]
        self.section("last", round_units(B - 1))
        self.section("end", ["H2T", "RS", "POS", "COUNT", "HST", "SD"])

    def section(self, section, names):
        for name in names:
            bank = self.seq % 2
            self.seq += 1
            self.count[bank] += 1
            self.table[section, name] = bank, self.count[bank]

    def use(self, section, name, b):
        bank, v = self.table[section, name]
        if section == "mid":
            return bank, v + (b - 2) * self.per, v + (b - 2) * self.per - 1
        return bank, v, v - 1 if v > 1 else None


AHEAD = 2
MID_ROUNDS = B - 3
NG_ALL = B * HKV
NORM_AT = 3
MID_AT = {2: "RS", 4: "HST", 5: "SD"}
END_AT = {1: "H2T", 4: "POS"}


def exists(n):
    return not isinstance(n, int) or 0 <= n < NG_ALL


def step_units(n, tag, b):
    ffn = b is not None and b != 0
    names = []
    if exists(n - 2):
        names.append(f"AT{tag}")
    if exists(n - 1):
        names += [f"P{h}{tag}" for h in range(R)]
    if exists(n + 1):
        names += [f"Q0{tag}", f"Q1{tag}"]
    if ffn and tag in MID_AT:
        names.append(MID_AT[tag])
    if b is not None and b != B - 1 and tag == NORM_AT:
        names.append("H")
    if exists(n + 1):
        names.append(f"KT{tag}")
    if ffn and tag in END_AT:
        names.append(END_AT[tag])
    return names


def round_units(b):
    names = []
    for l in range(HKV):
        names += step_units(NG_ALL // 2 if b == "mid" else b * HKV + AHEAD + l, l, b)
    return names


def build(nc, t):
    xbuf = nc.dram_tensor("expert_rows_in", [SLOTS, M], F32, kind="Internal").ap()
    ybuf = nc.dram_tensor("expert_rows_out", [SLOTS, M], F32, kind="Internal").ap()
    mod_dram = nc.dram_tensor("modulation", [B, 6, M], F32, kind="Internal").ap()

    with ExitStack() as ctx:
        def sb(name, shape, dt=F32, c=ctx):
            return c.enter_context(nc.sbuf_tensor(name, shape, dt))

        x = sb("x", [P, B * NT, M])
        ident = sb("ident", [P, P])
        slot_index = sb("slot_index", [P, B * NT, 8], U32)
        slot_weight = sb("slot_weight", [P, B * NT, K])
        base = nc.sbuf_base
        w_hi = sb("w_hi", [P, KM, HKV, GW], F32R)
        w_lo = sb("w_lo", [P, KM, HKV, GW], F32R)
        w = expert_weights(nc, ctx, base, nc.sbuf_base)
        with ExitStack() as c:
            def sa(name, shape, dt=F32):
                return sb(name, shape, dt, c)

            k = dict(
                x=x, ident=ident, slot_index=slot_index, slot_weight=slot_weight,
                w_hi=w_hi, w_lo=w_lo,
                wo=sa("wo", [P, H * D // P, M]),
                bias=sa("bias", [P, HKV, GW]), bo=sa("bo", [P, M]),
                cos=sa("cos", [P, NT, D]), sin=sa("sin", [P, NT, D]),
                ident_r=sa("ident_r", [P, P], F32R), ident_b=sa("ident_b", [P, P], BF16),
                ones_b=sa("ones_b", [P, P], BF16), tri_b=sa("tri_b", [P, P], BF16),
                mask_b=sa("mask_b", [P, NT, P], BF16),
                sink=sa("sink", [P, HKV, R]), neg_sink=sa("neg_sink", [P, HKV, R]),
                w_router=sa("w_router", [P, KM, NX]), w_sdown=sa("w_sdown", [F, M]),
                r_bias=sa("r_bias", [P, E]), slot_base=sa("slot_base", [P, E]),
                rstd=sa("rstd", [P, B * NT]),
                nmr=sa("nmr", [P, B * NT]),
            )
            late = {n: c.enter_context(nc.semaphore(n)) for n in ("wo_in", "zero_out", "ffn_in", "first_mod_in")}
            zero = sa("zero", [P, M])
            k["mod_a"] = sa("mod_a", [P, 2, M])
            setup(nc, t, k, late, zero, xbuf, mod_dram)
            attention(nc, t, k, w, late, xbuf, mod_dram)
        experts(nc, t, w, x, ident, slot_index, slot_weight, xbuf, ybuf, mod_dram)


def split(dve_or_pool, hi, lo, full):
    return dve_or_pool.tensor_tensor(lo, full, hi.bitcast(F32), ALU.subtract)


def wait_alone(eng, semaphore, value, met):
    if not isinstance(value, int):
        value = eng.to_reg(value)
    eng.wait_ge(met, 1)
    eng.wait_ge(semaphore, value)


def setup(nc, t, k, late, zero, xbuf, mod_dram):
    with ExitStack() as c:
        def sb(name, shape, dt=F32):
            return c.enter_context(nc.sbuf_tensor(name, shape, dt))

        def sem(name):
            return c.enter_context(nc.semaphore(name))

        w_raw = sb("w_raw", [P, HKV, KM, GW])
        cond = sb("cond", [B, M])
        cond_e = sb("cond_e", [B, M])
        cond_s = sb("cond_s", [B, M])
        cond_t = sb("cond_t", [P, KM, B])
        w_mod = sb("w_mod", [P, KM, 6 * M])
        mod = sb("mod", [B, 6, M])
        sign = sb("sign", [B, 2, M])
        size = sb("size", [B, 2, M])
        stats = sb("stats", [P, B * NT, 6])
        mv = sb("mv", [P, B * NT, 2])
        eps = sb("eps", [P, 1])
        tri = sb("tri", [P, P])
        mask = sb("mask", [P, NT, P])
        std = sb("std", [P, B * NT])
        nwt = sb("nwt", [P, B * NT])
        ps_t = c.enter_context(nc.psum_tensor("ps_cond", [P, KM, B], F32))
        ps_m = c.enter_context(nc.psum_tensor("ps_mod", [B, 3, 512], F32))

        small_in, x_in, mod_in = (sem(n) for n in ("small_in", "x_in", "mod_in"))
        w_in = [sem(f"w_in{g}") for g in range(HKV)]
        const_in, zeroed = sem("const_in"), sem("zeroed")
        cond_exp, cond_step, cond_turned, cond_copied = (sem(n) for n in ("cond_exp", "cond_step", "cond_turned", "cond_copied"))
        mod_done, mod_step, mod_out, hi_done, lo_done = (sem(n) for n in ("mod_done", "mod_step", "mod_out", "hi_done", "lo_done"))
        stat_step, std_done, eps_set, neg_done, idr_done = (sem(n) for n in ("stat_step", "std_done", "eps_set", "neg_done", "idr_done"))
        block = c.enter_context(nc.Block())
        N_CONST = 6
        POOL_LO = 5

        @block.sync
        def _(sp):
            sp.dma_start(cond[:], t["c"]).then_inc(small_in, 16)
            sp.dma_start(k["ident"][:], t["ident"]).then_inc(small_in, 16)
            sp.dma_start(w_mod[:], t["wmod"].rearrange("(k p) n -> p k n", p=P)).then_inc(mod_in, 16)
            sp.dma_start(k["x"][:], t["x"].rearrange("(t p) m -> p t m", p=P)).then_inc(x_in, 16)
            for name, dst, src in (
                ("bias", k["bias"][:].rearrange("p g w -> p (g w)"), t["bias"].to_broadcast((P, HKV * GW))),
                ("cos", k["cos"][:], t["cos"]), ("sin", k["sin"][:], t["sin"]),
                ("tri", tri[:], t["tri"]), ("mask", mask[:], t["mask"]),
                ("sink", k["sink"][:].rearrange("p g r -> p (g r)"), t["sinks"].to_broadcast((P, H))),
            ):
                sp.dma_start(dst, src).then_inc(const_in, 16)
            sp.wait_ge(mod_step, 8)
            sp.dma_start(mod_dram, mod[:]).then_inc(mod_out, 16)
            sp.wait_ge(mod_out, 16)
            sp.dma_start(k["mod_a"][:], mod_dram[0:1, 0:2].to_broadcast((P, 2, M))).then_inc(late["first_mod_in"], 16)
            sp.dma_start(k["wo"][:], t["wo"].rearrange("(d p) m -> p d m", p=P)).then_inc(late["wo_in"], 16)
            for dst, src in (
                (k["bo"][:], t["bo"].to_broadcast((P, M))),
                (k["w_router"][:], t["w_router"].rearrange("(k p) n -> p k n", p=P)),
                (k["w_sdown"][:], t["ws_down"]),
                (k["r_bias"][:], t["r_bias"].to_broadcast((P, E))),
                (k["slot_base"][:], t["slot_base"].to_broadcast((P, E))),
            ):
                sp.dma_start(dst, src).then_inc(late["ffn_in"], 16)
            sp.wait_ge(zeroed, 1)
            sp.dma_start(xbuf.rearrange("(p n) m -> p n m", p=P),
                         zero[:].unsqueeze(1).to_broadcast((P, SLOTS // P, M))).then_inc(late["zero_out"], 16)
            sp.wait_ge(const_in, 16 * N_CONST)

        @block.gpsimd
        def _(pool):
            pool.memset(zero[:], 0.0).then_inc(zeroed, 1)
            for g in range(POOL_LO):
                pool.wait_ge(hi_done, g + 1)
                split(nc.gpsimd, k["w_hi"][:, :, g], k["w_lo"][:, :, g], w_raw[:, g]).then_inc(lo_done, 1)

        @block.scalar
        def _(act):
            act.wait_ge(small_in, 32)
            nc.scalar.activation(cond_e[:], cond[:], ACT.Exp, scale=-1.0).then_inc(cond_exp, 1)
            for g in range(HKV):
                act.dma_start(w_raw[:, g], t["wqkv"][g].rearrange("(k p) w -> p k w", p=P)).then_inc(w_in[g], 16)
            for g in range(HKV):
                act.wait_ge(w_in[g], 16)
                nc.scalar.activation(k["w_hi"][:, :, g], w_raw[:, g], ACT.Copy).then_inc(hi_done, 1)
                if g == 1:
                    act.wait_ge(stat_step, 2 * B * NT)
                    act.wait_ge(eps_set, 1)
                    nc.scalar.activation(std[:], mv[:, :, 1], ACT.Sqrt, bias=eps[:]).then_inc(std_done, 1)

        @block.vector
        def _(dve):
            link_count = [0]

            def link(ins):
                link_count[0] += 1
                ins.then_inc(cond_step, 1)
                dve.wait_ge(cond_step, link_count[0])

            nc.vector.memset(eps[:], EPS).then_inc(eps_set, 1)
            dve.wait_ge(cond_exp, 1)
            link(nc.vector.tensor_scalar_add(cond_e[:], cond_e[:], 1.0))
            link(nc.vector.reciprocal(cond_e[:], cond_e[:]))
            link(nc.vector.tensor_tensor(cond_s[:], cond_e[:], cond[:], ALU.mult))
            dve.wait_ge(cond_turned, 1)
            nc.vector.tensor_copy(cond_t[:], ps_t[:]).then_inc(cond_copied, 1)
            dve.wait_ge(x_in, 16)
            for i in range(B * NT):
                nc.vector.bn_stats(stats[:, i], k["x"][:, i]).then_inc(stat_step, 1)
            for i in range(B * NT):
                dve.wait_ge(stat_step, i + 1)
                nc.vector.bn_aggr(mv[:, i], stats[:, i]).then_inc(stat_step, 1)
            dve.wait_ge(mod_done, 1)
            nc.vector.tensor_copy(mod[:].rearrange("b a m -> b (a m)"),
                                  ps_m[:].rearrange("b a m -> b (a m)")).then_inc(mod_step, 1)
            dve.wait_ge(mod_step, 1)
            scales = mod[:].rearrange("b (l a) m -> b l a m", l=2)[:, :, 1]
            gates = mod[:].rearrange("b (l a) m -> b l a m", l=2)[:, :, 2]
            nc.vector.tensor_scalar_add(scales, scales, 1.0).then_inc(mod_step, 1)
            nc.vector.tensor_scalar(sign[:], gates, 0.0, 2.0, ALU.is_ge, ALU.mult).then_inc(mod_step, 1)
            nc.vector.scalar_tensor_tensor(size[:], gates, -1.0, gates, ALU.mult, ALU.max).then_inc(mod_step, 1)
            dve.wait_ge(mod_step, 4)
            nc.vector.tensor_scalar_add(sign[:], sign[:], -1.0).then_inc(mod_step, 1)
            nc.vector.tensor_scalar_max(size[:], size[:], 0.25).then_inc(mod_step, 1)
            dve.wait_ge(mod_step, 6)
            nc.vector.tensor_tensor(gates, size[:], sign[:], ALU.mult).then_inc(mod_step, 2)
            dve.wait_ge(stat_step, 2 * B * NT)
            dve.wait_ge(std_done, 1)
            rstd, nmr = k["rstd"], k["nmr"]
            link(nc.vector.reciprocal(rstd[:], std[:]))
            link(nc.vector.tensor_tensor(nwt[:], rstd[:], rstd[:], ALU.mult))
            link(nc.vector.tensor_scalar_add(std[:], mv[:, :, 1], EPS))
            link(nc.vector.tensor_tensor(nwt[:], nwt[:], std[:], ALU.mult))
            link(nc.vector.tensor_scalar(nwt[:], nwt[:], -0.5, 1.5, ALU.mult, ALU.add))
            link(nc.vector.tensor_tensor(rstd[:], rstd[:], nwt[:], ALU.mult))
            link(nc.vector.scalar_tensor_tensor(nmr[:], mv[:, :, 0], -1.0, rstd[:], ALU.mult, ALU.mult))
            dve.wait_ge(const_in, 16 * N_CONST)
            nc.vector.tensor_scalar_mul(k["neg_sink"][:], k["sink"][:], -1.0).then_inc(neg_done, 1)
            nc.vector.tensor_copy(k["ident_r"][:], k["ident"][:]).then_inc(idr_done, 1)
            nc.vector.tensor_copy(k["ident_b"][:], k["ident"][:]).then_inc(idr_done, 1)
            nc.vector.tensor_copy(k["tri_b"][:], tri[:]).then_inc(idr_done, 1)
            nc.vector.tensor_copy(k["mask_b"][:], mask[:]).then_inc(idr_done, 1)
            nc.vector.memset(k["ones_b"][:], 1.0).then_inc(idr_done, 1)
            for g in range(POOL_LO, HKV):
                dve.wait_ge(hi_done, g + 1)
                split(nc.vector, k["w_hi"][:, :, g], k["w_lo"][:, :, g], w_raw[:, g]).then_inc(lo_done, 1)

        @block.tensor
        def _(pe):
            pe.wait_ge(small_in, 32)
            pe.wait_ge(cond_step, 3)
            for m in range(KM):
                last = nc.tensor.transpose(ps_t[:, m], cond_s[:, m * P:(m + 1) * P], k["ident"][0:B, 0:B])
            last.then_inc(cond_turned, 1)
            pe.wait_ge(cond_copied, 1)
            pe.wait_ge(mod_in, 16)
            for n in range(3):
                for m in range(KM):
                    last = nc.tensor.matmul(ps_m[:, n], cond_t[:, m], w_mod[:, m, n * 512:(n + 1) * 512],
                                            start=(m == 0), stop=(m == KM - 1))
            last.then_inc(mod_done, 1)


def attention(nc, t, k, w, late, xbuf, mod_dram):
    x, ident = k["x"], k["ident"]
    tickets = Tickets()
    with ExitStack() as c:
        def sb(name, shape, dt=F32):
            return c.enter_context(nc.sbuf_tensor(name, shape, dt))

        def psum(name, shape):
            return c.enter_context(nc.psum_tensor(name, shape, F32))

        def sem(name):
            return c.enter_context(nc.semaphore(name))

        mod_a = k["mod_a"]
        h_norm = sb("h_norm", [P, NT, M])
        ht_hi = sb("ht_hi", [P, KM, S], F32R)
        ht_lo = sb("ht_lo", [P, KM, S], F32R)
        qk_raw = sb("qk_raw", [P, NT, RW])
        v = sb("v", [P, 4, NT, D + 1])
        rope_a = sb("rope_a", [P, NT, RW])
        rope_b = sb("rope_b", [P, NT, RW])
        qk_split = sb("qk_split", [P, 2, NT, 2 * R + 3, D], F32R)
        q_t = sb("q_t", [P, 2, R, S], F32R)
        k_t = sb("k_t", [P, 2, 2, S], F32R)
        row_max = sb("row_max", [P, 2, NT, R])
        neg_max = sb("neg_max", [P, 2, NT, R])
        sink_arg = sb("sink_arg", [P, 2, NT, R])
        sink_exp = sb("sink_exp", [P, 2, NT, R])
        probs = sb("probs", [P, 2, NT, R, S])
        probs_t = sb("probs_t", [P, R, NT, S])
        denom = sb("denom", [P, NT, R])
        heads = sb("heads", [P, 2, NT, QW])
        heads_t = sb("heads_t", [P, QW // P, S])
        gate_a = sb("gate_a", [P, 1, M])
        mod_b = sb("mod_b", [P, 3, M])
        attn = sb("attn", [P, NT, M])
        st2 = sb("st2", [P, NT, 6])
        mv2 = sb("mv2", [P, NT, 2])
        var2 = sb("var2", [P, NT])
        y2 = sb("y2", [P, NT])
        z2 = sb("z2", [P, NT])
        nmr2 = sb("nmr2", [P, NT])
        h2 = sb("h2", [P, NT, M])
        h2_t = sb("h2_t", [P, KM, S])
        rs = sb("rs", [P, NT, NX])
        sg = sb("sg", [P, NT, E + F])
        hs = sb("hs", [P, NT, F])
        hs_t = sb("hs_t", [F, S])
        shared = sb("shared", [P, NT, M])
        sbias = sb("sbias", [P, NT, E])
        top2 = sb("top2", [P, NT, G, 8])
        gscore = sb("gscore", [P, NT, 2 * G])
        gtop = sb("gtop", [P, NT, 8])
        grep = sb("grep", [P, NT, 2 * G])
        gmask = sb("gmask", [P, NT, G])
        gneg = sb("gneg", [P, NT, G])
        cand = sb("cand", [P, NT, E])
        etop = sb("etop", [P, NT, 8])
        erep = sb("erep", [P, NT, E])
        sel = sb("sel", [P, NT, E], BF16)
        taken = sb("taken", [P, E], BF16)
        wsum = sb("wsum", [P, NT])
        weight = sb("weight", [P, NT, E])
        pos = sb("pos", [P, NT, E])
        valid = sb("valid", [P, NT, E])
        key = sb("key", [P, NT, E])
        ktop = sb("ktop", [P, NT, 8])
        match = sb("match", [P, K, E])
        kmiss = sb("kmiss", [P, NT, 8])
        scatter_index = sb("scatter_index", [P, NT, 8], U32)
        has_slot = sb("has_slot", [P, NT, K], BF16)
        any_slot = sb("any_slot", [1, NT, K])
        counts_f = sb("counts_f", [1, NT])
        n_scatters = sb("n_scatters", [1, NT], I32)

        pj = psum("pj", [P, 512])
        tb = [psum(f"tb{i}", [P, 512]) for i in range(2)]
        sc = [psum(f"sc{i}", [P, 2, S]) for i in range(2)]
        po = [psum(f"po{i}", [P, 512]) for i in range(NT)]
        op = psum("op", [P, NT, M])

        mod_a_in, mod_b_in, gate_a_in = sem("mod_a_in"), sem("mod_b_in"), sem("gate_a_in")
        preset, h_scaled, h_mult, h_ready, ht_hi_done, ht_ready = (
            sem(n) for n in ("preset", "h_scaled", "h_mult", "h_ready", "ht_hi_done", "ht_ready"))
        proj_done, proj_read, v_read, sin_done, cos_done, roped, qk_hi_done, qk_lo_done, key_again_done = (
            sem(n) for n in ("proj_done", "proj_read", "v_read", "sin_done", "cos_done", "roped", "qk_hi_done", "qk_lo_done", "key_again_done"))
        filled = [sem(f"filled{i}") for i in range(2)]
        drained = [sem(f"drained{i}") for i in range(2)]
        scores_done, row_max_done, neg_max_done, sink_arg_done, probs_done, sink_exp_done = (
            sem(n) for n in ("scores_done", "row_max_done", "neg_max_done", "sink_arg_done", "probs_done", "sink_exp_done"))
        pv_done, denom_done, heads_done, op_done = (sem(n) for n in ("pv_done", "denom_done", "heads_done", "op_done"))
        attn_read, attn_gated, x1_done, norm_step, h2_scaled, h2_mult, h2_done = (
            sem(n) for n in ("attn_read", "attn_gated", "x1_done", "norm_step", "h2_scaled", "h2_mult", "h2_done"))
        sg_exp, rs_copied, sg_step, hs_step, shared_gated, x_done = (
            sem(n) for n in ("sg_exp", "rs_copied", "sg_step", "hs_step", "shared_gated", "x_done"))
        route_step, sel_done, pos_copied, scattered, index_done = (
            sem(n) for n in ("route_step", "sel_done", "pos_copied", "scattered", "index_done"))
        slots_flagged, scatters_counted = sem("slots_flagged"), sem("scatters_counted")
        block = c.enter_context(nc.Block())

        def rounds(eng, step, start, end):
            start()
            for n in range(AHEAD):
                step("steps 0, 1", n, 0, n, None)
            for b, section in enumerate(("first", "second")):
                for l in range(HKV):
                    step(section, l, b, b * HKV + AHEAD + l, l)
            with eng.Fori(2, B - 1) as b:
                for l in range(HKV):
                    step("mid", l, b, b * HKV + AHEAD + l, l)
            for l in range(HKV):
                step("last", l, B - 1, (B - 1) * HKV + AHEAD + l, l)
            end()

        def n_par(l, n):
            return (n if l is None else l) % 2

        def group_of(l, n, lag):
            return (n if l is None else AHEAD + l) % HKV + lag & HKV - 1

        def batch_of(l, n, b, lag):
            return (n + lag) // HKV if l is None else b + (AHEAD + l + lag) // HKV

        def await_full(eng, section, name, b):
            bank, v, _ = tickets.use(section, name, b)
            eng.wait_ge(filled[bank], v)
            return bank

        def await_drained(eng, section, name, b):
            bank, v, _ = tickets.use(section, name, b)
            eng.wait_ge(drained[bank], v)

        def wait_apart(eng, semaphore, value):
            wait_alone(eng, semaphore, value, preset)

        def norm2_modulate(eng, b):
            eng.wait_ge(h2_scaled, 2 * b + 2)
            eng.wait_ge(mod_b_in, 16 * (b + 1))
            eng.tensor_tensor(h2[:], h2[:], mod_b[:, 1:2].to_broadcast((P, NT, M)), ALU.mult).then_inc(h2_mult, 1)
            eng.wait_ge(h2_mult, b + 1)
            eng.tensor_tensor(h2[:], h2[:], mod_b[:, 0:1].to_broadcast((P, NT, M)), ALU.add).then_inc(h2_done, 1)

        def residual(eng, b):
            eng.wait_ge(attn_read, b + 1)
            eng.wait_ge(gate_a_in, 16 * (b + 1))
            eng.tensor_tensor(attn[:], attn[:], gate_a[:].to_broadcast((P, NT, M)), ALU.mult).then_inc(attn_gated, 1)
            wait_apart(eng, attn_gated, b + 1)
            xb = x[:, bass.ds(b * NT, NT)]
            eng.tensor_tensor(xb, xb, attn[:], ALU.add).then_inc(x1_done, 1)

        def add_shared(eng, b):
            wait_apart(eng, shared_gated, b + 1)
            xb = x[:, bass.ds(b * NT, NT)]
            eng.tensor_tensor(xb, xb, shared[:], ALU.add).then_inc(x_done, 1)

        @block.sync
        def _(sp):
            def load_a(b):
                sp.dma_start(mod_a[:], mod_dram[bass.ds(b, 1), 0:2].to_broadcast((P, 2, M))).then_inc(mod_a_in, 16)

            def load_gate(b):
                sp.dma_start(gate_a[:], mod_dram[bass.ds(b, 1), 2:3].to_broadcast((P, 1, M))).then_inc(gate_a_in, 16)

            def load_b(b):
                sp.dma_start(mod_b[:], mod_dram[bass.ds(b, 1), 3:6].to_broadcast((P, 3, M))).then_inc(mod_b_in, 16)

            def step(section, tag, b, n, l):
                if l == 0:
                    if section != "last":
                        sp.wait_ge(h_ready, 2 * b + 2)
                        load_a(b + 1)
                    if section != "first":
                        sp.wait_ge(x1_done, b)
                    load_gate(b)
                    if not isinstance(b, int) or b > 1:
                        sp.wait_ge(shared_gated, b - 1)
                    if section != "first":
                        load_b(b - 1)

            def end():
                sp.wait_ge(shared_gated, B - 1)
                load_b(B - 1)

                sp.wait_ge(proj_done, NT * NG_ALL)
                for r in range(RING):
                    load_gate_up(sp, t, w, r, r)
                    load_down(sp, t, w, r, r)

            rounds(sp, step, lambda: None, end)

        @block.gpsimd
        def _(pool):
            def norm_modulate(b):
                pool.wait_ge(h_scaled, 2 * b + 2)
                if isinstance(b, int) and b == 0:
                    pool.wait_ge(late["first_mod_in"], 16)
                else:
                    pool.wait_ge(mod_a_in, 16 * b)
                nc.gpsimd.tensor_tensor(h_norm[:], h_norm[:], mod_a[:, 1:2].to_broadcast((P, NT, M)), ALU.mult)\
                    .then_inc(h_mult, 1)
                pool.wait_ge(h_mult, b + 1)
                nc.gpsimd.tensor_tensor(h_norm[:], h_norm[:], mod_a[:, 0:1].to_broadcast((P, NT, M)), ALU.add)\
                    .then_inc(h_ready, 2)

            def rope_cos(n, i):
                pool.wait_ge(proj_read, 2 * n + i + 1)
                if not (isinstance(n, int) and n == 0):
                    pool.wait_ge(key_again_done, n)
                nc.gpsimd.tensor_tensor(rope_a[:, i].rearrange("p (h d) -> p h d", d=D),
                                        qk_raw[:, i].rearrange("p (h d) -> p h d", d=D),
                                        k["cos"][:, i:i + 1].to_broadcast((P, R + 1, D)), ALU.mult).then_inc(cos_done, 1)

            def rope_add(n, i):
                pool.wait_ge(cos_done, 2 * n + i + 1)
                pool.wait_ge(sin_done, 2 * n + i + 1)
                nc.gpsimd.tensor_tensor(rope_a[:, i], rope_a[:, i], rope_b[:, i], ALU.add).then_inc(roped, 1)

            def rope_lo(n, par, i):
                pool.wait_ge(qk_hi_done, 2 * n + i + 1)
                full = rope_a[:, i].rearrange("p (h d) -> p h d", d=D)
                split(nc.gpsimd, qk_split[:, par, i, 0:2 * R + 1:2], qk_split[:, par, i, 1:2 * R + 2:2], full)\
                    .then_inc(qk_lo_done, 1)

            def shared_act(b):
                pool.wait_ge(sg_step, 3 * b + 3)
                pool.wait_ge(rs_copied, b + 1)
                nc.gpsimd.tensor_tensor(hs[:], sg[:, :, E:], rs[:, :, E:E + F], ALU.mult).then_inc(hs_step, 1)
                pool.wait_ge(hs_step, 2 * b + 1)
                nc.gpsimd.tensor_tensor(hs[:], hs[:], rs[:, :, E + F:], ALU.mult).then_inc(hs_step, 1)

            def scatter_rows(i, j):
                nc.gpsimd.indirect_dma_start(
                    xbuf, bass.IndirectOffsetOnAxis(ap=scatter_index[:, i, j:j + 1], axis=0),
                    h2[:, i], None, bounds_check=SLOTS - 1, oob_is_err=False).then_inc(scattered, 16)

            def scatter(b, pairs):
                wait_apart(pool, index_done, b + 1)
                if isinstance(b, int) and b == 0 and pairs[0] == (0, 0):
                    pool.wait_ge(late["zero_out"], 16)
                for i, j in pairs:
                    scatter_rows(i, j)

            pairs = [(i, j) for i in range(NT) for j in range(K)]

            def step(section, tag, b, n, l):
                ffn = l is not None and section != "first"
                nxt = l is not None and section != "last"
                if exists(n + 2):
                    rope_cos(n + 2, 0)
                    rope_add(n + 2, 0)
                    rope_cos(n + 2, 1)
                    rope_lo(n + 2, n_par(l, n), 0)
                    rope_add(n + 2, 1)
                if ffn and l == 7:
                    scatter(b - 1, pairs[10:])
                if ffn and l == 1:
                    norm2_modulate(pool, b - 1)
                if nxt and l == 2:
                    norm_modulate(b + 1)
                if exists(n + 2):
                    rope_lo(n + 2, n_par(l, n), 1)
                if ffn and l == 3:
                    shared_act(b - 1)
                if ffn and l == 5:
                    scatter(b - 1, pairs[:5])
                if ffn and l == 6:
                    scatter(b - 1, pairs[5:10])
                if l == 7 and section != "last":
                    residual(pool, b)
                if ffn and l == 7:
                    add_shared(pool, b - 1)

            def start():
                norm_modulate(0)
                for n in range(2):
                    for i in range(NT):
                        rope_cos(n, i)
                        rope_add(n, i)
                        rope_lo(n, n, i)

            def end():
                shared_act(B - 1)
                pool.wait_ge(scatters_counted, 3)
                counts = [pool.value_load(n_scatters[0:1, i:i + 1], min_val=0, max_val=K) for i in range(NT)]
                for i, j in pairs:
                    with pool.If(counts[i] > j):
                        scatter_rows(i, j)
                pool.wait_ge(scattered, 16 * (NT * K * (B - 1) + counts[0] + counts[1]))

            rounds(pool, step, start, end)

        @block.scalar
        def _(act):
            def copy_out(section, name, b, dst, width=512, rows=P):
                bank = await_full(act, section, name, b)
                nc.scalar.activation(dst, tb[bank][0:rows, 0:width], ACT.Copy).then_inc(drained[bank], 1)

            def norm_scale(b):
                if not isinstance(b, int) or b > 0:
                    act.wait_ge(ht_ready, b)
                for i in range(NT):
                    nc.scalar.activation(h_norm[:, i], x[:, bass.ds(b * NT + i, 1)], ACT.Identity,
                                         bias=k["nmr"][:, bass.ds(b * NT + i, 1)],
                                         scale=k["rstd"][:, bass.ds(b * NT + i, 1)]).then_inc(h_scaled, 1)

            def ht_high(section, name, b, nb):
                bank = await_full(act, section, name, b)
                nc.scalar.activation(ht_hi[:].rearrange("p k s -> p (k s)"), tb[bank][:, :], ACT.Copy)\
                    .then_inc(ht_hi_done, 1)

            def qk_high(n, par, i):
                act.wait_ge(roped, 2 * n + i + 1)
                if i == 1:
                    nc.scalar.activation(qk_split[:, par, :, 2 * R + 2], rope_a[:, :, QW:RW], ACT.Copy)\
                        .then_inc(key_again_done, 1)
                nc.scalar.activation(qk_split[:, par, i, 0:2 * R + 1:2], rope_a[:, i].rearrange("p (h d) -> p h d", d=D),
                                     ACT.Copy).then_inc(qk_hi_done, 1)

            def turn_q(section, names, b, par):
                for i in range(NT):
                    copy_out(section, names[i], b, q_t[:, par, :, i * P:(i + 1) * P])

            def positions_out(section, b, fb):
                bank = await_full(act, section, "POS", b)
                if not isinstance(fb, int) or fb > 0:
                    act.wait_ge(index_done, fb)
                nc.scalar.activation(pos[:].rearrange("p i e -> p (i e)"), tb[bank][:, 0:NT * E], ACT.Copy)\
                    .then_inc(pos_copied, 1)
                act.wait_ge(pos_copied, fb + 1)
                act.sem_inc(drained[bank], 1)

            def exps(n, par, i):
                act.wait_ge(neg_max_done, 2 * n + i + 1)
                for h in range(R):
                    nc.scalar.activation(probs[:, par, i, h], sc[h // 2][:, h % 2], ACT.Exp,
                                         bias=neg_max[:, par, i, h:h + 1]).then_inc(probs_done, 1)

            def exp_sink(n, par):
                act.wait_ge(sink_arg_done, n + 1)
                nc.scalar.activation(sink_exp[:, par], sink_arg[:, par], ACT.Exp).then_inc(sink_exp_done, 1)

            def norm2_scale(b):
                act.wait_ge(norm_step, NORM_STEPS * (b + 1))
                if not isinstance(b, int) or b > 0:
                    act.wait_ge(scattered, 16 * NT * K * b)
                for i in range(NT):
                    nc.scalar.activation(h2[:, i], x[:, bass.ds(b * NT + i, 1)], ACT.Identity,
                                         bias=nmr2[:, i:i + 1], scale=y2[:, i:i + 1]).then_inc(h2_scaled, 1)

            def router_out(section, b, fb):
                bank = await_full(act, section, "RS", b)
                full = tb[bank][:, :].rearrange("p (i n) -> p i n", i=NT)
                nc.scalar.activation(sg[:], full[:, :, 0:E + F], ACT.Exp, scale=-1.0).then_inc(sg_exp, 1)
                nc.scalar.activation(rs[:], full, ACT.Copy).then_inc(rs_copied, 1)

            def turned_probs(section, name, b, h):
                copy_out(section, name, b, probs_t[:, h].rearrange("p i s -> p (i s)"))

            def step(section, tag, b, n, l):
                par = n_par(l, n)
                ffn = l is not None and section != "first"
                nxt = l is not None and section != "last"
                if ffn and l == 1:
                    norm2_scale(b - 1)
                if nxt and l == 2:
                    norm_scale(b + 1)
                if exists(n - 1):
                    turned_probs(section, f"P0{tag}", b, 0)
                if exists(n):
                    exps(n, par, 0)
                if exists(n - 1):
                    turned_probs(section, f"P1{tag}", b, 1)
                if exists(n + 2):
                    qk_high(n + 2, par, 0)
                if exists(n - 1):
                    turned_probs(section, f"P2{tag}", b, 2)
                if exists(n - 1):
                    turned_probs(section, f"P3{tag}", b, 3)
                if exists(n + 1):
                    turn_q(section, [f"Q0{tag}", f"Q1{tag}"], b, (par + 1) % 2)
                if exists(n):
                    exps(n, par, 1)
                    exp_sink(n, par)
                if exists(n + 2):
                    qk_high(n + 2, par, 1)
                if ffn and l == 2:
                    router_out(section, b, b - 1)
                if nxt and l == NORM_AT:
                    ht_high(section, "H", b, b + 1)
                if ffn and l == 4:
                    copy_out(section, "HST", b, hs_t[:], S, F)
                if exists(n + 1):
                    copy_out(section, f"KT{tag}", b, k_t[:, (par + 1) % 2])
                if ffn and l == 1:
                    copy_out(section, f"H2T", b, h2_t[:].rearrange("p k s -> p (k s)"))
                if ffn and l == 4:
                    positions_out(section, b, b - 1)

            def start():
                act.wait_ge(preset, 1)
                norm_scale(0)
                ht_high("start", "H", 0, 0)
                for n in range(2):
                    for i in range(NT):
                        qk_high(n, n, i)
                turn_q("start", ["Q0", "Q1"], 0, 0)
                copy_out("start", "KT", 0, k_t[:, 0])

            def end():
                norm2_scale(B - 1)
                copy_out("end", "H2T", 0, h2_t[:].rearrange("p k s -> p (k s)"))
                router_out("end", 0, B - 1)
                positions_out("end", 0, B - 1)
                copy_out("end", "HST", 0, hs_t[:], S, F)

            rounds(act, step, start, end)

        @block.vector
        def _(dve):
            def copy_out(section, name, b, dst, width=512):
                bank = await_full(dve, section, name, b)
                nc.vector.tensor_copy(dst, tb[bank][:, 0:width]).then_inc(drained[bank], 1)

            def ht_low(section, name, b, nb):
                bank, v_, _ = tickets.use(section, name, b)
                dve.wait_ge(ht_hi_done, nb + 1)
                split(nc.vector, ht_hi[:].rearrange("p k s -> p (k s)"), ht_lo[:].rearrange("p k s -> p (k s)"),
                      tb[bank][:, :]).then_inc(ht_ready, 1)
                dve.wait_ge(ht_ready, nb + 1)
                dve.sem_inc(drained[bank], 1)

            def add_bias(n, g, quad, i):
                dve.wait_ge(proj_done, 2 * n + i + 1)
                if not (isinstance(n, int) and n == 0):
                    dve.wait_ge(cos_done, 2 * n + i - 1)
                nc.vector.tensor_tensor(qk_raw[:, i], pj[:, 0:RW], k["bias"][:, g, 0:RW], ALU.add)\
                    .then_inc(proj_read, 1)
                nc.vector.tensor_tensor(v[:, quad, i, 0:D], pj[:, RW:GW], k["bias"][:, g, RW:GW], ALU.add)\
                    .then_inc(v_read, 1)

            def rope_sin(n, i):
                dve.wait_ge(proj_read, 2 * n + i + 1)
                if not (isinstance(n, int) and n == 0):
                    dve.wait_ge(roped, 2 * n + i - 1)
                q2 = qk_raw[:, i].rearrange("p (h e d) -> p h e d", e=2, d=D // 2)[:, :, ::-1]
                b2 = rope_b[:, i].rearrange("p (h e d) -> p h e d", e=2, d=D // 2)
                sn = k["sin"][:, i:i + 1].rearrange("p o (e d) -> p o e d", e=2).to_broadcast((P, R + 1, 2, D // 2))
                nc.vector.tensor_tensor(b2, q2, sn, ALU.mult).then_inc(sin_done, 1)

            def row_maxima(n, par, i, pair):
                dve.wait_ge(scores_done, 2 * (2 * n + i) + pair + 1)
                nc.vector.tensor_reduce(row_max[:, par, i, 2 * pair:2 * pair + 2], sc[pair][:], AX.X, ALU.max)\
                    .then_inc(row_max_done, 1)

            def negate_maxima(n, g, par, i):
                dve.wait_ge(row_max_done, 2 * (2 * n + i) + 2)
                nc.vector.scalar_tensor_tensor(neg_max[:, par, i], row_max[:, par, i], -1.0,
                                               k["neg_sink"][:, g], ALU.mult, ALU.min).then_inc(neg_max_done, 1)

            def sink_exponents(n, g, par):
                dve.wait_ge(neg_max_done, 2 * n + 2)
                nc.vector.tensor_tensor(sink_arg[:, par], neg_max[:, par],
                                        k["sink"][:, g:g + 1].to_broadcast((P, NT, R)), ALU.add)\
                    .then_inc(sink_arg_done, 1)

            def normalise(n, par, i):
                dve.wait_ge(pv_done, 2 * n + i + 1)
                dve.wait_ge(sink_exp_done, n + 1)
                full = po[i][:, 0:R * (D + 1)].rearrange("p (h w) -> p h w", w=D + 1)
                d = denom[:, i].unsqueeze(2)
                nc.vector.tensor_tensor(d, full[:, :, D:D + 1], sink_exp[:, par, i].unsqueeze(2), ALU.add)\
                    .then_inc(denom_done, 1)
                dve.wait_ge(denom_done, 2 * (2 * n + i) + 1)
                nc.vector.reciprocal(denom[:, i], denom[:, i]).then_inc(denom_done, 1)
                dve.wait_ge(denom_done, 2 * (2 * n + i) + 2)
                nc.vector.tensor_tensor(heads[:, par, i].rearrange("p (h d) -> p h d", d=D), full[:, :, 0:D],
                                        d.to_broadcast((P, R, D)), ALU.mult).then_inc(heads_done, 1)

            def attention_out(b):
                dve.wait_ge(op_done, HKV * (b + 1))
                if isinstance(b, int) and b == 0:
                    dve.wait_ge(late["ffn_in"], 16 * 5)
                if not isinstance(b, int) or b > 0:
                    dve.wait_ge(x1_done, b)
                nc.vector.tensor_tensor(attn[:], op[:], k["bo"][:].unsqueeze(1).to_broadcast((P, NT, M)), ALU.add)\
                    .then_inc(attn_read, 1)

            class Chain:

                def __init__(self, semaphore, total):
                    self.semaphore, self.total, self.done = semaphore, total, 0

                def __call__(self, fb, *instructions):
                    for ins in instructions:
                        ins.then_inc(self.semaphore, 1)
                        self.done += 1
                    wait_apart(dve, self.semaphore, self.total * fb + self.done)
                    if self.done == self.total:
                        self.done = 0

            norm, pick = Chain(norm_step, NORM_STEPS), Chain(route_step, ROUTE_STEPS)
            two = range(NT)

            def norm2_stats(b):
                dve.wait_ge(x1_done, b + 1)
                if not isinstance(b, int) or b > 0:
                    dve.wait_ge(h2_scaled, 2 * b)
                norm(b, *[nc.vector.bn_stats(st2[:, i], x[:, bass.ds(b * NT + i, 1)]) for i in two])
                norm(b, *[nc.vector.bn_aggr(mv2[:, i], st2[:, i]) for i in two])

            def norm2_guess(b):
                norm(b, nc.vector.tensor_scalar_add(var2[:], mv2[:, :, 1], EPS))
                norm(b, nc.vector.tensor_scalar(z2[:].bitcast(I32), var2[:].bitcast(I32), 1, None,
                                                ALU.logical_shift_right))
                norm(b, nc.vector.tensor_scalar(y2[:].bitcast(I32), z2[:].bitcast(I32), -1.0, float(SEED),
                                                ALU.mult, ALU.add))

            def norm2_newton(b):
                norm(b, nc.vector.tensor_tensor(z2[:], y2[:], y2[:], ALU.mult))
                norm(b, nc.vector.scalar_tensor_tensor(z2[:], z2[:], -0.5, var2[:], ALU.mult, ALU.mult))
                norm(b, nc.vector.scalar_tensor_tensor(y2[:], z2[:], 1.5, y2[:], ALU.add, ALU.mult))

            def norm2_shift(b):
                norm(b, nc.vector.scalar_tensor_tensor(nmr2[:], mv2[:, :, 0], -1.0, y2[:], ALU.mult, ALU.mult))

            def sigmoid_scores(b):
                dve.wait_ge(sg_exp, b + 1)
                nc.vector.tensor_scalar_add(sg[:], sg[:], 1.0).then_inc(sg_step, 1)
                dve.wait_ge(sg_step, 3 * b + 1)
                nc.vector.reciprocal(sg[:, :, 0:E], sg[:, :, 0:E]).then_inc(sg_step, 1)
                dve.wait_ge(sg_step, 3 * b + 2)

            def sigmoid_gate(b):
                nc.vector.reciprocal(sg[:, :, E:], sg[:, :, E:]).then_inc(sg_step, 1)

            def release_rs(section, b, fb):
                bank, _, _ = tickets.use(section, "RS", b)
                dve.wait_ge(rs_copied, fb + 1)
                dve.sem_inc(drained[bank], 1)

            full = (P, NT, G, E // G)

            def each(a):
                return a[:].rearrange("p i (g e) -> p i g e", g=G)

            def route_bests(fb):
                pick(fb, nc.vector.tensor_tensor(sbias[:], sg[:, :, 0:E], k["r_bias"][:].unsqueeze(1).to_broadcast((P, NT, E)), ALU.add))
                pick(fb, *[nc.vector.max(top2[:, i, g], sbias[:, i, g * 8:g * 8 + 8]) for i in two for g in range(G)])

            def route_groups(fb):
                pick(fb, nc.vector.tensor_tensor(gscore[:, :, 0:G], top2[:, :, :, 0], top2[:, :, :, 1], ALU.add))
                pick(fb, *[nc.vector.max(gtop[:, i], gscore[:, i]) for i in two])
                pick(fb, nc.vector.memset(gtop[:, :, KG:], -BIG))
                pick(fb, *[nc.vector.match_replace(grep[:, i], gtop[:, i], gscore[:, i], -2.0 * BIG) for i in two])

            def route_candidates(fb):
                pick(fb, nc.vector.tensor_tensor(gmask[:], grep[:, :, 0:G], gscore[:, :, 0:G], ALU.not_equal))
                pick(fb, nc.vector.tensor_scalar(gneg[:], gmask[:], -1.0, BIG, ALU.add, ALU.mult),
                     nc.vector.tensor_tensor(each(cand), each(sbias), gmask[:].unsqueeze(3).to_broadcast(full), ALU.mult))
                pick(fb, nc.vector.tensor_tensor(each(cand), each(cand), gneg[:].unsqueeze(3).to_broadcast(full), ALU.add))

            def route_experts(fb):
                pick(fb, *[nc.vector.max(etop[:, i], cand[:, i]) for i in two])
                pick(fb, nc.vector.memset(etop[:, :, K:], -BIG))
                pick(fb, *[nc.vector.match_replace(erep[:, i], etop[:, i], cand[:, i], -2.0 * BIG) for i in two])
                pick(fb, nc.vector.tensor_tensor(erep[:], erep[:], cand[:], ALU.not_equal))
                pick(fb, nc.vector.tensor_tensor(each(sel), each(erep), gmask[:].unsqueeze(3).to_broadcast(full), ALU.mult))
                dve.sem_inc(sel_done, 1)

            def route_weights(fb):
                pick(fb, nc.vector.tensor_tensor(weight[:], sg[:, :, 0:E], sel[:], ALU.mult))
                pick(fb, nc.vector.tensor_reduce(wsum[:], weight[:], AX.X, ALU.add))
                pick(fb, nc.vector.reciprocal(wsum[:], wsum[:]))
                pick(fb, nc.vector.scalar_tensor_tensor(weight[:], weight[:], ROUTE_SCALE,
                                                        wsum[:].unsqueeze(2).to_broadcast((P, NT, E)), ALU.mult, ALU.mult))
                pick(fb, nc.vector.tensor_tensor(weight[:], weight[:], valid[:], ALU.mult))

            def route_slots(fb):
                dve.wait_ge(pos_copied, fb + 1)
                pick(fb, nc.vector.scalar_tensor_tensor(valid[:], pos[:], float(CAP), sel[:], ALU.is_lt, ALU.mult),
                     nc.vector.tensor_tensor(key[:], pos[:], k["slot_base"][:].unsqueeze(1).to_broadcast((P, NT, E)), ALU.add),
                     nc.vector.tensor_tensor(taken[:], taken[:], sel[:, 0], ALU.add))
                pick(fb, nc.vector.tensor_tensor(key[:], key[:], valid[:], ALU.mult),
                     nc.vector.tensor_tensor(taken[:], taken[:], sel[:, 1], ALU.add))
                pick(fb, *[nc.vector.max(ktop[:, i], key[:, i]) for i in two])

            def route_index(fb):
                if not isinstance(fb, int) or fb > 0:
                    dve.wait_ge(scattered, 16 * NT * K * fb)
                pick(fb, nc.vector.tensor_scalar(kmiss[:], ktop[:], 0.0, 1.0e6, ALU.is_equal, ALU.mult))
                pick(fb, nc.vector.scalar_tensor_tensor(kmiss[:], ktop[:], -1.0, kmiss[:], ALU.add, ALU.add))
                pick(fb, nc.vector.tensor_copy(scatter_index[:], kmiss[:]),
                     nc.vector.tensor_copy(k["slot_index"][:, bass.ds(fb * NT, NT)], kmiss[:]))
                dve.sem_inc(index_done, 1)

            def count_scatters():
                nc.vector.tensor_scalar(has_slot[:], kmiss[:, :, 0:K], float(SLOTS), None, ALU.is_lt).then_inc(slots_flagged, 1)
                bank = await_full(dve, "end", "COUNT", 0)
                nc.vector.tensor_scalar(any_slot[:], tb[bank][0:1, 0:NT * K].rearrange("o (i k) -> o i k", i=NT), 0.0, None,
                                        ALU.is_gt).then_inc(scatters_counted, 1)
                dve.wait_ge(scatters_counted, 1)
                dve.sem_inc(drained[bank], 1)
                nc.vector.tensor_reduce(counts_f[:], any_slot[:], AX.X, ALU.add).then_inc(scatters_counted, 1)
                dve.wait_ge(scatters_counted, 2)
                nc.vector.tensor_copy(n_scatters[:], counts_f[:]).then_inc(scatters_counted, 1)

            def route_match(fb, i):
                wide = (P, K, E)
                pick(fb, nc.vector.tensor_tensor(match[:], key[:, i:i + 1].to_broadcast(wide),
                                                 ktop[:, i, 0:K].unsqueeze(2).to_broadcast(wide), ALU.is_equal))
                pick(fb, nc.vector.tensor_tensor(match[:], match[:], weight[:, i:i + 1].to_broadcast(wide), ALU.mult))
                pick(fb, nc.vector.tensor_reduce(k["slot_weight"][:, bass.ds(fb * NT + i, 1)], match[:].unsqueeze(1),
                                                 AX.X, ALU.add))

            def shared_out(section, b, fb):
                bank = await_full(dve, section, "SD", b)
                if not isinstance(fb, int) or fb > 0:
                    dve.wait_ge(x_done, fb)
                nc.vector.tensor_tensor(shared[:], tb[bank][:, :].rearrange("p (i m) -> p i m", i=NT),
                                        mod_b[:, 2:3].to_broadcast((P, NT, M)), ALU.mult).then_inc(shared_gated, 1)
                dve.wait_ge(shared_gated, fb + 1)
                dve.sem_inc(drained[bank], 1)

            def ffn_part(section, b, l, at):
                fb = b - 1
                if (l, at) == (0, "early"):
                    norm2_stats(fb)
                    norm2_guess(fb)
                if (l, at) == (0, "before"):
                    for _ in range(3):
                        norm2_newton(fb)
                    norm2_shift(fb)
                if (l, at) == (2, "between"):
                    sigmoid_scores(fb)
                    release_rs(section, b, fb)
                if (l, at) == (3, "early"):
                    sigmoid_gate(fb)
                if (l, at) == (3, "before"):
                    route_bests(fb)
                if (l, at) == (4, "early"):
                    route_groups(fb)
                    route_candidates(fb)
                if (l, at) == (4, "before"):
                    route_experts(fb)
                if (l, at) == (5, "early"):
                    route_slots(fb)
                if (l, at) == (5, "before"):
                    route_index(fb)
                if (l, at) == (5, "between"):
                    shared_out(section, b, fb)
                if (l, at) == (6, "early"):
                    route_weights(fb)
                if (l, at) == (6, "before"):
                    route_match(fb, 0)
                if (l, at) == (7, "early"):
                    route_match(fb, 1)

            def step(section, tag, b, n, l):
                par = n_par(l, n)
                ffn = l is not None and section != "first"
                if exists(n + 2):
                    add_bias(n + 2, group_of(l, n, 2), group_of(l, n, 2) % 4, 0)
                if exists(n):
                    row_maxima(n, par, 0, 0)
                if exists(n - 2):
                    copy_out(section, f"AT{tag}", b, heads_t[:].rearrange("p k s -> p (k s)"))
                if exists(n):
                    row_maxima(n, par, 0, 1)
                    negate_maxima(n, group_of(l, n, 0), par, 0)
                if exists(n + 2):
                    rope_sin(n + 2, 0)
                    add_bias(n + 2, group_of(l, n, 2), group_of(l, n, 2) % 4, 1)
                if ffn:
                    ffn_part(section, b, l, "early")
                if exists(n):
                    row_maxima(n, par, 1, 0)
                if exists(n + 2):
                    rope_sin(n + 2, 1)
                if exists(n):
                    row_maxima(n, par, 1, 1)
                    negate_maxima(n, group_of(l, n, 0), par, 1)
                    sink_exponents(n, group_of(l, n, 0), par)
                if l == 7:
                    attention_out(b)
                if ffn:
                    ffn_part(section, b, l, "before")
                if exists(n - 1):
                    normalise(n - 1, 1 - par, 0)
                if l == NORM_AT and section != "last":
                    ht_low(section, "H", b, b + 1)
                if ffn:
                    ffn_part(section, b, l, "between")
                if exists(n - 1):
                    normalise(n - 1, 1 - par, 1)

            def start():
                nc.vector.memset(v[:, :, :, D:D + 1], 1.0)
                nc.vector.memset(taken[:], 0.0)
                nc.vector.memset(gscore[:, :, G:], -BIG).then_inc(preset, 1)
                ht_low("start", "H", 0, 0)
                for n in range(2):
                    for i in range(NT):
                        add_bias(n, n, n, i)
                        rope_sin(n, i)

            def end():
                fb = B - 1
                residual(dve, fb)
                norm2_stats(fb)
                norm2_guess(fb)
                for _ in range(3):
                    norm2_newton(fb)
                norm2_shift(fb)
                norm2_modulate(dve, fb)
                sigmoid_scores(fb)
                release_rs("end", 0, fb)
                route_bests(fb)
                route_groups(fb)
                route_candidates(fb)
                route_experts(fb)
                sigmoid_gate(fb)
                route_slots(fb)
                route_index(fb)
                count_scatters()
                route_weights(fb)
                for i in two:
                    route_match(fb, i)
                shared_out("end", 0, fb)
                add_shared(dve, fb)

            rounds(dve, step, start, end)

        @block.tensor
        def _(pe):
            def claim(section, name, b):
                bank, _, before = tickets.use(section, name, b)
                if before is not None:
                    pe.wait_ge(drained[bank], before)
                return bank

            def turn_norm(section, name, b, nb):
                pe.wait_ge(h_ready, 2 * nb + 2)
                bank = claim(section, name, b)
                for m in range(KM):
                    for i in range(NT):
                        last = nc.tensor.transpose(tb[bank][:, m * S + i * P:m * S + (i + 1) * P],
                                                   h_norm[:, i, m * P:(m + 1) * P], ident[:])
                last.then_inc(filled[bank], 1)

            def project(nb, n, g, i):
                pe.wait_ge(ht_ready, nb + 1)
                if not (isinstance(n, int) and n == 0 and i == 0):
                    pe.wait_ge(proj_read, 2 * n + i)
                    pe.wait_ge(v_read, 2 * n + i)
                rows = slice(i * P, (i + 1) * P)
                terms = [(a, w, m) for m in range(KM) for a, w in
                         ((ht_hi, k["w_hi"]), (ht_hi, k["w_lo"]), (ht_lo, k["w_hi"]))]
                for j, (a, w, m) in enumerate(terms):
                    last = nc.tensor.matmul(pj[:, 0:GW], a[:, m, rows], w[:, m, g],
                                            start=(j == 0), stop=(j == len(terms) - 1))
                last.then_inc(proj_done, 1)

            def turn_q(section, name, b, n, par, i):
                pe.wait_ge(qk_lo_done, 2 * n + i + 1)
                bank = claim(section, name, b)
                for h in range(R):
                    last = nc.tensor.matmul(tb[bank][:, h * P:(h + 1) * P],
                                            qk_split[:, par, i, 2 * h:2 * h + 2].rearrange("p e d -> p (e d)"),
                                            k["ident_r"][:], start=True, stop=True)
                last.then_inc(filled[bank], 1)

            def turn_k(section, name, b, n, par):
                pe.wait_ge(key_again_done, n + 1)
                bank = claim(section, name, b)
                for e in range(2):
                    for i in range(NT):
                        pair = qk_split[:, par, i, 2 * R + e:2 * R + e + 2].rearrange("p e d -> p (e d)")
                        last = nc.tensor.matmul(tb[bank][:, e * S + i * P:e * S + (i + 1) * P], pair,
                                                k["ident_r"][:], start=True, stop=True)
                last.then_inc(filled[bank], 1)

            def scores(n, par, i, pair):
                if not (isinstance(n, int) and n == 0 and i == 0):
                    pe.wait_ge(probs_done, R * (2 * n + i - 1) + 2 * pair + 2)
                rows = slice(i * P, (i + 1) * P)
                far = slice((1 - i) * P, (2 - i) * P)
                def product(e, part):
                    return nc.tensor.matmul(sc[pair][:, e], q_t[:, par, 2 * pair + e, rows], k_t[:, par, part],
                                            start=(part == 0 and e == 0), stop=(part == 1), skip_group_check=True)

                for e in range(2):
                    product(e, 0)
                nc.tensor.matmul(sc[pair][:, :, far], k["ident_b"][:],
                                 k["mask_b"][:, i:i + 1].to_broadcast((P, 2, P)),
                                 start=False, stop=False, skip_group_check=True)
                for e in range(2):
                    last = product(e, 1)
                last.then_inc(scores_done, 1)

            def turn_probs(section, name, b, n, par, h):
                if h == 0:
                    pe.wait_ge(probs_done, 2 * R * (n + 1))
                bank = claim(section, name, b)
                for j in range(NT):
                    for i in range(NT):
                        last = nc.tensor.transpose(tb[bank][:, j * S + i * P:j * S + (i + 1) * P],
                                                   probs[:, par, i, h, j * P:(j + 1) * P], ident[:])
                last.then_inc(filled[bank], 1)

            def values(section, names, b, n, quad, i):
                if i == 0:
                    for name in names[2:]:
                        await_drained(pe, section, name, b)
                if not (isinstance(n, int) and n == 0):
                    pe.wait_ge(heads_done, 2 * n + i - 1)
                for h in range(R):
                    for j in range(NT):
                        last = nc.tensor.matmul(po[i][:, h * (D + 1):(h + 1) * (D + 1)],
                                                probs_t[:, h, j, i * P:(i + 1) * P], v[:, quad, j],
                                                start=(j == 0), stop=(j == NT - 1))
                last.then_inc(pv_done, 1)

            def turn_heads(section, name, b, n, par):
                pe.wait_ge(heads_done, 2 * n + 2)
                bank = claim(section, name, b)
                for m in range(QW // P):
                    for i in range(NT):
                        last = nc.tensor.transpose(tb[bank][:, m * S + i * P:m * S + (i + 1) * P],
                                                   heads[:, par, i, m * P:(m + 1) * P], ident[:])
                last.then_inc(filled[bank], 1)

            def project_out(section, name, b, n, g, nb):
                await_drained(pe, section, name, b)
                if isinstance(n, int) and n == 0:
                    pe.wait_ge(late["wo_in"], 16)
                if g == 0 and not (isinstance(nb, int) and nb == 0):
                    pe.wait_ge(attn_read, nb)
                for i in range(NT):
                    for m in range(QW // P):
                        last = nc.tensor.matmul(op[:, i], heads_t[:, m, i * P:(i + 1) * P],
                                                k["wo"][:, g * (QW // P) + m],
                                                start=(g == 0 and i == 0 and m == 0),
                                                stop=(g == HKV - 1 and m == QW // P - 1), skip_group_check=True)
                last.then_inc(op_done, 1)

            def turn_norm2(section, b, fb):
                pe.wait_ge(h2_done, fb + 1)
                bank = claim(section, "H2T", b)
                for m in range(KM):
                    for i in range(NT):
                        last = nc.tensor.transpose(tb[bank][:, m * S + i * P:m * S + (i + 1) * P],
                                                   h2[:, i, m * P:(m + 1) * P], ident[:])
                last.then_inc(filled[bank], 1)

            def router(section, b):
                await_drained(pe, section, "H2T", b)
                if section == "second":
                    pe.wait_ge(late["ffn_in"], 16 * 5)
                bank = claim(section, "RS", b)
                for i in range(NT):
                    for m in range(KM):
                        last = nc.tensor.matmul(tb[bank][:, i * NX:(i + 1) * NX], h2_t[:, m, i * P:(i + 1) * P],
                                                k["w_router"][:, m], start=(m == 0), stop=(m == KM - 1))
                last.then_inc(filled[bank], 1)

            def turn_shared(section, b, fb):
                pe.wait_ge(hs_step, 2 * fb + 2)
                bank = claim(section, "HST", b)
                for i in range(NT):
                    last = nc.tensor.transpose(tb[bank][0:F, i * P:(i + 1) * P], hs[:, i], ident[:])
                last.then_inc(filled[bank], 1)

            def positions(section, b, fb):
                pe.wait_ge(sel_done, fb + 1)
                bank = claim(section, "POS", b)
                for i in range(NT):
                    out = tb[bank][:, i * E:(i + 1) * E]
                    nc.tensor.matmul(out, k["tri_b"][:], sel[:, i], start=True, stop=False)
                    last = nc.tensor.matmul(out, k["ones_b"][:], taken[:], start=False, stop=(i == 0))
                    if i == 1:
                        last = nc.tensor.matmul(out, k["ones_b"][:], sel[:, 0], start=False, stop=True)
                last.then_inc(filled[bank], 1)

            def shared_down(section, b):
                await_drained(pe, section, "HST", b)
                bank = claim(section, "SD", b)
                for i in range(NT):
                    last = nc.tensor.matmul(tb[bank][:, i * M:(i + 1) * M], hs_t[:, i * P:(i + 1) * P],
                                            k["w_sdown"][:], start=True, stop=True)
                last.then_inc(filled[bank], 1)

            def step(section, tag, b, n, l):
                par = n_par(l, n)
                ffn = l is not None and section != "first"
                turned = [f"P{h}{tag}" for h in range(R)]

                def probs_unit(h):
                    if exists(n - 1):
                        turn_probs(section, turned[h], b, n - 1, 1 - par, h)

                if exists(n + 2):
                    project(batch_of(l, n, b, 2), n + 2, group_of(l, n, 2), 0)
                if exists(n):
                    scores(n, par, 0, 0)
                if exists(n - 2):
                    turn_heads(section, f"AT{tag}", b, n - 2, par)
                if exists(n):
                    scores(n, par, 0, 1)
                probs_unit(0)
                if exists(n + 2):
                    project(batch_of(l, n, b, 2), n + 2, group_of(l, n, 2), 1)
                probs_unit(1)
                probs_unit(2)
                if exists(n - 2):
                    project_out(section, f"AT{tag}", b, n - 2, group_of(l, n, -2), batch_of(l, n, b, -2))
                if exists(n):
                    scores(n, par, 1, 0)
                probs_unit(3)
                if exists(n):
                    scores(n, par, 1, 1)
                if exists(n + 1):
                    for i in range(NT):
                        turn_q(section, f"Q{i}{tag}", b, n + 1, 1 - par, i)
                if exists(n - 1):
                    values(section, turned, b, n - 1, group_of(l, n, -1) % 4, 0)
                if ffn and l == 2:
                    router(section, b)
                if l == NORM_AT and section != "last":
                    turn_norm(section, "H", b, b + 1)
                if ffn and l == 4:
                    turn_shared(section, b, b - 1)
                if ffn and l == 5:
                    shared_down(section, b)
                if exists(n + 1):
                    turn_k(section, f"KT{tag}", b, n + 1, 1 - par)
                if exists(n - 1):
                    values(section, turned, b, n - 1, group_of(l, n, -1) % 4, 1)
                if ffn and l == 1:
                    turn_norm2(section, b, b - 1)
                if ffn and l == 4:
                    positions(section, b, b - 1)
                if exists(n + 1):
                    for unit in ("Q1", "KT"):
                        await_drained(pe, section, f"{unit}{tag}", b)

            def start():
                pe.wait_ge(preset, 1)
                turn_norm("start", "H", 0, 0)
                for n in range(2):
                    for i in range(NT):
                        project(0, n, n, i)
                for i in range(NT):
                    turn_q("start", f"Q{i}", 0, 0, 0, i)
                turn_k("start", "KT", 0, 0, 0)
                for name in ("Q1", "KT"):
                    await_drained(pe, "start", name, 0)

            def end():
                turn_norm2("end", 0, B - 1)
                router("end", 0)
                positions("end", 0, B - 1)
                pe.wait_ge(slots_flagged, 1)
                bank = claim("end", "COUNT", 0)
                nc.tensor.matmul(tb[bank][0:1, 0:NT * K], k["ones_b"][:, 0:1], has_slot[:].rearrange("p i k -> p (i k)"),
                                 start=True, stop=True).then_inc(filled[bank], 1)
                turn_shared("end", 0, B - 1)
                shared_down("end", 0)

            rounds(pe, step, start, end)


NORM_STEPS = 2 * NT + 3 + 3 * 3 + 1
ROUTE_STEPS = (1 + NT * G) + (1 + NT + 1 + NT) + (1 + 2 + 1) + (NT + 1 + NT + 1 + 1) + 4 \
    + (3 + 3 + NT) + (1 + 1 + 2) + 3 * NT


CHUNK = 4
CS = CHUNK * CAP
RING = 4
NCHUNK = E // CHUNK
HALF = CS // 2
PAIR_ROWS = P // 2


def expert_weights(nc, ctx, base, end):
    w = dict(gate_up=[], down=[],
             gate_up_in=[ctx.enter_context(nc.semaphore(f"gate_up_in{i}")) for i in range(RING)],
             down_in=[ctx.enter_context(nc.semaphore(f"down_in{i}")) for i in range(RING)])
    at = base
    for r in range(RING):
        w["gate_up"].append(nc.alloc_sbuf_tensor_at(f"w_gate_up{r}", [P, 2, CHUNK, KM * F], F32, offset=at))
        at += 2 * CHUNK * KM * F * 4
        w["down"].append(nc.alloc_sbuf_tensor_at(f"w_down{r}", [F, CHUNK, M], F32, offset=at))
        at += CHUNK * M * 4
    assert at <= end
    return w


def load_gate_up(sp, t, w, a, r):
    e = bass.ds(a * CHUNK, CHUNK)
    for u, name in enumerate(("w_gate", "w_up")):
        sp.dma_start(w["gate_up"][r][:, u], t[name].rearrange("e (p k) f -> p e (k f)", k=KM)[:, e])\
            .then_inc(w["gate_up_in"][r], 16)


def load_down(sp, t, w, a, r):
    sp.dma_start(w["down"][r][:], t["w_down"].rearrange("e f m -> f e m")[:, bass.ds(a * CHUNK, CHUNK)])\
        .then_inc(w["down_in"][r], 16)


def experts(nc, t, w, x, ident, slot_index, slot_weight, xbuf, ybuf, mod_dram):
    with ExitStack() as c:
        def sb(name, shape, dt=F32):
            return c.enter_context(nc.sbuf_tensor(name, shape, dt))

        def sem(name):
            return c.enter_context(nc.semaphore(name))

        rows = sb("rows", [HALF, RING, 2, M])
        rows_t = sb("rows_t", [P, 2, KM, CS + PAIR_ROWS - CAP])
        ex = sb("ex", [P, 2, CHUNK // 2, F])
        hid = sb("hid", [P, 2, CHUNK // 2, F])
        hid_t = sb("hid_t", [F, 2, CHUNK // 2, P])
        out_rows = sb("out_rows", [P, 2, CHUNK // 2, M])
        has_slot = sb("all_has_slot", [P, B * NT, K], BF16)
        ones = sb("ones", [P, 1], BF16)
        any_slot = sb("all_any_slot", [1, B * NT, K])
        n_gathers = sb("n_gathers", [1, B * NT])
        n_gathers_i = sb("n_gathers_i", [1, B * NT], I32)
        arrived = sb("arrived", [1, B // 2, 2])
        n_arrivals = sb("n_arrivals", [1, B // 2, 2], I32)
        gathered = sb("gathered", [P, 2, NT, K, M])
        index = sb("index", [P, 2, NT, 8], U32)
        wts = sb("wts", [P, 2, NT, K])
        total = sb("total", [P, 2, NT, M])
        gate = sb("gate", [P, B, M])
        result = sb("result", [P, 2, NT, M])
        pt, pg, ph, pd = ([c.enter_context(nc.psum_tensor(f"{n}{i}", [P, 512], F32)) for i in range(2)]
                          for n in ("pt", "pg", "ph", "pd"))

        rows_in = [sem(f"rows_in{i}") for i in range(RING)]
        turned, turned_out, hidden_done, exp_done, act_step, hid_done, hid_turned, hid_t_done, down_done = (
            sem(n) for n in ("turned", "turned_out", "hidden_done", "exp_done", "act_step", "hid_done", "hid_turned",
                             "hid_t_done", "down_done"))
        out_done, padded, stored = sem("out_done"), sem("padded"), [sem(f"stored{i}") for i in range(2)]
        flagged, counted, count_step = sem("flagged"), sem("counted"), sem("count_step")
        gate_in, cleared, picked, wts_done, begun, sum_step, gated, result_done = (
            sem(n) for n in ("gate_in", "cleared", "picked", "wts_done", "begun", "sum_step", "gated", "result_done"))
        gathered_in, written, summed = ([sem(f"{n}{i}") for i in range(2)] for n in ("gathered_in", "written", "summed"))
        block = c.enter_context(nc.Block())
        y_rows = ybuf.rearrange("(e two s) m -> two s e m", two=2, s=CAP)
        x_rows = xbuf.rearrange("(a h s) m -> s a h m", h=2, s=HALF)

        def chunks(eng, step):
            for r in range(RING):
                step(r, r)
            with eng.Fori(1, NCHUNK // RING - 1) as i:
                for r in range(RING):
                    step(i * RING + r, r)
            for r in range(RING):
                step(NCHUNK - RING + r, r)

        def exists(a):
            return not isinstance(a, int) or a < NCHUNK

        def batches(eng, step):
            for par in range(2):
                step(par, B - 2 + par, par, 0)
            with eng.Fori(1, B // 2) as i:
                for par in range(2):
                    step(i * 2 + par, i * 2 - 2 + par, par, i)

        def is_first(a, n):
            return isinstance(a, int) and a < n

        @block.sync
        def _(sp):
            def load_rows(a, r):
                sp.dma_start(rows[:, r], x_rows[:, bass.ds(a, 1)]).then_inc(rows_in[r], 16)

            def refill(a, r):
                if exists(a + RING):
                    sp.wait_ge(turned, a + 1)
                    load_rows(a + RING, r)
                    sp.wait_ge(hidden_done, a + 1)
                    load_gate_up(sp, t, w, a + RING, r)
                if not is_first(a, 2) and exists(a - 2 + RING):
                    sp.wait_ge(down_done, a - 1)
                    load_down(sp, t, w, a - 2 + RING, (r - 2) % RING)

            for r in range(RING):
                load_rows(r, r)
            sp.dma_start(gate[:], mod_dram[:, 5].unsqueeze(0).to_broadcast((P, B, M))).then_inc(gate_in, 16)
            chunks(sp, refill)
            out = t["out"].rearrange("(t p) m -> p t m", p=P)

            def store_out(s, b, par, i):
                sp.wait_ge(result_done, s + 1)
                sp.dma_start(out[:, bass.ds(b * NT, NT)], result[:, par]).then_inc(written[par], 16)

            batches(sp, store_out)
            for par in range(2):
                sp.wait_ge(written[par], 16 * B // 2)

        @block.tensor
        def _(pe):
            pe.wait_ge(flagged, 2)
            nc.tensor.matmul(pd[1][0:1, 0:B * NT * K], ones[:], has_slot[:].rearrange("p n k -> p (n k)"),
                             start=True, stop=True).then_inc(counted, 1)

            def loads(a, r):
                return a // RING + 1 if isinstance(a, int) else (a - r) // RING + 1

            def turn_rows(a, r):
                pe.wait_ge(rows_in[r], 16 * loads(a, r))
                if not is_first(a, 2):
                    pe.wait_ge(turned_out, a - 1)
                for m in range(KM):
                    for h in range(2):
                        src = rows[:, r, h].rearrange("s (p k) -> s k p", k=KM)[:, m]
                        last = nc.tensor.transpose(pt[r % 2][:, m * CS + h * HALF:m * CS + (h + 1) * HALF],
                                                   src, ident[0:HALF, 0:HALF])
                last.then_inc(turned, 1)

            def gate_up(a, r):
                par = r % 2
                pe.wait_ge(w["gate_up_in"][r], 32 * loads(a, r))
                pe.wait_ge(turned_out, a + 1)
                if is_first(a, 1):
                    pe.wait_ge(padded, 1)
                if not is_first(a, 2):
                    pe.wait_ge(hid_done, a - 1)
                for pair in range(CHUNK // 2):
                    for m in range(KM):
                        for q in range(2):
                            e = 2 * pair + q
                            last = nc.tensor.matmul(
                                pg[par][q * PAIR_ROWS:(q + 1) * PAIR_ROWS, pair * 2 * F:(pair + 1) * 2 * F]
                                .rearrange("s (u f) -> s u f", u=2),
                                rows_t[:, par, m, e * CAP:e * CAP + PAIR_ROWS],
                                w["gate_up"][r][:, :, e, m * F:(m + 1) * F],
                                start=(m == 0), stop=(m == KM - 1))
                last.then_inc(hidden_done, 1)

            def turn_hidden(a, r):
                par = r % 2
                pe.wait_ge(hid_done, a + 1)
                if not is_first(a, 2):
                    pe.wait_ge(hid_t_done, a - 1)
                for pair in range(CHUNK // 2):
                    last = nc.tensor.transpose(ph[par][0:F, pair * P:(pair + 1) * P], hid[:, par, pair], ident[:])
                last.then_inc(hid_turned, 1)

            def down(a, r):
                par = r % 2
                pe.wait_ge(w["down_in"][r], 16 * loads(a, r))
                pe.wait_ge(hid_t_done, a + 1)
                if not is_first(a, 2):
                    pe.wait_ge(out_done, a - 1)
                elif a == 1:
                    pe.wait_ge(count_step, 1)
                for pair in range(CHUNK // 2):
                    for q in range(2):
                        rows_q = slice(q * PAIR_ROWS, (q + 1) * PAIR_ROWS)
                        last = nc.tensor.matmul(pd[par][rows_q, pair * M:(pair + 1) * M], hid_t[:, par, pair, rows_q],
                                                w["down"][r][:, 2 * pair + q], start=True, stop=True)
                last.then_inc(down_done, 1)

            def step(a, r):
                if exists(a + 2):
                    gate_up(a + 2, (r + 2) % RING)
                if exists(a + 3):
                    turn_rows(a + 3, (r + 3) % RING)
                if exists(a + 1):
                    turn_hidden(a + 1, (r + 1) % RING)
                down(a, r)

            for a in range(3):
                turn_rows(a, a)
                if a < 2:
                    gate_up(a, a)
            turn_hidden(0, 0)
            chunks(pe, step)

        def stores_before(a, r):
            return 32 * (a // 2) if isinstance(a, int) else 32 * ((a - r) // 2 + r // 2)

        @block.scalar
        def _(act):
            def rows_out(a, r):
                act.wait_ge(turned, a + 1)
                if not is_first(a, 2):
                    act.wait_ge(hidden_done, a - 1)
                nc.scalar.activation(rows_t[:, r % 2, :, 0:CS],
                                     pt[r % 2][:, 0:KM * CS].rearrange("p (k s) -> p k s", k=KM), ACT.Copy).then_inc(turned_out, 1)

            def exp_gate(a, r):
                act.wait_ge(hidden_done, a + 1)
                if not is_first(a, 2):
                    act.wait_ge(hid_done, a - 1)
                gates = pg[r % 2][:, 0:CHUNK * F].rearrange("s (p u f) -> s p u f", u=2, f=F)[:, :, 0]
                nc.scalar.activation(ex[:, r % 2], gates, ACT.Exp, scale=-1.0).then_inc(exp_done, 1)

            def hidden_out(a, r):
                act.wait_ge(hid_turned, a + 1)
                if not is_first(a, 2):
                    act.wait_ge(down_done, a - 1)
                nc.scalar.activation(hid_t[:, r % 2].rearrange("f p s -> f (p s)"), ph[r % 2][0:F, 0:CHUNK // 2 * P],
                                     ACT.Copy).then_inc(hid_t_done, 1)

            def out(a, r):
                par = r % 2
                act.wait_ge(down_done, a + 1)
                if not is_first(a, 2):
                    act.wait_ge(stored[par], stores_before(a, r))
                nc.scalar.activation(out_rows[:, par].rearrange("s p m -> s (p m)"), pd[par][:], ACT.Copy)\
                    .then_inc(out_done, 1)
                act.wait_ge(out_done, a + 1)
                pairs = bass.ds(a * (CHUNK // 2), CHUNK // 2)
                for q in range(2):
                    act.dma_start(y_rows[q, :, pairs], out_rows[q * PAIR_ROWS:q * PAIR_ROWS + CAP, par])\
                        .then_inc(stored[par], 16)

            def step(a, r):
                if exists(a + 2):
                    exp_gate(a + 2, (r + 2) % RING)
                if exists(a + 3):
                    rows_out(a + 3, (r + 3) % RING)
                if exists(a + 1):
                    hidden_out(a + 1, (r + 1) % RING)
                out(a, r)

            for a in range(3):
                rows_out(a, a)
                if a < 2:
                    exp_gate(a, a)
            hidden_out(0, 0)
            chunks(act, step)

            def begin_sum(s, b, par, i):
                arrivals = act.value_load(n_arrivals[0:1, bass.ds(i, 1), par], min_val=16, max_val=16 * NT * K * B)
                if not isinstance(i, int):
                    act.wait_ge(result_done, s - 1)
                nc.scalar.activation(wts[:, par], slot_weight[:, bass.ds(b * NT, NT)], ACT.Copy).then_inc(wts_done, 1)
                act.wait_ge(wts_done, s + 1)
                act.wait_ge(gathered_in[par], arrivals)
                for n in range(NT):
                    nc.scalar.activation(total[:, par, n], gathered[:, par, n, 0], ACT.Copy, scale=wts[:, par, n, 0:1])\
                        .then_inc(begun, 1)

            act.wait_ge(count_step, 6 + B // 2)
            batches(act, begin_sum)

        @block.vector
        def _(dve):
            nc.vector.memset(rows_t[:, :, :, CS:], 0.0).then_inc(padded, 1)
            nc.vector.memset(ones[:], 1.0).then_inc(flagged, 1)
            nc.vector.tensor_scalar(has_slot[:], slot_index[:, :, 0:K], float(SLOTS), None, ALU.is_lt).then_inc(flagged, 1)
            dve.wait_ge(counted, 1)
            nc.vector.tensor_scalar(any_slot[:].rearrange("o n k -> o (n k)"), pd[1][0:1, 0:B * NT * K], 0.0, None,
                                    ALU.is_gt).then_inc(count_step, 1)
            dve.wait_ge(count_step, 1)
            nc.vector.tensor_reduce(n_gathers[:], any_slot[:], AX.X, ALU.add).then_inc(count_step, 1)
            dve.wait_ge(count_step, 2)
            first = n_gathers[:, (B - 2) * NT:]
            nc.vector.tensor_scalar_max(first, first, 1.0).then_inc(count_step, 1)
            dve.wait_ge(count_step, 3)
            nc.vector.tensor_copy(n_gathers_i[:], n_gathers[:]).then_inc(count_step, 1)
            by_batch = n_gathers[:].rearrange("o (b n) -> o b n", n=NT)
            nc.vector.tensor_reduce(arrived[:, 0], by_batch[:, B - 2:], AX.X, ALU.add).then_inc(count_step, 1)
            nc.vector.tensor_reduce(arrived[:, 1:].rearrange("o i p -> o (i p)"), by_batch[:, :B - 2], AX.X, ALU.add)\
                .then_inc(count_step, 1)
            for i in range(1, B // 2):
                dve.wait_ge(count_step, 5 + i)
                nc.vector.tensor_tensor(arrived[:, i], arrived[:, i], arrived[:, i - 1], ALU.add).then_inc(count_step, 1)
            dve.wait_ge(count_step, 5 + B // 2)
            nc.vector.tensor_scalar_mul(n_arrivals[:], arrived[:], 16.0).then_inc(count_step, 1)

            def hidden(a, r):
                par = r % 2
                dve.wait_ge(exp_done, a + 1)
                nc.vector.tensor_scalar_add(ex[:, par], ex[:, par], 1.0).then_inc(act_step, 1)
                dve.wait_ge(act_step, 3 * a + 1)
                nc.vector.reciprocal(ex[:, par], ex[:, par]).then_inc(act_step, 1)
                dve.wait_ge(act_step, 3 * a + 2)
                both = pg[par][:, 0:CHUNK * F].rearrange("s (p u f) -> s p u f", u=2, f=F)
                nc.vector.tensor_tensor(ex[:, par], ex[:, par], both[:, :, 0], ALU.mult).then_inc(act_step, 1)
                dve.wait_ge(act_step, 3 * a + 3)
                if not is_first(a, 2):
                    dve.wait_ge(hid_turned, a - 1)
                nc.vector.tensor_tensor(hid[:, par], ex[:, par], both[:, :, 1], ALU.mult).then_inc(hid_done, 1)

            def step(a, r):
                if exists(a + 2):
                    hidden(a + 2, (r + 2) % RING)

            hidden(0, 0)
            hidden(1, 1)
            chunks(dve, step)

            dve.wait_ge(gate_in, 16)
            STEPS = NT * (K - 1)

            def combine(s, b, par, i):
                for j in range(1, K):
                    for n in range(NT):
                        if j == 1:
                            dve.wait_ge(begun, NT * s + n + 1)
                        else:
                            dve.wait_ge(sum_step, STEPS * s + NT * (j - 2) + n + 1)
                        nc.vector.scalar_tensor_tensor(total[:, par, n], gathered[:, par, n, j], wts[:, par, n, j:j + 1],
                                                       total[:, par, n], ALU.mult, ALU.add).then_inc(sum_step, 1)
                dve.wait_ge(sum_step, STEPS * (s + 1))
                dve.sem_inc(summed[par], 1)
                nc.vector.tensor_tensor(total[:, par], total[:, par], gate[:, bass.ds(b, 1)].to_broadcast((P, NT, M)),
                                        ALU.mult).then_inc(gated, 1)
                dve.wait_ge(gated, s + 1)
                if not isinstance(i, int):
                    dve.wait_ge(written[par], 16 * i)
                nc.vector.tensor_tensor(result[:, par], total[:, par], x[:, bass.ds(b * NT, NT)], ALU.add)\
                    .then_inc(result_done, 1)

            batches(dve, combine)

        @block.gpsimd
        def _(pool):
            nc.gpsimd.memset(gathered[:], 0.0).then_inc(cleared, 1)
            pool.wait_ge(cleared, 1)
            pool.wait_ge(count_step, 4)
            for par in range(2):
                pool.wait_ge(stored[par], 32 * NCHUNK // 2)

            def gather_rows(par, n, j):
                nc.gpsimd.indirect_dma_start(
                    gathered[:, par, n, j], None, ybuf,
                    bass.IndirectOffsetOnAxis(ap=index[:, par, n, j:j + 1], axis=0),
                    bounds_check=SLOTS - 1, oob_is_err=False).then_inc(gathered_in[par], 16)

            def gather(s, b, par, i):
                if not isinstance(i, int):
                    pool.wait_ge(summed[par], i)
                nc.gpsimd.tensor_copy(index[:, par], slot_index[:, bass.ds(b * NT, NT)]).then_inc(picked, 1)
                wait_alone(pool, picked, s + 1, cleared)
                for n in range(NT):
                    count = pool.value_load(n_gathers_i[0:1, bass.ds(b * NT + n, 1)], min_val=0, max_val=K)
                    if isinstance(i, int):
                        gather_rows(par, n, 0)
                    for j in range(1 if isinstance(i, int) else 0, K):
                        with pool.If(count > j):
                            gather_rows(par, n, j)

            batches(pool, gather)


def constants():
    half = D // 2
    inv = (1.0 / np.float32(150000.0) ** (np.arange(half, dtype=np.float32) * 2.0 / D)).astype(np.float32)
    angle = np.arange(S, dtype=np.float32)[:, None] * inv[None, :]
    scale = np.float32(D ** -0.25)
    cos, sin = np.cos(angle) * scale, np.sin(angle) * scale
    tiles = lambda a: np.ascontiguousarray(a.reshape(NT, P, D).transpose(1, 0, 2)).astype(np.float32)
    i, j = np.arange(P)[:, None], np.arange(P)[None, :]
    mask = np.stack([np.where(P + j - i > WINDOW, NEG, 0.0), np.where(P + i - j > WINDOW, NEG, 0.0)], 1)
    return {
        "cos": tiles(np.concatenate([cos, cos], 1)), "sin": tiles(np.concatenate([-sin, sin], 1)),
        "ident": np.eye(P, dtype=np.float32), "tri": (i < j).astype(np.float32), "mask": mask.astype(np.float32),
        "slot_base": (np.arange(E) * CAP + 1).astype(np.float32)[None, :],
    }


def kernel(**inputs):
    import concourse.bacc as bacc
    from concourse.bass_utils import run_bass_kernel_spmd

    a = {n: np.asarray(v) for n, v in inputs.items()}
    turn = lambda w: np.concatenate([w[..., 0::2], w[..., 1::2]], -1)
    wq = turn(a["L0_attn_Wq"]).reshape(M, HKV, QW)
    wk, wv = turn(a["L0_attn_Wk"]), a["L0_attn_Wv"]
    bq = turn(a["L0_attn_bq"]).reshape(HKV, QW)
    bk, bv = turn(a["L0_attn_bk"]), a["L0_attn_bv"]
    arrays = {
        "x": a["L0_attn_hidden_states"].reshape(B * S, M),
        "wqkv": np.concatenate([wq, wk, wv], -1).transpose(1, 0, 2),
        "bias": np.concatenate([bq, bk, bv], -1).reshape(1, HKV * GW),
        "wo": a["L0_attn_Wo"].reshape(H * D, M), "bo": a["L0_attn_bo"].reshape(1, M),
        "sinks": a["L0_attn_sinks"].reshape(1, H),
        "w_router": np.concatenate([a["L0_ffn_gate_w"], a["L0_ffn_ws_gate"], a["L0_ffn_ws_up"]], -1),
        "ws_down": a["L0_ffn_ws_down"], "r_bias": a["L0_ffn_bias"].reshape(1, E),
        "w_gate": a["L0_ffn_w_gate"], "w_up": a["L0_ffn_w_up"], "w_down": a["L0_ffn_w_down"],
        "c": a["L0_c"], "wmod": a["L0_wmod"],
        **constants(),
    }
    nc = bacc.Bacc("TRN2", target_bir_lowering=False, num_devices=1)
    feed, t = {}, {}
    for name, value in arrays.items():
        value = np.ascontiguousarray(value)
        feed[f"in_{name}"] = value
        t[name] = nc.dram_tensor(f"in_{name}", value.shape, mybir.dt.from_np(value.dtype), kind="ExternalInput").ap()
    t["out"] = nc.dram_tensor("out", [B * S, M], F32, kind="ExternalOutput").ap()
    build(nc, t)
    got = run_bass_kernel_spmd(nc, [feed], core_ids=[0])
    return got.results[0]["out"].reshape(B, S, M)
```
